# Optimizing a Trainium2 kernel written in Bass

```python
import numpy as np
import jax
import jax.numpy as jnp

def _softmax(x, axis=-1):
    return jax.nn.softmax(x, axis=axis)

def _gelu(x):
    return jax.nn.gelu(x, approximate=True)

def _silu(x):
    return jax.nn.silu(x)

def _sigmoid(x):
    return jax.nn.sigmoid(x)

def _layernorm(x, axis=-1, eps=1e-05):
    m = jnp.mean(x, axis=axis, keepdims=True)
    v = jnp.var(x, axis=axis, keepdims=True)
    return (x - m) / jnp.sqrt(v + eps)

def _scatter_add(tgt, idx, src, axis=0):
    return tgt.at[idx].add(src)

def _segment_sum(src, seg, n):
    return jax.ops.segment_sum(src, seg, n)
kernel_name = 'mk_xattn_seq_d4_seqx_r8_eb9bf3'

def setup_inputs(seed: int=0):
    np.random.seed(seed)
    _w = jnp.asarray

    def _rec_inputs():
        import jax
        import jax.numpy as jnp
        _rk = jax.random.key(seed)
        x = -0.0003929 + 0.9999 * jax.random.normal(jax.random.fold_in(_rk, 1), (8, 100, 256), jnp.float32)
        _lenS = 100 - jax.random.randint(jax.random.fold_in(_rk, 7), (8,), 0, max(1, 100 // 4) + 1, jnp.int32)
        _lenS2 = 1444 - jax.random.randint(jax.random.fold_in(_rk, 8), (8,), 0, max(1, 1444 // 4) + 1, jnp.int32)
        _ctx_1024P = jax.random.normal(jax.random.fold_in(_rk, 11), (8, 16, 128), jnp.float32)
        _ctx_1024c = jax.random.dirichlet(jax.random.fold_in(_rk, 511), 0.3 * jnp.ones((16,), jnp.float32), (8, 1444))
        _ctx_1024t = jnp.einsum('bsk,bkd->bsd', _ctx_1024c, _ctx_1024P)
        _ctx_1024t = _ctx_1024t * jax.lax.rsqrt(jnp.mean(jnp.square(_ctx_1024t)) + 1e-12) * 0.953939
        ctx_1024 = 0.00191187 + 0.999416 * (_ctx_1024t + 0.3 * jax.random.normal(jax.random.fold_in(_rk, 611), (8, 1444, 128), jnp.float32))
        pos_1xS = jnp.broadcast_to(jnp.arange(100, dtype=jnp.int32), (1, 100))
        _validS = jnp.arange(100)[None, :] < _lenS[:, None]
        _validS2 = jnp.arange(1444)[None, :] < _lenS2[:, None]
        _causal = jnp.tril(jnp.ones((100, 100), dtype=bool))
        mask_BxS2_bk0 = jnp.logical_not(jnp.broadcast_to(_validS2[:, :], (8, 1444)))
        mask_BxS_ik0 = jnp.where(jnp.broadcast_to(_validS[:, :], (8, 100)), 0, 1).astype(jnp.int32)
        return (x, ctx_1024, pos_1xS, mask_BxS2_bk0, mask_BxS_ik0)
    x, ctx_1024, pos_1xS, mask_BxS2_bk0, mask_BxS_ik0 = _rec_inputs()

    def _L0_xattn_setup():
        import jax, jax.numpy as jnp
        import numpy as np
        DIM = 256
        DIM_MEDIA = 128
        HEADS = 16
        DIM_HEAD = 64
        INNER = HEADS * DIM_HEAD
        FF_INNER = 4 * DIM
        B, N_TOK, N_LAT = (4, 256, 64)
        EPS = 1e-05

        def layernorm(x, g, b):
            mu = jnp.mean(x, axis=-1, keepdims=True)
            var = jnp.var(x, axis=-1, keepdims=True)
            return (x - mu) * jax.lax.rsqrt(var + EPS) * g + b
        key = jax.random.key(seed)
        ks = jax.random.split(key, 12)
        x = jax.random.normal(ks[0], (B, N_TOK, DIM), dtype=jnp.float32)
        media = jax.random.normal(ks[1], (B, N_LAT, DIM_MEDIA), dtype=jnp.float32)
        media_mask = jax.random.randint(ks[2], (B, N_LAT), 0, 2).astype(bool)
        media_mask = media_mask.at[:, 0].set(True)
        s = lambda d: 1.0 / np.sqrt(d)
        Wq = jax.random.normal(ks[3], (DIM, INNER), dtype=jnp.float32) * s(DIM)
        Wkv = jax.random.normal(ks[4], (DIM_MEDIA, 2 * INNER), dtype=jnp.float32) * s(DIM_MEDIA)
        Wo = jax.random.normal(ks[5], (INNER, DIM), dtype=jnp.float32) * s(INNER)
        W1 = jax.random.normal(ks[6], (DIM, FF_INNER), dtype=jnp.float32) * s(DIM)
        W2 = jax.random.normal(ks[7], (FF_INNER, DIM), dtype=jnp.float32) * s(FF_INNER)
        return {'x': x, 'media': media, 'media_mask': media_mask, 'ln_q_g': jnp.ones((DIM,), jnp.float32), 'ln_q_b': jnp.zeros((DIM,), jnp.float32), 'Wq': Wq, 'Wkv': Wkv, 'Wo': Wo, 'attn_gate': jax.random.normal(ks[8], (1,), jnp.float32) * 0.5, 'ln_ff_g': jnp.ones((DIM,), jnp.float32), 'ln_ff_b': jnp.zeros((DIM,), jnp.float32), 'W1': W1, 'W2': W2, 'ff_gate': jax.random.normal(ks[9], (1,), jnp.float32) * 0.5}
    _L0_xattn_all = _L0_xattn_setup()
    _L0_xattn_in = {k: v for k, v in _L0_xattn_all.items() if k in ('ln_q_g', 'ln_q_b', 'Wq', 'Wkv', 'Wo', 'attn_gate', 'ln_ff_g', 'ln_ff_b', 'W1', 'W2', 'ff_gate')}
    del _L0_xattn_all

    def _L1_xattn_setup():
        import jax, jax.numpy as jnp
        import numpy as np
        H = 256
        NH = 16
        HD = H // NH
        CH = 128
        CC = 128
        CHD = CC // NH
        I = 688
        B = 2
        L = 256
        LE = 128
        EPS = 1e-06

        def rms_norm(x, w):
            xf = x.astype(jnp.float32)
            var = jnp.mean(xf * xf, axis=-1, keepdims=True)
            return (w * (xf * jax.lax.rsqrt(var + EPS))).astype(x.dtype)

        def expert_mask(tt):
            vm = jnp.zeros(tt.shape, dtype=bool)
            vm = vm.at[:, :-1].set((tt[:, :-1] == 1) & (tt[:, 1:] == 1))
            return vm

        def rotate_half(x):
            d = x.shape[-1] // 2
            return jnp.concatenate([-x[..., d:], x[..., :d]], axis=-1)

        def apply_rotary(q, k, position_ids, seq_len):
            inv = 1.0 / 10000.0 ** (jnp.arange(0, HD, 2, dtype=jnp.float32) / HD)
            t = jnp.arange(seq_len, dtype=jnp.float32)
            freqs = jnp.outer(t, inv)
            emb = jnp.concatenate([freqs, freqs], axis=-1)
            cos = jnp.cos(emb)[position_ids][:, None].astype(q.dtype)
            sin = jnp.sin(emb)[position_ids][:, None].astype(q.dtype)
            return (q * cos + rotate_half(q) * sin, k * cos + rotate_half(k) * sin)

        def sdpa(q, k, v, causal):
            scale = 1.0 / np.sqrt(q.shape[-1])
            scores = jnp.einsum('bhqd,bhkd->bhqk', q * scale, k)
            if causal:
                mask = jnp.tril(jnp.ones((q.shape[-2], k.shape[-2]), dtype=bool))
                scores = jnp.where(mask, scores, jnp.finfo(jnp.float32).min)
            p = jax.nn.softmax(scores.astype(jnp.float32), axis=-1).astype(q.dtype)
            return jnp.einsum('bhqk,bhkd->bhqd', p, v)

        def heads(x, nh, hd):
            b, l, _ = x.shape
            return x.reshape(b, l, nh, hd).transpose(0, 2, 1, 3)
        key = jax.random.key(seed)
        ks = jax.random.split(key, 20)
        s = 0.02
        f32 = jnp.float32
        return {'hidden_states': jax.random.normal(ks[0], (B, L, H), f32), 'encoder_outputs': jax.random.normal(ks[1], (B, LE, CH), f32), 'token_type_ids': jax.random.randint(ks[2], (B, L), 0, 2, jnp.int32), 'position_ids': jnp.arange(L, dtype=jnp.int32)[None, :], 'ln_in_w': jnp.ones((H,), f32), 'ln_post_attn_w': jnp.ones((H,), f32), 'ln_post_cross_w': jnp.ones((H,), f32), 'v_qkv': jax.random.normal(ks[3], (H, 3 * H), f32) * s, 'l_qkv': jax.random.normal(ks[4], (H, 3 * H), f32) * s, 'v_dense': jax.random.normal(ks[5], (H, H), f32) * s, 'l_dense': jax.random.normal(ks[6], (H, H), f32) * s, 'cq_w': jax.random.normal(ks[7], (H, CC), f32) * s, 'ckv_w': jax.random.normal(ks[8], (CH, 2 * CC), f32) * s, 'cdense_w': jax.random.normal(ks[9], (CC, H), f32) * s, 'v_gate': jax.random.normal(ks[10], (H, I), f32) * s, 'v_up': jax.random.normal(ks[11], (H, I), f32) * s, 'v_down': jax.random.normal(ks[12], (I, H), f32) * s, 'l_gate': jax.random.normal(ks[13], (H, I), f32) * s, 'l_up': jax.random.normal(ks[14], (H, I), f32) * s, 'l_down': jax.random.normal(ks[15], (I, H), f32) * s}
    _L1_xattn_all = _L1_xattn_setup()
    _L1_xattn_in = {k: v for k, v in _L1_xattn_all.items() if k in ('ln_in_w', 'ln_post_attn_w', 'ln_post_cross_w', 'v_qkv', 'l_qkv', 'v_dense', 'l_dense', 'cq_w', 'ckv_w', 'cdense_w', 'v_gate', 'v_up', 'v_down', 'l_gate', 'l_up', 'l_down')}
    del _L1_xattn_all

    def _L2_xattn_setup():
        import jax, jax.numpy as jnp
        import numpy as np
        EPS = 1e-06

        def _rmsnorm(x, w):
            var = jnp.mean(jnp.square(x), axis=-1, keepdims=True)
            return x * jax.lax.rsqrt(var + EPS) * w
        key = jax.random.key(seed)
        ks = jax.random.split(key, 6)
        B, N, M = (4, 512, 256)
        d_model, memory_dim = (256, 128)
        hidden_states = jax.random.normal(ks[0], (B, N, d_model), dtype=jnp.float32)
        memory = jax.random.normal(ks[1], (B, M, memory_dim), dtype=jnp.float32)
        W_mem = jax.random.normal(ks[2], (d_model, memory_dim), dtype=jnp.float32) / np.sqrt(memory_dim)
        W_gate = jax.random.normal(ks[3], (d_model, 2 * d_model), dtype=jnp.float32) / np.sqrt(2 * d_model)
        b_gate = jax.random.normal(ks[4], (d_model,), dtype=jnp.float32) * 0.01
        norm_w = jnp.ones((d_model,), dtype=jnp.float32)
        return {'hidden_states': hidden_states, 'memory': memory, 'W_mem': W_mem, 'W_gate': W_gate, 'b_gate': b_gate, 'norm_w': norm_w}
    _L2_xattn_all = _L2_xattn_setup()
    _L2_xattn_in = {k: v for k, v in _L2_xattn_all.items() if k in ('W_mem', 'W_gate', 'b_gate', 'norm_w')}
    del _L2_xattn_all

    def _L3_xattn_setup():
        import jax, jax.numpy as jnp
        import numpy as np
        EPS = 1e-06

        def _rmsnorm(x, w):
            var = jnp.mean(jnp.square(x), axis=-1, keepdims=True)
            return x * jax.lax.rsqrt(var + EPS) * w
        key = jax.random.key(seed)
        ks = jax.random.split(key, 6)
        B, N, M = (4, 512, 256)
        d_model, memory_dim = (256, 128)
        hidden_states = jax.random.normal(ks[0], (B, N, d_model), dtype=jnp.float32)
        memory = jax.random.normal(ks[1], (B, M, memory_dim), dtype=jnp.float32)
        W_mem = jax.random.normal(ks[2], (d_model, memory_dim), dtype=jnp.float32) / np.sqrt(memory_dim)
        W_gate = jax.random.normal(ks[3], (d_model, 2 * d_model), dtype=jnp.float32) / np.sqrt(2 * d_model)
        b_gate = jax.random.normal(ks[4], (d_model,), dtype=jnp.float32) * 0.01
        norm_w = jnp.ones((d_model,), dtype=jnp.float32)
        return {'hidden_states': hidden_states, 'memory': memory, 'W_mem': W_mem, 'W_gate': W_gate, 'b_gate': b_gate, 'norm_w': norm_w}
    _L3_xattn_all = _L3_xattn_setup()
    _L3_xattn_in = {k: v for k, v in _L3_xattn_all.items() if k in ('W_mem', 'W_gate', 'b_gate', 'norm_w')}
    del _L3_xattn_all
    return {'x': x, 'ctx_1024': ctx_1024, 'pos_1xS': pos_1xS, 'mask_BxS2_bk0': mask_BxS2_bk0, 'mask_BxS_ik0': mask_BxS_ik0, 'L0_xattn_ln_q_g': _L0_xattn_in['ln_q_g'], 'L0_xattn_ln_q_b': _L0_xattn_in['ln_q_b'], 'L0_xattn_Wq': _L0_xattn_in['Wq'], 'L0_xattn_Wkv': _L0_xattn_in['Wkv'], 'L0_xattn_Wo': _L0_xattn_in['Wo'], 'L0_xattn_attn_gate': _L0_xattn_in['attn_gate'], 'L0_xattn_ln_ff_g': _L0_xattn_in['ln_ff_g'], 'L0_xattn_ln_ff_b': _L0_xattn_in['ln_ff_b'], 'L0_xattn_W1': _L0_xattn_in['W1'], 'L0_xattn_W2': _L0_xattn_in['W2'], 'L0_xattn_ff_gate': _L0_xattn_in['ff_gate'], 'L1_xattn_ln_in_w': _L1_xattn_in['ln_in_w'], 'L1_xattn_ln_post_attn_w': _L1_xattn_in['ln_post_attn_w'], 'L1_xattn_ln_post_cross_w': _L1_xattn_in['ln_post_cross_w'], 'L1_xattn_v_qkv': _L1_xattn_in['v_qkv'], 'L1_xattn_l_qkv': _L1_xattn_in['l_qkv'], 'L1_xattn_v_dense': _L1_xattn_in['v_dense'], 'L1_xattn_l_dense': _L1_xattn_in['l_dense'], 'L1_xattn_cq_w': _L1_xattn_in['cq_w'], 'L1_xattn_ckv_w': _L1_xattn_in['ckv_w'], 'L1_xattn_cdense_w': _L1_xattn_in['cdense_w'], 'L1_xattn_v_gate': _L1_xattn_in['v_gate'], 'L1_xattn_v_up': _L1_xattn_in['v_up'], 'L1_xattn_v_down': _L1_xattn_in['v_down'], 'L1_xattn_l_gate': _L1_xattn_in['l_gate'], 'L1_xattn_l_up': _L1_xattn_in['l_up'], 'L1_xattn_l_down': _L1_xattn_in['l_down'], 'L2_xattn_W_mem': _L2_xattn_in['W_mem'], 'L2_xattn_W_gate': _L2_xattn_in['W_gate'], 'L2_xattn_b_gate': _L2_xattn_in['b_gate'], 'L2_xattn_norm_w': _L2_xattn_in['norm_w'], 'L3_xattn_W_mem': _L3_xattn_in['W_mem'], 'L3_xattn_W_gate': _L3_xattn_in['W_gate'], 'L3_xattn_b_gate': _L3_xattn_in['b_gate'], 'L3_xattn_norm_w': _L3_xattn_in['norm_w']}

def reference(x, ctx_1024, pos_1xS, mask_BxS2_bk0, mask_BxS_ik0, L0_xattn_ln_q_g, L0_xattn_ln_q_b, L0_xattn_Wq, L0_xattn_Wkv, L0_xattn_Wo, L0_xattn_attn_gate, L0_xattn_ln_ff_g, L0_xattn_ln_ff_b, L0_xattn_W1, L0_xattn_W2, L0_xattn_ff_gate, L1_xattn_ln_in_w, L1_xattn_ln_post_attn_w, L1_xattn_ln_post_cross_w, L1_xattn_v_qkv, L1_xattn_l_qkv, L1_xattn_v_dense, L1_xattn_l_dense, L1_xattn_cq_w, L1_xattn_ckv_w, L1_xattn_cdense_w, L1_xattn_v_gate, L1_xattn_v_up, L1_xattn_v_down, L1_xattn_l_gate, L1_xattn_l_up, L1_xattn_l_down, L2_xattn_W_mem, L2_xattn_W_gate, L2_xattn_b_gate, L2_xattn_norm_w, L3_xattn_W_mem, L3_xattn_W_gate, L3_xattn_b_gate, L3_xattn_norm_w):
    import jax
    import jax.numpy as jnp

    def _L0_xattn_ref(x, media, media_mask, ln_q_g, ln_q_b, Wq, Wkv, Wo, attn_gate, ln_ff_g, ln_ff_b, W1, W2, ff_gate):
        import jax, jax.numpy as jnp
        import numpy as np
        DIM = 256
        DIM_MEDIA = 128
        HEADS = 16
        DIM_HEAD = 64
        INNER = HEADS * DIM_HEAD
        FF_INNER = 4 * DIM
        B, N_TOK, N_LAT = (4, 256, 64)
        EPS = 1e-05

        def layernorm(x, g, b):
            mu = jnp.mean(x, axis=-1, keepdims=True)
            var = jnp.var(x, axis=-1, keepdims=True)
            return (x - mu) * jax.lax.rsqrt(var + EPS) * g + b
        scale = DIM_HEAD ** (-0.5)
        qn = layernorm(x, ln_q_g, ln_q_b)
        q = qn @ Wq * scale
        kv = media @ Wkv
        k, v = jnp.split(kv, 2, axis=-1)
        split_heads = lambda t: t.reshape(t.shape[0], t.shape[1], HEADS, DIM_HEAD).transpose(0, 2, 1, 3)
        q, k, v = (split_heads(q), split_heads(k), split_heads(v))
        sim = jnp.einsum('bhid,bhjd->bhij', q, k)
        neg_inf = jnp.finfo(sim.dtype).min
        sim = jnp.where(media_mask[:, None, None, :], sim, neg_inf)
        attn = jax.nn.softmax(sim, axis=-1)
        out = jnp.einsum('bhij,bhjd->bhid', attn, v)
        out = out.transpose(0, 2, 1, 3).reshape(x.shape[0], x.shape[1], INNER)
        attn_out = out @ Wo
        x = x + jnp.tanh(attn_gate) * attn_out
        h = layernorm(x, ln_ff_g, ln_ff_b)
        h = jax.nn.gelu(h @ W1, approximate=False) @ W2
        x = x + jnp.tanh(ff_gate) * h
        return x

    def _L1_xattn_ref(hidden_states, encoder_outputs, token_type_ids, position_ids, ln_in_w, ln_post_attn_w, ln_post_cross_w, v_qkv, l_qkv, v_dense, l_dense, cq_w, ckv_w, cdense_w, v_gate, v_up, v_down, l_gate, l_up, l_down):
        import jax, jax.numpy as jnp
        import numpy as np
        H = 256
        NH = 16
        HD = H // NH
        CH = 128
        CC = 128
        CHD = CC // NH
        I = 688
        B = 2
        L = 256
        LE = 128
        EPS = 1e-06

        def rms_norm(x, w):
            xf = x.astype(jnp.float32)
            var = jnp.mean(xf * xf, axis=-1, keepdims=True)
            return (w * (xf * jax.lax.rsqrt(var + EPS))).astype(x.dtype)

        def expert_mask(tt):
            vm = jnp.zeros(tt.shape, dtype=bool)
            vm = vm.at[:, :-1].set((tt[:, :-1] == 1) & (tt[:, 1:] == 1))
            return vm

        def rotate_half(x):
            d = x.shape[-1] // 2
            return jnp.concatenate([-x[..., d:], x[..., :d]], axis=-1)

        def apply_rotary(q, k, position_ids, seq_len):
            inv = 1.0 / 10000.0 ** (jnp.arange(0, HD, 2, dtype=jnp.float32) / HD)
            t = jnp.arange(seq_len, dtype=jnp.float32)
            freqs = jnp.outer(t, inv)
            emb = jnp.concatenate([freqs, freqs], axis=-1)
            cos = jnp.cos(emb)[position_ids][:, None].astype(q.dtype)
            sin = jnp.sin(emb)[position_ids][:, None].astype(q.dtype)
            return (q * cos + rotate_half(q) * sin, k * cos + rotate_half(k) * sin)

        def sdpa(q, k, v, causal):
            scale = 1.0 / np.sqrt(q.shape[-1])
            scores = jnp.einsum('bhqd,bhkd->bhqk', q * scale, k)
            if causal:
                mask = jnp.tril(jnp.ones((q.shape[-2], k.shape[-2]), dtype=bool))
                scores = jnp.where(mask, scores, jnp.finfo(jnp.float32).min)
            p = jax.nn.softmax(scores.astype(jnp.float32), axis=-1).astype(q.dtype)
            return jnp.einsum('bhqk,bhkd->bhqd', p, v)

        def heads(x, nh, hd):
            b, l, _ = x.shape
            return x.reshape(b, l, nh, hd).transpose(0, 2, 1, 3)
        b, l, _ = hidden_states.shape
        vm = expert_mask(token_type_ids)[..., None]
        residual = hidden_states
        x = rms_norm(hidden_states, ln_in_w)
        mixed = jnp.where(vm, x @ v_qkv, x @ l_qkv)
        q, k, v = jnp.split(mixed, 3, axis=-1)
        q, k, v = (heads(q, NH, HD), heads(k, NH, HD), heads(v, NH, HD))
        q, k = apply_rotary(q, k, position_ids, l)
        ctx = sdpa(q, k, v, causal=True)
        ctx = ctx.transpose(0, 2, 1, 3).reshape(b, l, H)
        attn_out = jnp.where(vm, ctx @ v_dense, ctx @ l_dense)
        hidden_states = residual + attn_out
        ci = rms_norm(hidden_states, ln_post_cross_w)
        cq = heads(ci @ cq_w, NH, CHD)
        ckv = encoder_outputs @ ckv_w
        ck, cv = jnp.split(ckv, 2, axis=-1)
        ck, cv = (heads(ck, NH, CHD), heads(cv, NH, CHD))
        cctx = sdpa(cq, ck, cv, causal=False)
        cctx = cctx.transpose(0, 2, 1, 3).reshape(b, l, CC)
        hidden_states = hidden_states + cctx @ cdense_w
        mi = rms_norm(hidden_states, ln_post_attn_w)
        v_out = jax.nn.silu(mi @ v_gate) * (mi @ v_up) @ v_down
        l_out = jax.nn.silu(mi @ l_gate) * (mi @ l_up) @ l_down
        hidden_states = hidden_states + jnp.where(vm, v_out, l_out)
        return hidden_states

    def _L2_xattn_ref(hidden_states, memory, W_mem, W_gate, b_gate, norm_w):
        import jax, jax.numpy as jnp
        import numpy as np
        EPS = 1e-06

        def _rmsnorm(x, w):
            var = jnp.mean(jnp.square(x), axis=-1, keepdims=True)
            return x * jax.lax.rsqrt(var + EPS) * w
        D = hidden_states.shape[-1]
        memory_proj = jnp.einsum('bme,de->bmd', memory, W_mem)
        scores = jnp.einsum('bnd,bmd->bnm', hidden_states, memory_proj) / jnp.sqrt(jnp.float32(D))
        attn = jax.nn.softmax(scores, axis=-1)
        memory_context = jnp.einsum('bnm,bmd->bnd', attn, memory_proj)
        gate_input = jnp.concatenate([hidden_states, memory_context], axis=-1)
        gate = jax.nn.sigmoid(jnp.einsum('bnf,df->bnd', gate_input, W_gate) + b_gate)
        fused = hidden_states + gate * memory_context
        return _rmsnorm(fused, norm_w)

    def _L3_xattn_ref(hidden_states, memory, W_mem, W_gate, b_gate, norm_w):
        import jax, jax.numpy as jnp
        import numpy as np
        EPS = 1e-06

        def _rmsnorm(x, w):
            var = jnp.mean(jnp.square(x), axis=-1, keepdims=True)
            return x * jax.lax.rsqrt(var + EPS) * w
        D = hidden_states.shape[-1]
        memory_proj = jnp.einsum('bme,de->bmd', memory, W_mem)
        scores = jnp.einsum('bnd,bmd->bnm', hidden_states, memory_proj) / jnp.sqrt(jnp.float32(D))
        attn = jax.nn.softmax(scores, axis=-1)
        memory_context = jnp.einsum('bnm,bmd->bnd', attn, memory_proj)
        gate_input = jnp.concatenate([hidden_states, memory_context], axis=-1)
        gate = jax.nn.sigmoid(jnp.einsum('bnf,df->bnd', gate_input, W_gate) + b_gate)
        fused = hidden_states + gate * memory_context
        return _rmsnorm(fused, norm_w)
    x = _L0_xattn_ref(x, ctx_1024, mask_BxS2_bk0, L0_xattn_ln_q_g, L0_xattn_ln_q_b, L0_xattn_Wq, L0_xattn_Wkv, L0_xattn_Wo, L0_xattn_attn_gate, L0_xattn_ln_ff_g, L0_xattn_ln_ff_b, L0_xattn_W1, L0_xattn_W2, L0_xattn_ff_gate)
    x = _L1_xattn_ref(x, ctx_1024, mask_BxS_ik0, pos_1xS, L1_xattn_ln_in_w, L1_xattn_ln_post_attn_w, L1_xattn_ln_post_cross_w, L1_xattn_v_qkv, L1_xattn_l_qkv, L1_xattn_v_dense, L1_xattn_l_dense, L1_xattn_cq_w, L1_xattn_ckv_w, L1_xattn_cdense_w, L1_xattn_v_gate, L1_xattn_v_up, L1_xattn_v_down, L1_xattn_l_gate, L1_xattn_l_up, L1_xattn_l_down)
    x = _L2_xattn_ref(x, ctx_1024, L2_xattn_W_mem, L2_xattn_W_gate, L2_xattn_b_gate, L2_xattn_norm_w)
    x = _L3_xattn_ref(x, ctx_1024, L3_xattn_W_mem, L3_xattn_W_gate, L3_xattn_b_gate, L3_xattn_norm_w)
    return x

_drawn_inputs = setup_inputs


def setup_inputs(seed=0):
    import zlib

    import numpy as np

    out = dict(_drawn_inputs(seed))
    spreads = {'L0_xattn_ln_q_g': (1.0, 0.6),
     'L0_xattn_ln_q_b': (0.0, 0.8),
     'L0_xattn_ln_ff_g': (1.0, 0.6),
     'L0_xattn_ln_ff_b': (0.0, 0.8),
     'L1_xattn_ln_in_w': (1.0, 0.6),
     'L1_xattn_ln_post_attn_w': (1.0, 0.6),
     'L1_xattn_ln_post_cross_w': (1.0, 0.6),
     'L2_xattn_norm_w': (1.0, 0.2),
     'L3_xattn_norm_w': (1.0, 0.2)}
    factors = {'L0_xattn_W1': 2.74,
     'L1_xattn_v_qkv': 8.0,
     'L1_xattn_v_dense': 8.0,
     'L1_xattn_cq_w': 61.534,
     'L1_xattn_v_gate': 5.302,
     'L1_xattn_v_up': 5.281,
     'L1_xattn_v_down': 5.306,
     'L2_xattn_b_gate': 62.881,
     'L3_xattn_b_gate': 48.996}
    for name, (base, spread) in spreads.items():
        noise = np.random.default_rng([zlib.crc32(name.encode()), seed]).standard_normal(out[name].shape)
        drawn = base * np.exp(spread * noise) if base else spread * noise
        out[name] = jnp.asarray(drawn.astype(out[name].dtype))
    for name, factor in factors.items():
        out[name] = (out[name] * factor).astype(out[name].dtype)
    return out
```

```python
import numpy as np
import concourse.bass as bass
from concourse import mybir
from contextlib import ExitStack

FP32 = mybir.dt.float32
FP32R = mybir.dt.float32r
U8 = mybir.dt.uint8
I32 = mybir.dt.int32
ALU = mybir.AluOpType
ACT = mybir.ActivationFunctionType
AX = mybir.AxisListType

P = 128
B, S, D = 8, 100, 256
T = B * S
HALF = T // 2
C = D // P
SK, DM = 1444, 128
HEADS = 16
DH0 = 64
F0 = 1024
HD1, CHD1 = 16, 8
FF1 = 688
FC1 = -(-FF1 // P)
BIG = 3.0e38
FMAX = 3.4e38

CHUNKS = 12
FULL = 10
TAIL = (SK - FULL * P) // 2
assert FULL * P + 2 * TAIL == SK


def chunk_rows(c):
    return P if c < FULL else TAIL


def chunk_start(c):
    return c * P if c < FULL else FULL * P + (c - FULL) * TAIL


PIECES = [(0, 512), (512, 1024), (1024, SK)]

WIDE = dict(groups=[[128] * 4, [128] * 3, [128] * 3, [128, 128, 64]],
            q_pieces=[(0, 3), (3, 6), (6, 8), (8, 11), (11, 14), (14, 16)],
            tiles=[[c] for c in range(CHUNKS)], ring=3, item_slots=10, rb_slot=8)
NARROW = dict(groups=[[S]], q_pieces=[(0, 1)],
              tiles=[[0, 1, 2, 3], [4, 5, 6, 7], [8, 9], [10, 11]], ring=2, item_slots=3, rb_slot=3)
ATTS = [dict(WIDE, kind=0, c_pieces=2), dict(WIDE, kind=1, c_pieces=1),
        dict(NARROW, kind=2, c_pieces=1), dict(NARROW, kind=3, c_pieces=1)]


def head_at(n):
    return 2 * n if n < HEADS // 2 else 2 * n - HEADS + 1


LEAD = 1024


def batch_counts(a):
    nu = sum(len(g) for g in a["groups"])
    ng, nt, nq = len(a["groups"]), len(a["tiles"]), len(a["q_pieces"])
    return dict(raw_t=16, raw_n=32, raw_m=16 if a["kind"] == 0 else 0, q_in=16,
                t_hi=1, n_hi=1, t_lo=1, n_lo=1, bias=1 if a["kind"] == 0 else 0,
                qbd=1 if a["kind"] == 1 else 0, q_mm=nq, q_hi=nq, q_lo=nq,
                s_mm=3 * nu, s_neg=3 * nu, nmax=nu, p_exp=nu, rden=nu, diag=nu,
                t_mm=ng * nt, pt_hi=ng * nt, pt_lo=ng * nt, pv_mm=ng * nt,
                rb_mm=ng, rb_sb=ng, o_ev=ng, c_mm=a["c_pieces"], c_ev=a["c_pieces"])


COUNTS = [batch_counts(a) for a in ATTS]
STARTED_BY = dict(sync=["raw_t", "raw_n", "raw_m", "q_in"],
                  vector=["t_hi", "n_hi", "bias", "q_lo", "s_neg", "nmax", "rden", "pt_lo", "o_ev"],
                  gpsimd=["t_lo", "n_lo", "qbd", "diag"],
                  scalar=["q_hi", "p_exp", "pt_hi", "rb_sb", "c_ev"],
                  tensor=["q_mm", "s_mm", "t_mm", "pv_mm", "rb_mm", "c_mm"])


def build_layers(nc, ins, out):
    ctx = ExitStack()
    with ctx:
        def sb(name, shape, dt=FP32):
            return ctx.enter_context(nc.sbuf_tensor(name, shape, dt))

        def sem(name):
            return ctx.enter_context(nc.semaphore(name))

        x = sb("x", [P, C, T])
        big = sb("big", [P, 8 * T])
        wide = sb("wide", [P, 7, SK])
        work = sb("work", [P, 9160])
        qhi = sb("qhi", [P, 2, 1664], FP32R)
        qlo = sb("qlo", [P, 2, 1664], FP32R)
        thi = sb("thi", [P, 2, SK], FP32R)
        tlo = sb("tlo", [P, 2, SK], FP32R)
        nhi = sb("nhi", [P, 2, CHUNKS, DM], FP32R)
        nlo = sb("nlo", [P, 2, CHUNKS, DM], FP32R)
        pthi = sb("pthi", [P, 3, 512], FP32R)
        ptlo = sb("ptlo", [P, 3, 512], FP32R)
        watt = sb("watt", [P, 2304])
        vec = sb("vec", [P, 24])
        rstat = sb("rstat", [P, 3 * HEADS])
        ident = sb("ident", [P, P])
        ones = sb("ones", [P, P])
        hmask8 = sb("hmask8", [P, 8])
        hmask16 = sb("hmask16", [P, HEADS])
        eps5 = sb("eps5", [P, 1])
        eps6 = sb("eps6", [P, 1])
        vm = sb("vm", [P, T])
        cossin = sb("cossin", [P, 2, S])
        late = sb("late", [P, SK // 4])
        tgate = sb("tgate", [P, 2])
        negmin3 = sb("negmin3", [P, 7, 3])
        negmax = sb("negmax", [P, 7])
        den = sb("den", [P, 7])
        rdn = sb("rdn", [P, 7])
        ps = ctx.enter_context(nc.psum_tensor("ps", [P, 8, 512], FP32))

        mask_u8 = late[:, :].bitcast(U8)
        rot = late[:, 0:P]
        causal = late[0:S, P:P + S]
        raw = work[:, 0:1536]
        outT = work[:, 1536:3136]
        bias = work[:, 3136:6024].rearrange("p (j k) -> p j k", j=2)
        rbc = work[:, 6024:7048].rearrange("p (j k) -> p j k", j=2)
        diag = work[:, 7048:7560].rearrange("p (j k) -> p j k", j=4)
        qb = work[:, 7560:9160].rearrange("p (j k) -> p j k", j=2)
        xe = work[:, 1536:4736].rearrange("p (e c t) -> p e c t", e=2, c=C)
        xn = work[:, 4736:6336].rearrange("p (c t) -> p c t", c=C)
        xc = work[:, 6336:7936].rearrange("p (c t) -> p c t", c=C)
        rstd = work[:, 7936:8736]
        vtok = work[0:S, 6336:8384].rearrange("p (b d) -> p b d", b=B)
        wflat = wide[:, :, :].rearrange("p u k -> p (u k)")
        wq = wflat[:, 0:2048].rearrange("p (c n) -> p c n", c=C)
        wo = wflat[:, 0:2048].rearrange("p (c n) -> p c n", c=8)
        w1 = wflat[:, 2048:4096].rearrange("p (c n) -> p c n", c=C)
        w2 = wflat[:, 4096:6144].rearrange("p (c n) -> p c n", c=8)
        wqkv = wflat[:, 6144:9216].rearrange("p (e c n) -> p e c n", e=2, c=C)
        wcq = wflat[:, 9216:9472].rearrange("p (c n) -> p c n", c=C)
        wdn1 = wflat[:, 0:1024].rearrange("p (e c n) -> p e c n", e=2, c=C)
        kbd = wflat[:, 1024:4224].rearrange("p (j h q) -> p j h q", j=2, h=HEADS)
        sself = wflat[0:S, 4224:5824].rearrange("p (h q) -> p h q", h=HEADS)
        wgu = wflat[:, 0:5504].rearrange("p (g e c n) -> p g e c n", g=2, e=2, c=C)
        wdown = wflat[:, 5504:8576].rearrange("p (e c n) -> p e c n", e=2, c=FC1)
        gsilu = wflat[:, 8576:9376].rearrange("p (j t) -> p j t", j=2)
        hgu = wflat[:, 9376:9776]
        wcd = wflat[:, 9776:10032]
        wk0 = watt[:, 0:1024].rearrange("p (c n) -> p c n", c=8)
        wv0 = watt[:, 1024:2048]
        wck = watt[:, 2048:2176]
        wcv = watt[:, 2176:2304]
        wcvh = watt[:, 0:2048].rearrange("p (h n) -> p h n", h=HEADS)
        wmem = watt[:, 0:256].rearrange("p (c n) -> p c n", c=C)
        wmemT = watt[:, 256:512]
        wgate = watt[:, 512:1536].rearrange("p (c n) -> p c n", c=4)
        big8 = big[:, :].rearrange("p (c t) -> p c t", c=8)
        qk = big[:, 0:4 * T].rearrange("p (c t) -> p c t", c=4)
        qkb = big[:, 4 * T:5 * T].rearrange("p (j c t) -> p j c t", j=2, c=4)
        ptself = big[0:S, 5 * T:7 * T].rearrange("p (h q) -> p h q", h=HEADS)
        vb = big[0:S, 7 * T:7 * T + 512].rearrange("p (j d) -> p j d", j=2)
        ctok = big[0:S, 7 * T + 512:7 * T + 768]
        cq = big[:, 0:T]
        cT = big[:, T:2 * T]
        qbd1 = big[:, 4 * T:6 * T]
        hexp = big[:, 0:12 * HALF].rearrange("p (e c t) -> p e c t", e=2, c=FC1)
        mc = big[:, 0:2 * T].rearrange("p (c t) -> p c t", c=C)
        gate = big[:, 2 * T:4 * T].rearrange("p (c t) -> p c t", c=C)
        ctxT = xn
        rotated = work[:, 4736:5536].rearrange("p (j t) -> p j t", j=2)
        postab = rbc[0:S, 0, 0:2 * P]
        pos_i = rbc[:, 0, 256:356].bitcast(I32)
        pos_f = rbc[:, 1, 100:200]
        pos_neg = rbc[:, 1, 200:300]
        onehot = rbc[0:S, 1, 0:S]
        tt_i = big[:, 0:T].bitcast(I32)
        tt_one = big[:, T:2 * T].rearrange("p (b s) -> p b s", b=B)
        VEC = {n: k for k, n in enumerate(
            ["ln_q_g", "ln_q_b", "ln_ff_g", "ln_ff_b", "ln_in", "ln_cross", "ln_post", "n2", "n3", "b2", "b3"])}

        def vcol(name, c):
            return vec[:, 2 * VEC[name] + c:2 * VEC[name] + c + 1]

        A = {n: sem(n) for names in STARTED_BY.values() for n in names}
        passed = {n: sem(f"passed_{n}") for n in ("loads", "scores")}
        load_consts = sem("load_consts")
        load_x = sem("load_x")
        load_w0 = sem("load_w0")
        load_wo = sem("load_wo")
        load_w12 = sem("load_w12")
        load_qkv = sem("load_qkv")
        load_w1att = sem("load_w1att")
        load_d1 = sem("load_d1")
        load_rot = sem("load_rot")
        load_cd = sem("load_cd")
        load_gu = sem("load_gu")
        load_down = sem("load_down")
        load_w23 = sem("load_w23")
        consts = sem("consts")
        mean_mm = sem("mean_mm")
        centred = sem("centred")
        squared = sem("squared")
        var_mm = sem("var_mm")
        std_ok = sem("std_ok")
        norm_step = sem("norm_step")
        norm_ok = sem("norm_ok")
        gates_ok = sem("gates_ok")
        DENSE = ["q0", "o0", "f1", "f2", "qk", "rt", "vt", "d1", "cq", "cd", "gu", "dn", "g2", "g3"]
        mm = {n: sem(f"{n}_mm") for n in DENSE}
        ev = {n: sem(f"{n}_ev") for n in DENSE}
        rt_s = sem("rt_s")
        xe_v = sem("xe_v")
        xe_l = sem("xe_l")
        gu_h = sem("gu_h")
        gu_silu = sem("gu_silu")
        pos_ok = sem("pos_ok")
        cossin_mm = sem("cossin_mm")
        cossin_ok = sem("cossin_ok")
        bias_zero = sem("bias_zero")
        gu_v = sem("gu_v")
        vm_step = sem("vm_step")
        wcv_step = sem("wcv_step")
        fuse = sem("fuse")
        rope = sem("rope")
        sa_in = [sem("sa_in_even"), sem("sa_in_odd")]
        sa_kbd = sem("sa_kbd")
        sa_s = sem("sa_s")
        sa_m = sem("sa_m")
        sa_x = sem("sa_x")
        sa_sub = sem("sa_sub")
        sa_e = sem("sa_e")
        sa_den = sem("sa_den")
        sa_t = sem("sa_t")
        sa_pt = sem("sa_pt")
        sa_c = sem("sa_c")
        sa_ct = sem("sa_ct")
        sa_ctt = sem("sa_ctt")
        sa_out = sem("sa_out")
        wcv_ok = sem("wcv_ok")
        stored = sem("stored")

        base = [{n: LEAD + B * sum(COUNTS[m][n] for m in range(l)) for n in A} for l in range(5)]

        def at(l, name, i, j, k=0):
            n = COUNTS[l][name]
            return i * (2 * n) + (base[l][name] + j * n + k)

        def done(l, name):
            return base[l + 1][name]

        def wait(eng, l, name, i, j, k=0):
            eng.wait_ge(A[name], at(l, name, i, j, k))

        def carry_wait(eng, name):
            eng.sem_inc(passed[name], 1)

        def next_batch(i, j):
            return i, j + 1

        def plan(a, k, nxt):
            groups = a["groups"]
            last = k == len(groups) - 1
            if last and not nxt:
                return []
            ng = 0 if last else k + 1
            items = [("q", x) for x in range(len(a["q_pieces"]))] if last else []
            items += [("s", ng, u, j) for u in range(len(groups[ng])) for j in range(3)]
            n = len(items)
            return [(m * a["item_slots"] // n, it) for m, it in enumerate(items)]

        def unit_index(a, g, u):
            return sum(len(x) for x in a["groups"][:g]) + u

        def unit_col(a, g, u):
            return sum(sum(x) for x in a["groups"][:g]) + sum(a["groups"][g][:u])

        def slot_of(a, g, u, j):
            odd = (g if len(a["groups"]) > 1 else j) % 2
            return 4 * odd + u

        def q_cols(a, x):
            h0, h1 = a["q_pieces"][x]
            return h0 * S, h1 * S

        def q_need(a, col):
            return next(x + 1 for x in range(len(a["q_pieces"])) if q_cols(a, x)[1] >= min(col, q_cols(a, len(a["q_pieces"]) - 1)[1]))

        def s_cols(a):
            return P if a["kind"] < 2 else S

        block = ctx.enter_context(nc.Block())

        @block.sync
        def _(sp):
            for n in STARTED_BY["sync"]:
                sp.sem_inc(A[n], LEAD)
            sp.dma_start(x[:, :, :], ins["xT"]).then_inc(load_x, 16)
            for dst, src in [(vec[:, :], ins["vec"]), (ident[:, :], ins["ident"]), 
                             (hmask8[:, :], ins["hmask8"]), (hmask16[:, :], ins["hmask16"]),
                             (tgate[:, :], ins["gates"].partition_broadcast(P)),
                             (postab, ins["postab"]), (pos_i, ins["pos"].partition_broadcast(P)),
                             (tt_i, ins["tt"].partition_broadcast(P))]:
                sp.dma_start(dst, src).then_inc(load_consts, 16)
            sp.dma_start(wq, ins["wq"]).then_inc(load_w0, 16)
            sp.dma_start(wk0, ins["wk0"]).then_inc(load_w0, 16)
            sp.dma_start(wv0, ins["wv0"]).then_inc(load_w0, 16)

            def attention_loads(l):
                a = ATTS[l]
                with sp.Fori(0, B // 2) as i:
                    for j in range(2):
                        b = sp.snap(i * 2 + j)
                        wait(sp, l, "n_lo", i, j - 1, 1)
                        carry_wait(sp, "loads")
                        sp.dma_start(raw[:, 0:SK], ins["ctxT"][bass.ds(b, 1), :, :].rearrange("o p k -> p (o k)"))\
                          .then_inc(A["raw_t"], 16)
                        if l == 1:
                            wait(sp, l, "qbd", i, j - 1, 0)
                        else:
                            wait(sp, l, "q_mm", i, j - 1, 0)
                        carry_wait(sp, "loads")
                        if l == 0:
                            sp.dma_start(qb[:, j, :].rearrange("p (c t) -> p c t", c=8),
                                         big8[:, :, bass.ds(b * S, S)]).then_inc(A["q_in"], 16)
                        elif l == 1:
                            sp.dma_start(qb[:, j, 0:S], cq[:, bass.ds(b * S, S)]).then_inc(A["q_in"], 16)
                        else:
                            sp.dma_start(qb[:, j, 0:2 * S].rearrange("p (c t) -> p c t", c=C),
                                         x[:, :, bass.ds(b * S, S)]).then_inc(A["q_in"], 16)
                        if l == 0:
                            wait(sp, l, "bias", i, j - 1, 1)
                            carry_wait(sp, "loads")
                            sp.dma_start(mask_u8, ins["mask"][bass.ds(b, 1), :].rearrange("o k -> (o k)")
                                         .partition_broadcast(P)).then_inc(A["raw_m"], 16)
                        wait(sp, l, "t_lo", i, j, 1)
                        carry_wait(sp, "loads")
                        ctx_b = ins["ctx"][bass.ds(b, 1), :, :]
                        rawn = raw.rearrange("p (c d) -> p c d", c=CHUNKS)
                        sp.dma_start(rawn[:, 0:FULL, :], ctx_b[:, 0:FULL * P, :]
                                     .rearrange("o (c p) d -> p (o c) d", p=P)).then_inc(A["raw_n"], 16)
                        sp.dma_start(rawn[0:TAIL, FULL:CHUNKS, :], ctx_b[:, FULL * P:SK, :]
                                     .rearrange("o (c p) d -> p (o c) d", p=TAIL)).then_inc(A["raw_n"], 16)

            sp.wait_ge(ev["q0"], 16)
            attention_loads(0)
            sp.wait_ge(A["t_mm"], done(0, "t_mm"))
            sp.dma_start(wo, ins["wo"]).then_inc(load_wo, 16)
            sp.dma_start(w1, ins["w1"]).then_inc(load_w12, 16)
            sp.dma_start(w2, ins["w2"]).then_inc(load_w12, 16)
            for e in range(2):
                sp.dma_start(wqkv[:, e, :, :], ins["qkv"][e]).then_inc(load_qkv, 16)
            sp.dma_start(wcq, ins["wcq"]).then_inc(load_qkv, 16)
            sp.wait_ge(A["bias"], done(0, "bias"))
            sp.dma_start(rot, ins["rot"]).then_inc(load_rot, 16)
            sp.dma_start(causal, ins["causal"]).then_inc(load_rot, 16)
            sp.wait_ge(A["c_mm"], done(0, "c_mm"))
            sp.dma_start(wck, ins["wck"]).then_inc(load_w1att, 16)
            sp.dma_start(wcv, ins["wcv"]).then_inc(load_w1att, 16)
            sp.wait_ge(mm["o0"], 4)
            for e in range(2):
                sp.dma_start(wdn1[:, e, :, :], ins["dense1"][e]).then_inc(load_d1, 16)

            sp.wait_ge(rope, 16)
            sp.wait_ge(ev["vt"], 8)
            with sp.Fori(0, B // 2) as i:
                for j in range(2):
                    b = sp.snap(i * 2 + j)
                    sp.wait_ge(sa_ctt, i * 2 + (LEAD + j - 1))
                    carry_wait(sp, "loads")
                    sp.dma_start(qkb[:, j, :, :], qk[:, :, bass.ds(b * S, S)]).then_inc(sa_in[j], 16)
                    sp.dma_start(vb[:, j, :], vtok[:, bass.ds(b, 1), :].rearrange("p o d -> p (o d)"))\
                      .then_inc(sa_in[j], 16)

            sp.wait_ge(ev["cq"], 2)
            attention_loads(1)
            sp.wait_ge(A["t_mm"], done(1, "t_mm"))
            sp.dma_start(wcd, ins["wcd"]).then_inc(load_cd, 16)
            for g in range(2):
                for e in range(2):
                    sp.dma_start(wgu[:, g, e, :, :], ins["gu"][g, e]).then_inc(load_gu, 16)
            for e in range(2):
                sp.dma_start(wdown[:, e, 0:FC1 - 1, :], ins["down"][e, 0:(FC1 - 1) * P, :]
                             .rearrange("(c p) n -> p c n", p=P)).then_inc(load_down, 16)
                sp.dma_start(wdown[0:FF1 % P, e, FC1 - 1, :], ins["down"][e, (FC1 - 1) * P:FF1, :])\
                  .then_inc(load_down, 16)
            for l in (2, 3):
                if l == 2:
                    sp.wait_ge(mm["cd"], 4)
                else:
                    sp.wait_ge(mm["g2"], 4)
                sp.dma_start(wmem, ins["wmem"][l - 2]).then_inc(load_w23, 16)
                sp.dma_start(wmemT, ins["wmemT"][l - 2]).then_inc(load_w23, 16)
                sp.dma_start(wgate, ins["wgate"][l - 2]).then_inc(load_w23, 16)
                if l == 2:
                    sp.wait_ge(ev["dn"], 4)
                else:
                    sp.wait_ge(norm_ok, 24)
                attention_loads(l)
            sp.wait_ge(norm_ok, 28)
            sp.dma_start(out, x[:, :, :]).then_inc(stored, 16)
            sp.wait_ge(stored, 16)

        @block.tensor
        def _(pe):
            for n in STARTED_BY["tensor"]:
                pe.sem_inc(A[n], LEAD)
            pe.sem_inc(sa_ctt, LEAD)

            def bank(t, m):
                return ps[:, 4 * t + m % 4, 0:HALF]

            def half(ap, t):
                return ap[:, t * HALF:(t + 1) * HALF]

            def norm(n, centre):
                if centre:
                    for t in range(2):
                        if n == 0:
                            pe.wait_ge(load_x, 16)
                            pe.wait_ge(consts, 1)
                        else:
                            pe.wait_ge(ev["o0"], 2 * t + 2)
                        for c in range(C):
                            last = pe.matmul(bank(t, 0), ones[:, :], half(x[:, c, :], t), start=c == 0, stop=c == C - 1)
                        last.then_inc(mean_mm, 1)
                for t in range(2):
                    pe.wait_ge(squared, 2 * n + t + 1)
                    for c in range(C):
                        last = pe.matmul(bank(t, 1), ones[:, :], half(xn[:, c, :], t), start=c == 0, stop=c == C - 1)
                    last.then_inc(var_mm, 1)

            def dense(name, tiles, operands, ready):
                for t in range(2):
                    ready(t)
                    for m in range(tiles):
                        if m >= 4:
                            pe.wait_ge(ev[name], t * tiles + m - 3)
                        ops = operands(t, m)
                        rows = ops[0][0].shape[1]
                        for n, (w, v) in enumerate(ops):
                            last = pe.matmul(bank(t, m)[0:rows, :], w, v, start=n == 0, stop=n == len(ops) - 1)
                        last.then_inc(mm[name], 1)

            def attention(l):
                a = ATTS[l]
                groups, tiles, ring = a["groups"], a["tiles"], a["ring"]
                nu = sum(len(g) for g in groups)
                nq, nt, ngr = len(a["q_pieces"]), len(tiles), len(groups)

                def q_piece(i, j, xq):
                    p = j % 2
                    c0, c1 = q_cols(a, xq)
                    if xq < 3:
                        wait(pe, l, "s_neg", i, j - 1, 3 * nu - 3 + xq + 1)
                    else:
                        wait(pe, l, "q_lo", i, j, xq - 2)
                    if l == 1:
                        wait(pe, l, "qbd", i, j, 1)
                    elif xq == 0:
                        wait(pe, l, "q_in", i, j, 16)
                    dst = ps[:, xq % 3, :]
                    if l == 0:
                        h0, h1 = a["q_pieces"][xq]
                        for n in range(h0, h1):
                            h = head_at(n)
                            r = DH0 * (h % 2)
                            last = pe.matmul(dst[:, (n - h0) * S:(n - h0 + 1) * S], wk0[r:r + DH0, h // 2, :],
                                             qb[r:r + DH0, p, (h // 2) * S:(h // 2 + 1) * S], start=True, stop=True)
                    elif l == 1:
                        last = pe.matmul(dst[:, 0:c1 - c0], wck, qbd1[:, c0:c1], start=True, stop=True)
                    else:
                        for c in range(C):
                            last = pe.matmul(dst[:, 0:S], wmem[:, c, :], qb[:, p, c * S:(c + 1) * S],
                                             start=c == 0, stop=c == C - 1)
                    last.then_inc(A["q_mm"], 1)

                def s_piece(i, j, g, u, jj):
                    p = j % 2
                    n = 3 * unit_index(a, g, u) + jj
                    col = unit_col(a, g, u)
                    m = s_cols(a)
                    if jj == 0:
                        wait(pe, l, "q_lo", i, j, q_need(a, col + m))
                    if n == 0:
                        wait(pe, l, "t_lo", i, j, 1)
                    if n < 3:
                        if nq == 1 and n > 0:
                            wait(pe, l, "s_neg", i, j - 1, 3 * nu - 3 + n + 1)
                        else:
                            wait(pe, l, "q_lo", i, j, nq if nq == 1 else nq - 3 + n + 1)
                    else:
                        wait(pe, l, "s_neg", i, j, n - 2)
                    k0, k1 = PIECES[jj]
                    dst = ps[0:m, jj, 0:k1 - k0]
                    for r, (w, v) in enumerate([(qhi, thi), (qhi, tlo), (qlo, thi)]):
                        last = pe.matmul(dst, w[:, p, col:col + m], v[:, p, k0:k1], start=r == 0, stop=r == 2)
                    last.then_inc(A["s_mm"], 1)

                def t_tile(i, j, k, c):
                    tt = k * nt + c
                    if c == 0:
                        wait(pe, l, "p_exp", i, j, unit_index(a, k, len(groups[k]) - 1) + 1)
                    wait(pe, l, "pt_lo", i, j, tt - ring + 1)
                    dst = ps[:, 3 + tt % ring, :]
                    off = 0
                    for ch in tiles[c]:
                        kr, ks = chunk_rows(ch), chunk_start(ch)
                        for u, rows in enumerate(groups[k]):
                            src = wide[0:rows, slot_of(a, k, u, j), ks:ks + kr]
                            last = pe.transpose(dst[0:kr, off:off + rows], src, ident[0:rows, 0:rows])
                            off += rows
                    last.then_inc(A["t_mm"], 1)

                def pv_tile(i, j, k, c):
                    p = j % 2
                    tt = k * nt + c
                    if c == 0:
                        wait(pe, l, "n_lo", i, j, 1)
                        wait(pe, l, "o_ev", i, j, k)
                    wait(pe, l, "pt_lo", i, j, tt + 1)
                    w = sum(groups[k])
                    for n, ch in enumerate(tiles[c]):
                        kr = chunk_rows(ch)
                        for r, (lh, rh) in enumerate([(nhi, pthi), (nhi, ptlo), (nlo, pthi)]):
                            last = pe.matmul(ps[:, 6, 0:w], lh[0:kr, p, ch, :],
                                             rh[0:kr, tt % ring, n * w:(n + 1) * w],
                                             start=ch == 0 and r == 0, stop=ch == CHUNKS - 1 and r == 2)
                    last.then_inc(A["pv_mm"], 1)

                def rb(i, j, k):
                    wait(pe, l, "diag", i, j, unit_index(a, k, len(groups[k]) - 1) + 1)
                    if k == 0:
                        wait(pe, l, "c_ev", i, j, 0)
                    else:
                        wait(pe, l, "rb_sb", i, j, k)
                    off = 0
                    for u, rows in enumerate(groups[k]):
                        last = pe.matmul(ps[:, 7, off:off + rows], ones[0:rows, :], diag[0:rows, u, 0:rows],
                                         start=True, stop=True)
                        off += rows
                    last.then_inc(A["rb_mm"], 1)

                def c_stage(i, j):
                    wait(pe, l, "o_ev", i, j, ngr)
                    for xc_ in range(a["c_pieces"]):
                        if xc_ == 0:
                            wait(pe, l, "rb_sb", i, j, ngr)
                        else:
                            wait(pe, l, "c_ev", i, j, xc_)
                        if l == 0:
                            for h in range(8 * xc_, 8 * xc_ + 8):
                                r, c = DH0 * (h % 2), (h // 2 - 4 * xc_) * S
                                n = next(n for n in range(HEADS) if head_at(n) == h)
                                last = pe.matmul(ps[r:r + DH0, 7, c:c + S], wv0[:, h * DH0:(h + 1) * DH0],
                                                 outT[:, n * S:(n + 1) * S], start=True, stop=True)
                        elif l == 1:
                            for h in range(HEADS):
                                last = pe.matmul(ps[:, 7, 0:S], wcvh[:, h, :], outT[:, h * S:(h + 1) * S],
                                                 start=h == 0, stop=h == HEADS - 1)
                        else:
                            for c in range(C):
                                last = pe.matmul(ps[:, 7, c * S:(c + 1) * S], wmemT[:, c * P:(c + 1) * P],
                                                 outT[:, 0:S], start=True, stop=True)
                        last.then_inc(A["c_mm"], 1)

                def item(i, j, it):
                    if it[0] == "q":
                        q_piece(i, j, it[1])
                    else:
                        s_piece(i, j, *it[1:])

                def step(i, j, k, nxt):
                    last = k == ngr - 1
                    items = plan(a, k, nxt)
                    for s in range(nt + 2):
                        if s < nt:
                            t_tile(i, j, k, s)
                        for at_slot, it in items:
                            if at_slot == s:
                                item(*(next_batch(i, j) if last else (i, j)), it)
                        if s >= 2:
                            pv_tile(i, j, k, s - 2)
                        if s == a["rb_slot"]:
                            rb(i, j, k)
                    if last:
                        c_stage(i, j)

                for xq in range(nq):
                    q_piece(0, 0, xq)
                for u in range(len(groups[0])):
                    for jj in range(3):
                        s_piece(0, 0, 0, u, jj)
                with pe.Fori(0, B // 2 - 1) as i:
                    for j in range(2):
                        for k in range(ngr):
                            step(i, j, k, True)
                for j in range(2):
                    for k in range(ngr):
                        step(B // 2 - 1, j, k, j == 0)

            pe.wait_ge(pos_ok, 5)
            for n in range(2):
                last = pe.matmul(ps[:, 7, n * S:(n + 1) * S], postab[:, n * P:(n + 1) * P], onehot, start=True, stop=True)
            last.then_inc(cossin_mm, 1)
            norm(0, True)

            def ready(t):
                pe.wait_ge(norm_ok, 2 * t + 2)
                if t == 0:
                    pe.wait_ge(load_w0, 48)
                    pe.wait_ge(cossin_ok, 1)
            dense("q0", 8, lambda t, m: [(wq[:, c, m * P:(m + 1) * P], half(xn[:, c, :], t)) for c in range(C)], ready)
            pe.wait_ge(ev["q0"], 16)
            attention(0)

            def ready(t):
                pe.wait_ge(A["c_ev"], done(0, "c_ev"))
                pe.wait_ge(load_wo, 16)
            dense("o0", 2, lambda t, m: [(wo[:, c, m * P:(m + 1) * P], half(big8[:, c, :], t)) for c in range(8)], ready)
            norm(1, True)

            def ready(t):
                pe.wait_ge(norm_ok, 4 + 2 * t + 2)
                pe.wait_ge(load_w12, 32)
            dense("f1", 8, lambda t, m: [(w1[:, c, m * P:(m + 1) * P], half(xn[:, c, :], t)) for c in range(C)], ready)

            def ready(t):
                pe.wait_ge(ev["f1"], 8 * t + 8)
            dense("f2", 2, lambda t, m: [(w2[:, c, m * P:(m + 1) * P], half(big8[:, c, :], t)) for c in range(8)], ready)

            norm(2, False)

            def experts(w, t, m, n=P):
                return [(w[:, e, c, m * P:m * P + n], half(xe[:, e, c, :], t)) for e in range(2) for c in range(C)]

            def ready(t):
                pe.wait_ge(xe_l, t + 1)
                pe.wait_ge(load_qkv, 48)
            dense("qk", 4, lambda t, m: experts(wqkv, t, m), ready)

            for b in range(B):
                if b % 4 == 0:
                    pe.wait_ge(ev["qk"], 4 * (b // 4) + 4)
                for n in range(4):
                    e, c = n // 2, n % 2
                    last = pe.matmul(ps[0:S, b, 0:D], xe[:, e, c, b * S:(b + 1) * S], wqkv[:, e, c, 2 * D:3 * D],
                                     start=n == 0, stop=n == 3)
                last.then_inc(mm["vt"], 1)

            def ready(t):
                pe.wait_ge(ev["vt"], 4 * t + 4)
                pe.wait_ge(load_rot, 32)
            dense("rt", 4, lambda t, m: [(rot, half(qk[:, m, :], t))], ready)

            def sa_scores(i, j):
                p = j % 2
                pe.wait_ge(sa_kbd, i * 2 + (LEAD + j + 1))
                for n in range(4):
                    pe.wait_ge(sa_m, i * 8 + (LEAD + 4 * (j - 1) + n + 1))
                    last = pe.matmul(ps[0:S, n, 0:4 * S], qkb[:, p, n // 2, :], kbd[:, p, 4 * n:4 * n + 4, :],
                                     start=True, stop=True)
                    last.then_inc(sa_s, 1)

            def sa_rest(i, j):
                p = j % 2
                pe.wait_ge(sa_e, i * 2 + (LEAD + j + 1))
                for n in range(4):
                    pe.wait_ge(sa_pt, i * 8 + (LEAD + 4 * j + n - 1))
                    for h in range(4):
                        last = pe.transpose(ps[0:S, 4 + n % 2, h * S:(h + 1) * S], sself[:, 4 * n + h, :],
                                            ident[0:S, 0:S])
                    last.then_inc(sa_t, 1)
                pe.wait_ge(sa_pt, i * 8 + (LEAD + 4 * j + 4))
                for h in range(HEADS):
                    last = pe.matmul(ps[0:S, 6, h * HD1:(h + 1) * HD1], ptself[:, h, :], vb[:, p, h * HD1:(h + 1) * HD1],
                                     start=True, stop=True)
                last.then_inc(sa_c, 1)
                pe.wait_ge(sa_ct, i * 2 + (LEAD + j + 1))
                pe.wait_ge(sa_out, i * 2 + (LEAD + j))
                for c in range(C):
                    last = pe.transpose(ps[:, 7, c * S:(c + 1) * S], ctok[:, c * P:(c + 1) * P], ident[0:S, 0:S])
                last.then_inc(sa_ctt, 1)

            pe.wait_ge(rope, 16)
            sa_scores(0, 0)
            with pe.Fori(0, B // 2 - 1) as i:
                for j in range(2):
                    sa_scores(i, j + 1)
                    sa_rest(i, j)
            sa_scores(B // 2 - 1, 1)
            sa_rest(B // 2 - 1, 0)
            sa_rest(B // 2 - 1, 1)

            def ready(t):
                pe.wait_ge(xe_l, 2 + t + 1)
                pe.wait_ge(load_d1, 32)
            dense("d1", 2, lambda t, m: experts(wdn1, t, m), ready)

            norm(3, False)

            def ready(t):
                pe.wait_ge(norm_ok, 12 + 2 * t + 2)
            dense("cq", 1, lambda t, m: [(wcq[:, c, :], half(xn[:, c, :], t)) for c in range(C)], ready)
            pe.wait_ge(ev["cq"], 2)
            pe.wait_ge(wcv_ok, 1)
            pe.wait_ge(load_w1att, 32)
            attention(1)

            def ready(t):
                pe.wait_ge(A["c_ev"], done(1, "c_ev"))
                pe.wait_ge(load_cd, 16)
            dense("cd", 2, lambda t, m: [(wcd[:, m * P:(m + 1) * P], half(cT, t))], ready)

            norm(4, False)
            for t in range(2):
                if t == 0:
                    pe.wait_ge(load_gu, 64)
                pe.wait_ge(xe_l, 4 + t + 1)
                for m in range(FC1):
                    rows = min(P, FF1 - m * P)
                    if m >= 2:
                        pe.wait_ge(gu_h, t * FC1 + m - 1)
                    for g in range(2):
                        for n in range(4):
                            e, c = n // 2, n % 2
                            last = pe.matmul(ps[0:rows, 4 * t + (2 * m + g) % 4, 0:HALF],
                                             wgu[:, g, e, c, m * P:m * P + rows], half(xe[:, e, c, :], t),
                                             start=n == 0, stop=n == 3)
                        last.then_inc(mm["gu"], 1)
                if t == 0:
                    pe.wait_ge(load_down, 64)
                pe.wait_ge(ev["gu"], t * FC1 + FC1)
                for m in range(C):
                    for n in range(2 * FC1):
                        e, c = n // FC1, n % FC1
                        rows = min(P, FF1 - c * P)
                        last = pe.matmul(bank(t, m), wdown[0:rows, e, c, m * P:(m + 1) * P], hexp[0:rows, e, c, :],
                                         start=n == 0, stop=n == 2 * FC1 - 1)
                    last.then_inc(mm["dn"], 1)

            for l in (2, 3):
                name = f"g{l}"
                pe.wait_ge(load_w23, 48 * (l - 1))
                if l == 2:
                    pe.wait_ge(ev["dn"], 4)
                else:
                    pe.wait_ge(norm_ok, 24)
                attention(l)

                def ready(t):
                    pe.wait_ge(A["c_ev"], done(l, "c_ev"))
                dense(name, 2, lambda t, m: [(wgate[:, n, m * P:(m + 1) * P], half((x if n < 2 else mc)[:, n % 2, :], t))
                                             for n in range(4)], ready)
                norm(l + 3, False)

        @block.scalar
        def _(act):
            for n in STARTED_BY["scalar"]:
                act.sem_inc(A[n], LEAD)
            act.sem_inc(sa_e, LEAD)
            act.sem_inc(sa_pt, LEAD)
            act.sem_inc(sa_out, LEAD)

            def bank(t, m):
                return ps[:, 4 * t + m % 4, 0:HALF]

            def tok(ap, t):
                return ap[:, :, t * HALF:(t + 1) * HALF]

            def norm(n, centre, eps):
                for t in range(2):
                    if centre:
                        act.wait_ge(centred, 2 * n + t + 1)
                        src = xc
                    else:
                        x_ready(n, t)
                        src = x
                    act.activation(tok(xn, t), tok(src, t), ACT.Square).then_inc(squared, 1)
                for t in range(2):
                    act.wait_ge(var_mm, 2 * n + t + 1)
                    act.activation(rstd[:, t * HALF:(t + 1) * HALF], bank(t, 1), ACT.Sqrt, bias=eps[:, 0:1],
                                   scale=1.0 / D)\
                       .then_inc(std_ok, 1)

            def x_ready(n, t):
                if n == 2:
                    act.wait_ge(ev["f2"], 2 * t + 2)
                elif n == 3:
                    act.wait_ge(ev["d1"], 2 * t + 2)
                elif n == 4:
                    act.wait_ge(ev["cd"], 2 * t + 2)
                else:
                    act.wait_ge(fuse, 4 * (n - 5) + 2 * t + 2)

            def attention(l):
                a = ATTS[l]
                groups, tiles, ring = a["groups"], a["tiles"], a["ring"]
                nt, ngr = len(tiles), len(groups)
                scale = 1.0 if l < 2 else D ** -0.5

                def q_hi(i, j, xq):
                    wait(act, l, "q_mm", i, j, xq + 1)
                    c0, c1 = q_cols(a, xq)
                    act.activation(qhi[:, j % 2, c0:c1], ps[:, xq % 3, 0:c1 - c0], ACT.Copy, scale=scale)\
                       .then_inc(A["q_hi"], 1)

                def p_exp(i, j, g, u):
                    s = slot_of(a, g, u, j)
                    m = s_cols(a)
                    wait(act, l, "nmax", i, j, unit_index(a, g, u) + 1)
                    act.activation(wide[0:m, s, :], wide[0:m, s, :], ACT.Exp, bias=negmax[0:m, s:s + 1], scale=-1.0,
                                   accum_out=den[0:m, s:s + 1]).then_inc(A["p_exp"], 1)

                def pt_hi(i, j, k, c):
                    tt = k * nt + c
                    kr = chunk_rows(tiles[c][0])
                    w = sum(groups[k]) * len(tiles[c])
                    wait(act, l, "pv_mm", i, j, tt - ring + 1)
                    wait(act, l, "t_mm", i, j, tt + 1)
                    act.activation(pthi[0:kr, tt % ring, 0:w], ps[0:kr, 3 + tt % ring, 0:w], ACT.Copy)\
                       .then_inc(A["pt_hi"], 1)

                def rb_out(i, j, k):
                    g_par = (k if ngr > 1 else j) % 2
                    w = sum(groups[k])
                    wait(act, l, "o_ev", i, j, k - 1)
                    wait(act, l, "rb_mm", i, j, k + 1)
                    act.activation(rbc[:, g_par, 0:w], ps[:, 7, 0:w], ACT.Copy).then_inc(A["rb_sb"], 1)

                def c_out(i, j):
                    b = i * 2 + j
                    for xq in range(a["c_pieces"]):
                        wait(act, l, "c_mm", i, j, xq + 1)
                        if l == 0:
                            dst, w = big8[:, 4 * xq:4 * xq + 4, bass.ds(b * S, S)], 4
                        elif l == 1:
                            dst, w = cT[:, bass.ds(b * S, S)].unsqueeze(1), 1
                        else:
                            dst, w = mc[:, :, bass.ds(b * S, S)], 2
                        act.activation(dst, ps[:, 7, 0:w * S].rearrange("p (c t) -> p c t", c=w), ACT.Copy)\
                           .then_inc(A["c_ev"], 1)

                def step(i, j, k, nxt):
                    last = k == ngr - 1
                    items = plan(a, k, nxt)
                    bi = next_batch(i, j) if last else (i, j)
                    for s in range(nt + 2):
                        if s < nt:
                            pt_hi(i, j, k, s)
                        for at_slot, it in items:
                            if at_slot == s and it[0] == "q":
                                q_hi(*bi, it[1])
                        for at_slot, it in items:
                            if at_slot == s - 1 and it[0] == "s" and it[3] == 2:
                                p_exp(*bi, it[1], it[2])
                        if s == a["rb_slot"] + 1:
                            rb_out(i, j, k)
                    if last:
                        c_out(i, j)

                for xq in range(len(a["q_pieces"])):
                    q_hi(0, 0, xq)
                for u in range(len(groups[0])):
                    p_exp(0, 0, 0, u)
                with act.Fori(0, B // 2 - 1) as i:
                    for j in range(2):
                        for k in range(ngr):
                            step(i, j, k, True)
                for j in range(2):
                    for k in range(ngr):
                        step(B // 2 - 1, j, k, j == 0)

            act.wait_ge(load_consts, 16 * 8)
            act.activation(tgate[:, :], tgate[:, :], ACT.Tanh).then_inc(gates_ok, 1)
            act.wait_ge(consts, 1)
            norm(0, True, eps5)
            act.wait_ge(consts, 2)
            for t in range(2):
                for m in range(8):
                    act.wait_ge(mm["q0"], 8 * t + m + 1)
                    act.activation(big8[:, m, t * HALF:(t + 1) * HALF], bank(t, m), ACT.Copy, scale=DH0 ** -0.5)\
                       .then_inc(ev["q0"], 1)
            attention(0)
            norm(1, True, eps5)
            for t in range(2):
                for m in range(8):
                    act.wait_ge(mm["f1"], 8 * t + m + 1)
                    act.activation(big8[:, m, t * HALF:(t + 1) * HALF], bank(t, m), ACT.Gelu).then_inc(ev["f1"], 1)
            norm(2, False, eps6)
            for t in range(2):
                for m in range(4):
                    act.wait_ge(mm["qk"], 4 * t + m + 1)
                    act.activation(qk[:, m, t * HALF:(t + 1) * HALF], bank(t, m), ACT.Copy).then_inc(ev["qk"], 1)
            for b in range(B):
                act.wait_ge(mm["vt"], b + 1)
                act.activation(vtok[:, b, :], ps[0:S, b, 0:D], ACT.Copy).then_inc(ev["vt"], 1)

            def sa_exp(i, j):
                act.wait_ge(sa_sub, i * 2 + (LEAD + j + 1))
                act.activation(sself[:, :, :], sself[:, :, :], ACT.Exp).then_inc(sa_e, 1)

            def sa_rest(i, j):
                for n in range(4):
                    act.wait_ge(sa_t, i * 8 + (4 * j + n + 1))
                    act.activation(ptself[:, 4 * n:4 * n + 4, :], ps[0:S, 4 + n % 2, 0:4 * S]
                                   .rearrange("p (h q) -> p h q", h=4), ACT.Copy).then_inc(sa_pt, 1)
                act.wait_ge(sa_ctt, i * 2 + (LEAD + j + 1))
                act.activation(ctxT[:, :, bass.ds((i * 2 + j) * S, S)],
                               ps[:, 7, 0:2 * S].rearrange("p (c t) -> p c t", c=C), ACT.Copy).then_inc(sa_out, 1)

            with act.Fori(0, B // 2) as i:
                for j in range(2):
                    sa_exp(i, j)
                    sa_rest(i, j)

            norm(3, False, eps6)
            for t in range(2):
                act.wait_ge(mm["cq"], t + 1)
                act.activation(cq[:, t * HALF:(t + 1) * HALF], bank(t, 0), ACT.Copy, scale=float(np.float32(CHD1 ** -0.5)))\
                   .then_inc(ev["cq"], 1)
            attention(1)
            norm(4, False, eps6)
            for t in range(2):
                for m in range(FC1):
                    rows = min(P, FF1 - m * P)
                    act.wait_ge(mm["gu"], 2 * (t * FC1 + m) + 1)
                    if t * FC1 + m >= 2:
                        act.wait_ge(gu_h, t * FC1 + m - 1)
                    act.activation(gsilu[0:rows, m % 2, :], ps[0:rows, 4 * t + (2 * m) % 4, 0:HALF], ACT.Silu)\
                       .then_inc(gu_silu, 1)
            for l in (2, 3):
                attention(l)
                name = f"g{l}"
                for t in range(2):
                    for m in range(C):
                        act.wait_ge(mm[name], 2 * t + m + 1)
                        act.activation(gate[:, m, t * HALF:(t + 1) * HALF], bank(t, m), ACT.Sigmoid,
                                       bias=vcol(f"b{l}", m)).then_inc(ev[name], 1)
                norm(l + 3, False, eps6)

        @block.vector
        def _(dve):
            for n in STARTED_BY["vector"]:
                dve.sem_inc(A[n], LEAD)
            for s_ in (sa_m, sa_x, sa_sub, sa_den, sa_ct):
                dve.sem_inc(s_, LEAD)
            steps = [0]

            def chain(ins):
                steps[0] += 1
                ins.then_inc(norm_step, 1)
                dve.wait_ge(norm_step, steps[0])

            def bank(t, m):
                return ps[:, 4 * t + m % 4, 0:HALF]

            def tok(ap, t):
                return ap[:, :, t * HALF:(t + 1) * HALF]

            def both(ap):
                return ap.unsqueeze(1).to_broadcast([P, C, HALF])

            def norm(n, centre, g, bvec, dst=xn):
                if centre:
                    for t in range(2):
                        dve.wait_ge(mean_mm, 2 * n + t + 1)
                        dve.scalar_tensor_tensor(tok(xc, t), both(bank(t, 0)), -1.0 / D, tok(x, t), ALU.mult, ALU.add)\
                           .then_inc(centred, 1)
                src = xc if centre else x
                for t in range(2):
                    r = rstd[:, t * HALF:(t + 1) * HALF]
                    dve.wait_ge(std_ok, 2 * n + t + 1)
                    chain(dve.reciprocal(r, r))
                    chain(dve.tensor_tensor(tok(dst, t), tok(src, t), both(r), ALU.mult))
                    for c in range(C):
                        d = dst[:, c, t * HALF:(t + 1) * HALF]
                        if bvec is None:
                            dve.tensor_scalar(d, d, vcol(g, c), None, ALU.mult).then_inc(norm_ok, 1)
                        else:
                            dve.tensor_scalar(d, d, vcol(g, c), vcol(bvec, c), ALU.mult, ALU.add).then_inc(norm_ok, 1)

            def residual(name, gcol=None):
                for t in range(2):
                    for m in range(C):
                        dve.wait_ge(mm[name], 2 * t + m + 1)
                        xs = x[:, m, t * HALF:(t + 1) * HALF]
                        if gcol is None:
                            dve.tensor_tensor(xs, bank(t, m), xs, ALU.add).then_inc(ev[name], 1)
                        else:
                            dve.scalar_tensor_tensor(xs, bank(t, m), tgate[:, gcol:gcol + 1], xs, ALU.mult, ALU.add)\
                               .then_inc(ev[name], 1)

            def expert_tokens(n, src, src_ready):
                for t in range(2):
                    src_ready(t)
                    dve.tensor_tensor(tok(xe[:, 0, :, :], t), tok(src, t), both(vm[:, t * HALF:(t + 1) * HALF]), ALU.mult)\
                       .then_inc(xe_v, 1)

            def attention(l):
                a = ATTS[l]
                groups, tiles, ring = a["groups"], a["tiles"], a["ring"]
                nu = sum(len(g) for g in groups)
                nt, ngr = len(tiles), len(groups)
                scale = 1.0 if l < 2 else D ** -0.5

                def t_hi(i, j):
                    wait(dve, l, "s_mm", i, j - 1, 0)
                    wait(dve, l, "raw_t", i, j, 16)
                    dve.tensor_copy(thi[:, j % 2, :], raw[:, 0:SK]).then_inc(A["t_hi"], 1)

                def n_hi(i, j):
                    wait(dve, l, "pv_mm", i, j - 1, 0)
                    wait(dve, l, "raw_n", i, j, 32)
                    dve.tensor_copy(nhi[:, j % 2, :, :], raw.rearrange("p (c d) -> p c d", c=CHUNKS)).then_inc(A["n_hi"], 1)

                def make_bias(i, j):
                    if l == 0:
                        wait(dve, l, "raw_m", i, j, 16)
                        dve.tensor_scalar(bias[:, j % 2, :], mask_u8, BIG, -BIG, ALU.mult, ALU.add)\
                           .then_inc(A["bias"], 1)

                def q_lo(i, j, xq):
                    c0, c1 = q_cols(a, xq)
                    wait(dve, l, "q_hi", i, j, xq + 1)
                    dve.scalar_tensor_tensor(qlo[:, j % 2, c0:c1], ps[:, xq % 3, 0:c1 - c0], scale,
                                             qhi[:, j % 2, c0:c1].bitcast(FP32), ALU.mult, ALU.subtract)\
                       .then_inc(A["q_lo"], 1)

                def s_neg(i, j, g, u, jj):
                    n = 3 * unit_index(a, g, u) + jj
                    s = slot_of(a, g, u, j)
                    m = s_cols(a)
                    k0, k1 = PIECES[jj]
                    if n == 0 and l > 0 and isinstance(i, int) and i == 0:
                        dve.wait_ge(bias_zero, l)
                    if jj == 0 and u == 0:
                        if n == 0 and l == 0:
                            wait(dve, l, "bias", i, j, 1)
                        wait(dve, l, "t_mm", i, j, (g - 1) * nt)
                    wait(dve, l, "s_mm", i, j, n + 1)
                    carry_wait(dve, "scores")
                    dve.tensor_tensor_reduce(out=wide[0:m, s, k0:k1], in0=ps[0:m, jj, 0:k1 - k0],
                                             in1=bias[0:m, j % 2 if l == 0 else 0, k0:k1], scale=-1.0, scalar=FMAX,
                                             op0=ALU.add, op1=ALU.min, accum_out=negmin3[0:m, s, jj:jj + 1])\
                       .then_inc(A["s_neg"], 1)

                def nmax(i, j, g, u):
                    s = slot_of(a, g, u, j)
                    m = s_cols(a)
                    wait(dve, l, "s_neg", i, j, 3 * unit_index(a, g, u) + 3)
                    dve.tensor_reduce(negmax[0:m, s:s + 1], negmin3[0:m, s, :], AX.X, ALU.min).then_inc(A["nmax"], 1)

                def rden(i, j, g, u):
                    s = slot_of(a, g, u, j)
                    m = s_cols(a)
                    wait(dve, l, "p_exp", i, j, unit_index(a, g, u) + 1)
                    dve.reciprocal(rdn[0:m, s:s + 1], den[0:m, s:s + 1]).then_inc(A["rden"], 1)

                def pt_lo(i, j, k, c):
                    tt = k * nt + c
                    kr = chunk_rows(tiles[c][0])
                    w = sum(groups[k]) * len(tiles[c])
                    wait(dve, l, "pt_hi", i, j, tt + 1)
                    dve.tensor_tensor(ptlo[0:kr, tt % ring, 0:w], ps[0:kr, 3 + tt % ring, 0:w],
                                      pthi[0:kr, tt % ring, 0:w].bitcast(FP32), ALU.subtract).then_inc(A["pt_lo"], 1)

                def o_ev(i, j, k):
                    g_par = (k if ngr > 1 else j) % 2
                    w = sum(groups[k])
                    c0 = unit_col(a, k, 0)
                    if k == 0:
                        wait(dve, l, "c_mm", i, j, 0)
                    wait(dve, l, "rb_sb", i, j, k + 1)
                    wait(dve, l, "pv_mm", i, j, (k + 1) * nt)
                    dve.tensor_tensor(outT[:, c0:c0 + w], ps[:, 6, 0:w], rbc[:, g_par, 0:w], ALU.mult)\
                       .then_inc(A["o_ev"], 1)

                def step(i, j, k, nxt):
                    last = k == ngr - 1
                    items = plan(a, k, nxt)
                    bi = next_batch(i, j) if last else (i, j)
                    nb = next_batch(i, j)
                    for s in range(nt + 2):
                        for at_slot, it in items:
                            if at_slot == s:
                                if it[0] == "q":
                                    q_lo(*bi, it[1])
                                else:
                                    s_neg(*bi, *it[1:])
                                    if it[3] == 2:
                                        nmax(*bi, it[1], it[2])
                        if s < nt:
                            pt_lo(i, j, k, s)
                        for at_slot, it in items:
                            if at_slot == s - 2 and it[0] == "s" and it[3] == 2:
                                rden(*bi, it[1], it[2])
                        if nxt and ngr > 1:
                            if k == 0 and s == 3:
                                t_hi(*nb)
                            if k == 1 and s == 3:
                                n_hi(*nb)
                            if k == 1 and s == 6:
                                make_bias(*nb)
                    for at_slot, it in items:
                        if at_slot > nt - 1 and it[0] == "s" and it[3] == 2:
                            rden(*bi, it[1], it[2])
                    o_ev(i, j, k)

                def step_narrow(i, j, nxt):
                    nb = next_batch(i, j)
                    if nxt:
                        t_hi(*nb)
                    step(i, j, 0, nxt)
                    if nxt:
                        n_hi(*nb)

                t_hi(0, 0)
                make_bias(0, 0)
                for xq in range(len(a["q_pieces"])):
                    q_lo(0, 0, xq)
                for u in range(len(groups[0])):
                    for jj in range(3):
                        s_neg(0, 0, 0, u, jj)
                    nmax(0, 0, 0, u)
                n_hi(0, 0)
                for u in range(len(groups[0])):
                    rden(0, 0, 0, u)
                with dve.Fori(0, B // 2 - 1) as i:
                    for j in range(2):
                        for k in range(ngr):
                            if ngr > 1:
                                step(i, j, k, True)
                            else:
                                step_narrow(i, j, True)
                for j in range(2):
                    for k in range(ngr):
                        if ngr > 1:
                            step(B // 2 - 1, j, k, j == 0)
                        else:
                            step_narrow(B // 2 - 1, j, j == 0)

            dve.wait_ge(cossin_mm, 1)
            dve.tensor_copy(cossin[:, :, :], ps[:, 7, 0:2 * S].rearrange("p (n s) -> p n s", n=2)).then_inc(cossin_ok, 1)
            norm(0, True, "ln_q_g", "ln_q_b")
            attention(0)
            dve.wait_ge(gates_ok, 1)
            residual("o0", 0)
            norm(1, True, "ln_ff_g", "ln_ff_b")
            residual("f2", 1)
            norm(2, False, "ln_in", None)
            expert_tokens(0, xn, lambda t: dve.wait_ge(norm_ok, 8 + 2 * t + 2))
            for t in range(2):
                for m in range(4):
                    n = 4 * t + m
                    q4 = qk[:, m, t * HALF:(t + 1) * HALF].rearrange("p (b s) -> p b s", s=S)
                    r4 = rotated[:, n % 2, :].rearrange("p (b s) -> p b s", s=S)
                    cos4 = cossin[:, 0, :].unsqueeze(1).to_broadcast([P, 4, S])
                    sin4 = cossin[:, 1, :].unsqueeze(1).to_broadcast([P, 4, S])
                    dve.wait_ge(mm["rt"], n + 1)
                    if n >= 2:
                        dve.wait_ge(rope, 2 * (n - 1))
                    dve.tensor_tensor(r4, bank(t, m).rearrange("p (b s) -> p b s", s=S), sin4, ALU.mult).then_inc(rt_s, 1)
                    dve.tensor_tensor(q4, q4, cos4, ALU.mult).then_inc(rope, 1)
                    dve.wait_ge(rope, 2 * n + 1)
                    dve.wait_ge(rt_s, n + 1)
                    if m < 2:
                        chain(dve.tensor_tensor(q4, q4, r4, ALU.add))
                        dve.tensor_scalar(q4, q4, HD1 ** -0.5, None, ALU.mult).then_inc(rope, 1)
                    else:
                        dve.tensor_tensor(q4, q4, r4, ALU.add).then_inc(rope, 1)

            def sa_soft(i, j):
                for n in range(4):
                    dve.wait_ge(sa_s, i * 8 + (4 * j + n + 1))
                    if n == 0:
                        dve.wait_ge(sa_pt, i * 8 + (LEAD + 4 * j))
                    dve.tensor_tensor(sself[:, 4 * n:4 * n + 4, :],
                                      ps[0:S, n, 0:4 * S].rearrange("p (h q) -> p h q", h=4),
                                      causal.unsqueeze(1).to_broadcast([S, 4, S]), ALU.add).then_inc(sa_m, 1)
                dve.wait_ge(sa_m, i * 8 + (LEAD + 4 * j + 4))
                dve.tensor_reduce(smax, sself[:, :, :], AX.X, ALU.max).then_inc(sa_x, 1)
                dve.wait_ge(sa_x, i * 2 + (LEAD + j + 1))
                dve.tensor_tensor(sself[:, :, :], sself[:, :, :], smax.unsqueeze(2).to_broadcast([S, HEADS, S]),
                                  ALU.subtract).then_inc(sa_sub, 1)

            def sa_norm(i, j):
                dve.wait_ge(sa_e, i * 2 + (LEAD + j + 1))
                dve.tensor_reduce(ssum, sself[:, :, :], AX.X, ALU.add).then_inc(sa_den, 1)
                dve.wait_ge(sa_den, i * 4 + (LEAD + 2 * j + 1))
                dve.reciprocal(srec, ssum).then_inc(sa_den, 1)
                dve.wait_ge(sa_den, i * 4 + (LEAD + 2 * j + 2))
                dve.wait_ge(sa_ctt, i * 2 + (LEAD + j))
                dve.wait_ge(sa_c, i * 2 + (j + 1))
                dve.tensor_tensor(ctok.rearrange("p (h d) -> p h d", h=HEADS),
                                  ps[0:S, 6, 0:D].rearrange("p (h d) -> p h d", h=HEADS),
                                  srec.unsqueeze(2).to_broadcast([S, HEADS, HD1]), ALU.mult).then_inc(sa_ct, 1)

            smax, ssum, srec = rstat[0:S, 0:16], rstat[0:S, 16:32], rstat[0:S, 32:48]
            with dve.Fori(0, B // 2) as i:
                for j in range(2):
                    sa_soft(i, j)
                    sa_norm(i, j)

            expert_tokens(1, ctxT, lambda t: dve.wait_ge(sa_out, LEAD + 4 * t + 4))
            residual("d1")
            norm(3, False, "ln_cross", None)
            attention(1)
            residual("cd")
            norm(4, False, "ln_post", None)
            expert_tokens(2, xn, lambda t: dve.wait_ge(norm_ok, 16 + 2 * t + 2))
            for t in range(2):
                for m in range(FC1):
                    n = t * FC1 + m
                    rows = min(P, FF1 - m * P)
                    dve.wait_ge(mm["gu"], 2 * n + 2)
                    dve.wait_ge(gu_silu, n + 1)
                    if n >= 1:
                        dve.wait_ge(ev["gu"], n)
                    dve.tensor_tensor(hgu[0:rows, :], ps[0:rows, 4 * t + (2 * m + 1) % 4, 0:HALF],
                                      gsilu[0:rows, m % 2, :], ALU.mult).then_inc(gu_h, 1)
                for m in range(C):
                    dve.wait_ge(mm["dn"], 2 * t + m + 1)
                    xs = x[:, m, t * HALF:(t + 1) * HALF]
                    dve.tensor_tensor(xs, bank(t, m), xs, ALU.add).then_inc(ev["dn"], 1)
            for l in (2, 3):
                attention(l)
                name = f"g{l}"
                for t in range(2):
                    for m in range(C):
                        dve.wait_ge(ev[name], 2 * t + m + 1)
                        gs = gate[:, m, t * HALF:(t + 1) * HALF]
                        xs = x[:, m, t * HALF:(t + 1) * HALF]
                        chain(dve.tensor_tensor(gs, gs, mc[:, m, t * HALF:(t + 1) * HALF], ALU.mult))
                        if m == 0:
                            dve.wait_ge(mm[name], 2 * t + 2)
                        dve.tensor_tensor(xs, xs, gs, ALU.add).then_inc(fuse, 1)
                norm(l + 3, False, f"n{l}", None, dst=x)

        @block.gpsimd
        def _(pool):
            for n in STARTED_BY["gpsimd"]:
                pool.sem_inc(A[n], LEAD)
            pool.sem_inc(sa_kbd, LEAD)
            pool.memset(eps5[:, :], 1e-5)
            pool.memset(eps6[:, :], 1e-6)
            pool.memset(raw, 0.0)
            for q in (qhi, qlo):
                pool.memset(q[:, :, HEADS * S:].bitcast(FP32), 0.0)
            pool.memset(vm[:, :], 0.0)
            pool.memset(ones[:, :], 1.0).then_inc(consts, 1)

            pool.wait_ge(load_consts, 16 * 8)
            pool.tensor_copy(pos_f, pos_i).then_inc(pos_ok, 1)
            pool.wait_ge(pos_ok, 1)
            pool.tensor_scalar(pos_neg, pos_f, 0.0, float(S), ALU.is_lt, ALU.mult).then_inc(pos_ok, 1)
            pool.wait_ge(pos_ok, 2)
            pool.tensor_tensor(pos_f, pos_f, pos_neg, ALU.add).then_inc(pos_ok, 1)
            pool.wait_ge(pos_ok, 3)
            pool.tensor_scalar(pos_f, pos_f, 0.0, float(S - 1), ALU.max, ALU.min).then_inc(pos_ok, 1)
            pool.wait_ge(pos_ok, 4)
            pool.tensor_scalar(onehot, pos_f[0:S, :], vec[0:S, 22:23], None, ALU.is_equal).then_inc(pos_ok, 1)

            pool.tensor_scalar(tt_one.rearrange("p b s -> p (b s)"), tt_i, 1.0, None, ALU.is_equal).then_inc(vm_step, 1)
            pool.wait_ge(vm_step, 1)
            pool.tensor_tensor(vm[:, :].rearrange("p (b s) -> p b s", b=B)[:, :, 0:S - 1],
                               tt_one[:, :, 0:S - 1], tt_one[:, :, 1:S], ALU.mult).then_inc(consts, 1)

            def tok(ap, t):
                return ap[:, :, t * HALF:(t + 1) * HALF]

            def expert_tokens(n, src):
                for t in range(2):
                    pool.wait_ge(xe_v, 2 * n + t + 1)
                    pool.tensor_tensor(tok(xe[:, 1, :, :], t), tok(src, t), tok(xe[:, 0, :, :], t), ALU.subtract)\
                        .then_inc(xe_l, 1)

            def attention(l):
                a = ATTS[l]
                groups = a["groups"]
                ngr = len(groups)

                def t_lo(i, j):
                    wait(pool, l, "t_hi", i, j, 1)
                    pool.tensor_tensor(tlo[:, j % 2, :], raw[:, 0:SK], thi[:, j % 2, :].bitcast(FP32), ALU.subtract)\
                        .then_inc(A["t_lo"], 1)

                def n_lo(i, j):
                    wait(pool, l, "n_hi", i, j, 1)
                    pool.tensor_tensor(nlo[:, j % 2, :, :], raw.rearrange("p (c d) -> p c d", c=CHUNKS),
                                       nhi[:, j % 2, :, :].bitcast(FP32), ALU.subtract).then_inc(A["n_lo"], 1)

                def make_qbd(i, j):
                    if l == 1:
                        wait(pool, l, "q_mm", i, j, 0)
                        wait(pool, l, "q_in", i, j, 16)
                        pool.tensor_tensor(qbd1.rearrange("p (h q) -> p h q", h=HEADS),
                                           qb[:, j % 2, 0:S].unsqueeze(1).to_broadcast([P, HEADS, S]),
                                           hmask16[:, :].unsqueeze(2).to_broadcast([P, HEADS, S]), ALU.mult)\
                            .then_inc(A["qbd"], 1)

                def make_diag(i, j, g, u):
                    s = slot_of(a, g, u, j)
                    m = s_cols(a)
                    if u == 0:
                        wait(pool, l, "rb_mm", i, j, g)
                    wait(pool, l, "rden", i, j, unit_index(a, g, u) + 1)
                    pool.tensor_tensor(diag[0:m, u, 0:m], ident[0:m, 0:m], rdn[0:m, s:s + 1].to_broadcast([m, m]),
                                       ALU.mult).then_inc(A["diag"], 1)

                def step(i, j, k, nxt):
                    last = k == ngr - 1
                    if nxt and k == 0:
                        t_lo(*next_batch(i, j))
                    if nxt and k == 2:
                        make_qbd(*next_batch(i, j))
                    for _, it in plan(a, k, nxt):
                        if it[0] == "s" and it[3] == 2:
                            make_diag(*(next_batch(i, j) if last else (i, j)), it[1], it[2])
                    if nxt and k == min(1, ngr - 1):
                        n_lo(*next_batch(i, j))

                make_qbd(0, 0)
                t_lo(0, 0)
                n_lo(0, 0)
                for u in range(len(groups[0])):
                    make_diag(0, 0, 0, u)
                with pool.Fori(0, B // 2 - 1) as i:
                    for j in range(2):
                        for k in range(ngr):
                            step(i, j, k, True)
                for j in range(2):
                    for k in range(ngr):
                        step(B // 2 - 1, j, k, j == 0)

            attention(0)
            expert_tokens(0, xn)

            def make_kbd(i, j):
                pool.wait_ge(sa_in[j], i * 32 + 32)
                for c in range(C):
                    ins_ = pool.tensor_tensor(kbd[:, j, 8 * c:8 * c + 8, :],
                                              qkb[:, j, 2 + c, :].unsqueeze(1).to_broadcast([P, 8, S]),
                                              hmask8[:, :].unsqueeze(2).to_broadcast([P, 8, S]), ALU.mult)
                ins_.then_inc(sa_kbd, 1)

            with pool.Fori(0, B // 2) as i:
                for j in range(2):
                    make_kbd(i, j)
            expert_tokens(1, ctxT)
            pool.wait_ge(load_w1att, 32)
            pool.memset(watt[:, 0:2048], 0.0).then_inc(wcv_step, 1)
            pool.wait_ge(wcv_step, 1)
            pool.tensor_copy(watt[:, 0:16 * (P + CHD1)].rearrange("p (h n) -> p h n", h=HEADS)[:, :, 0:CHD1],
                             wcv.rearrange("p (h d) -> p h d", h=HEADS)).then_inc(wcv_ok, 1)
            pool.wait_ge(ev["cq"], 2)
            pool.memset(bias[:, 0, :], 0.0).then_inc(bias_zero, 1)
            attention(1)
            expert_tokens(2, xn)
            for t in range(2):
                if t == 1:
                    pool.wait_ge(mm["dn"], 2)
                for m in range(FC1):
                    n = t * FC1 + m
                    rows = min(P, FF1 - m * P)
                    pool.wait_ge(gu_h, n + 1)
                    pool.tensor_tensor(hexp[0:rows, 0, m, :], hgu[0:rows, :], vm[0:rows, t * HALF:(t + 1) * HALF],
                                       ALU.mult).then_inc(gu_v, 1)
                    pool.wait_ge(gu_v, n + 1)
                    pool.tensor_tensor(hexp[0:rows, 1, m, :], hgu[0:rows, :], hexp[0:rows, 0, m, :],
                                       ALU.subtract).then_inc(ev["gu"], 1)
            for l in (2, 3):
                if l == 2:
                    pool.wait_ge(mm["gu"], 4 * FC1)
                else:
                    pool.wait_ge(norm_ok, 24)
                pool.memset(bias[:, 0, :], 0.0).then_inc(bias_zero, 1)
                attention(l)

    return nc


def _columns(v):
    return v.reshape(C, P).T


def _chunks(w):
    return w.reshape(-1, P, w.shape[1]).transpose(1, 0, 2)


def _constants():
    f = np.float32
    d = np.arange(P) % HD1
    rot = np.zeros((P, P), f)
    rot[(np.arange(P) // HD1) * HD1 + (d + HD1 // 2) % HD1, np.arange(P)] = 1
    inv = (f(1.0) / f(10000.0) ** (np.arange(0, HD1, 2).astype(f) / f(HD1))).astype(f)
    ang = np.outer(np.arange(S).astype(f), inv).astype(f)[:, d % (HD1 // 2)]
    sign = np.where(d < HD1 // 2, f(-1), f(1))
    return dict(
        ident=np.eye(P, dtype=f), rot=rot, postab=np.concatenate([np.cos(ang), np.sin(ang) * sign], 1).astype(f),
        hmask8=(np.arange(P)[:, None] // HD1 == np.arange(8)[None]).astype(f),
        hmask16=(np.arange(P)[:, None] // CHD1 == np.arange(HEADS)[None]).astype(f),
        causal=np.where(np.tril(np.ones((S, S), bool)), f(0), f(-BIG)).astype(f))


def kernel(**inputs):
    import concourse.bacc as bacc
    from concourse.bass_utils import run_bass_kernel_spmd

    g = {k: np.asarray(v) for k, v in inputs.items()}
    g0 = lambda k: g["L0_xattn_" + k]
    g1 = lambda k: g["L1_xattn_" + k]
    ctx = g["ctx_1024"]
    wkv, ckv = g0("Wkv"), g1("ckv_w")
    vec = [g0("ln_q_g"), g0("ln_q_b"), g0("ln_ff_g"), g0("ln_ff_b"), g1("ln_in_w"), g1("ln_post_cross_w"),
           g1("ln_post_attn_w"), g["L2_xattn_norm_w"], g["L3_xattn_norm_w"], g["L2_xattn_b_gate"], g["L3_xattn_b_gate"]]
    f = np.float32
    arrays = dict(
        xT=g["x"].reshape(T, D).T.reshape(C, P, T).transpose(1, 0, 2), ctx=ctx, ctxT=ctx.transpose(0, 2, 1),
        mask=g["mask_BxS2_bk0"], tt=g["mask_BxS_ik0"].reshape(T), pos=g["pos_1xS"].reshape(S),
        vec=np.concatenate([_columns(v) for v in vec] + [np.arange(P, dtype=f)[:, None], np.zeros((P, 1), f)], 1),
        gates=np.concatenate([g0("attn_gate"), g0("ff_gate")]),
        wq=_chunks(g0("Wq")), wk0=_chunks(wkv[:, :F0].T), wv0=wkv[:, F0:], wo=_chunks(g0("Wo")),
        w1=_chunks(g0("W1")), w2=_chunks(g0("W2")),
        qkv=np.stack([_chunks(g1("v_qkv")), _chunks(g1("l_qkv"))]),
        dense1=np.stack([_chunks(g1("v_dense")), _chunks(g1("l_dense"))]),
        wcq=_chunks(g1("cq_w")), wck=ckv[:, :DM].T, wcv=ckv[:, DM:], wcd=g1("cdense_w"),
        gu=np.stack([np.stack([_chunks(g1(e + k)) for e in ("v_", "l_")]) for k in ("gate", "up")]),
        down=np.stack([g1("v_down"), g1("l_down")]),
        wmem=np.stack([_chunks(g[f"L{n}_xattn_W_mem"]) for n in (2, 3)]),
        wmemT=np.stack([g[f"L{n}_xattn_W_mem"].T for n in (2, 3)]),
        wgate=np.stack([_chunks(g[f"L{n}_xattn_W_gate"].T) for n in (2, 3)]),
        **_constants())
    nc = bacc.Bacc("TRN2", target_bir_lowering=False, num_devices=1)
    maps, aps = {}, {}
    for n, v in arrays.items():
        maps["in_" + n] = np.ascontiguousarray(v)
        aps[n] = nc.dram_tensor("in_" + n, v.shape, mybir.dt.from_np(v.dtype), kind="ExternalInput").ap()
    out = nc.dram_tensor("out_xT", (P, C, T), FP32, kind="ExternalOutput").ap()
    build_layers(nc, aps, out)
    r = run_bass_kernel_spmd(nc, [maps], core_ids=[0])
    y = r.results[0]["out_xT"]
    return y.transpose(2, 1, 0).reshape(B, S, D)
```

```python
import numpy as np
import concourse.bass as bass
from concourse import mybir
from contextlib import ExitStack

FP32 = mybir.dt.float32
FP32R = mybir.dt.float32r
U8 = mybir.dt.uint8
I32 = mybir.dt.int32
ALU = mybir.AluOpType
ACT = mybir.ActivationFunctionType
AX = mybir.AxisListType

P = 128
B, S, D = 8, 100, 256
T = B * S
HALF = T // 2
C = D // P
SK, DM = 1444, 128
HEADS = 16
DH0 = 64
F0 = 1024
HD1, CHD1 = 16, 8
FF1 = 688
FC1 = -(-FF1 // P)
BIG = 3.0e38
FMAX = 3.4e38

CHUNKS = 12
FULL = 10
TAIL = (SK - FULL * P) // 2
assert FULL * P + 2 * TAIL == SK


def chunk_rows(c):
    return P if c < FULL else TAIL


def chunk_start(c):
    return c * P if c < FULL else FULL * P + (c - FULL) * TAIL


PIECES = [(0, 512), (512, 1024), (1024, SK)]

WIDE = dict(groups=[[128] * 4, [128] * 3, [128] * 3, [128, 128, 64]],
            q_pieces=[(0, 3), (3, 6), (6, 8), (8, 11), (11, 14), (14, 16)],
            tiles=[[c] for c in range(CHUNKS)], ring=3, item_slots=8, c_slot=3, rb_slot=8,
            exp_lag=1, rden_lag=2)
NARROW = dict(groups=[[S]], q_pieces=[(0, 1)],
              tiles=[[0, 1, 2, 3], [4, 5, 6, 7], [8, 9], [10, 11]], ring=2, c_slot=1, rb_slot=3,
              exp_lag=2, rden_lag=4, s_slots=(0, 0, 1), q_slot=3, n_slot=1, t_slot=2)
ATTS = [dict(WIDE, kind=0, c_pieces=2), dict(WIDE, kind=1, c_pieces=1),
        dict(NARROW, kind=2, c_pieces=1), dict(NARROW, kind=3, c_pieces=1)]


def head_at(n):
    return 2 * n if n < HEADS // 2 else 2 * n - HEADS + 1


LEAD = 1024


def batch_counts(a):
    nu = sum(len(g) for g in a["groups"])
    ng, nt, nq = len(a["groups"]), len(a["tiles"]), len(a["q_pieces"])
    return dict(raw_t=16, raw_n=32, raw_m=16 if a["kind"] == 0 else 0, q_in=16,
                t_hi=1, n_hi=1, t_lo=1, n_lo=1, bias=1 if a["kind"] == 0 else 0,
                qbd=1 if a["kind"] == 1 else 0, q_mm=nq, q_hi=nq, q_lo=nq,
                s_mm=3 * nu, s_neg=3 * nu, nmax=nu, p_exp=nu, rden=nu, diag=nu,
                t_mm=ng * nt, pt_hi=ng * nt, pt_lo=ng * nt, pv_mm=ng * nt,
                rb_mm=ng, rb_sb=ng, o_ev=ng, c_mm=a["c_pieces"], c_ev=a["c_pieces"])


COUNTS = [batch_counts(a) for a in ATTS]
STARTED_BY = dict(sync=["raw_t", "raw_n", "raw_m", "q_in"],
                  vector=["t_hi", "n_hi", "bias", "q_lo", "s_neg", "nmax", "rden", "pt_lo", "o_ev"],
                  gpsimd=["t_lo", "n_lo", "qbd", "diag"],
                  scalar=["q_hi", "p_exp", "pt_hi", "rb_sb", "c_ev"],
                  tensor=["q_mm", "s_mm", "t_mm", "pv_mm", "rb_mm", "c_mm"])


def build_layers(nc, ins, out):
    ctx = ExitStack()
    with ctx:
        def sb(name, shape, dt=FP32):
            return ctx.enter_context(nc.sbuf_tensor(name, shape, dt))

        def sem(name):
            return ctx.enter_context(nc.semaphore(name))

        x = sb("x", [P, C, T])
        big = sb("big", [P, 8 * T])
        wide = sb("wide", [P, 7, SK])
        work = sb("work", [P, 9160])
        qhi = sb("qhi", [P, 2, 1664], FP32R)
        qlo = sb("qlo", [P, 2, 1664], FP32R)
        thi = sb("thi", [P, 2, SK], FP32R)
        tlo = sb("tlo", [P, 2, SK], FP32R)
        nhi = sb("nhi", [P, 2, CHUNKS, DM], FP32R)
        nlo = sb("nlo", [P, 2, CHUNKS, DM], FP32R)
        pthi = sb("pthi", [P, 3, 512], FP32R)
        ptlo = sb("ptlo", [P, 3, 512], FP32R)
        watt = sb("watt", [P, 2304])
        vec = sb("vec", [P, 24])
        ident = sb("ident", [P, P])
        ones = sb("ones", [P, P])
        hmask8 = sb("hmask8", [P, 8])
        hmask16 = sb("hmask16", [P, HEADS])
        eps5 = sb("eps5", [P, 1])
        eps6 = sb("eps6", [P, 1])
        vm = sb("vm", [P, T])
        cossin = sb("cossin", [P, 2, S])
        late = sb("late", [P, SK // 4])
        tgate = sb("tgate", [P, 2])
        negmin3 = sb("negmin3", [P, 7, 3])
        negmax = sb("negmax", [P, 7])
        den = sb("den", [P, 7])
        rdn = sb("rdn", [P, 7])
        ps = ctx.enter_context(nc.psum_tensor("ps", [P, 8, 512], FP32))

        mask_u8 = late[:, :].bitcast(U8)
        rot = late[:, 0:P]
        causal = late[0:S, P:P + S]
        rstat = late[0:S, P + S:P + S + 6 * HEADS].rearrange("p (j n) -> p j n", j=2)
        raw = work[:, 0:1536]
        outT = work[:, 1536:3136]
        bias = work[:, 3136:6024].rearrange("p (j k) -> p j k", j=2)
        rbc = work[:, 6024:7048].rearrange("p (j k) -> p j k", j=2)
        diag = work[:, 7048:7560].rearrange("p (j k) -> p j k", j=4)
        qb = work[:, 7560:9160].rearrange("p (j k) -> p j k", j=2)
        raw_narrow = wide[:, 5:7, :].rearrange("p u k -> p (u k)")[:, 0:1536]
        xe = work[:, 1536:4736].rearrange("p (e c t) -> p e c t", e=2, c=C)
        xn = work[:, 4736:6336].rearrange("p (c t) -> p c t", c=C)
        xc = work[:, 6336:7936].rearrange("p (c t) -> p c t", c=C)
        rstd = work[:, 7936:8736]
        rmask = work[:, 6336:7136].rearrange("p (e t) -> p e t", e=2)
        vtok = work[0:S, 6336:8384].rearrange("p (b d) -> p b d", b=B)
        wflat = wide[:, :, :].rearrange("p u k -> p (u k)")
        wq = wflat[:, 0:2048].rearrange("p (c n) -> p c n", c=C)
        wo = wflat[:, 0:2048].rearrange("p (c n) -> p c n", c=8)
        w1 = wflat[:, 2048:4096].rearrange("p (c n) -> p c n", c=C)
        w2 = wflat[:, 4096:6144].rearrange("p (c n) -> p c n", c=8)
        wqkv = wflat[:, 6144:9216].rearrange("p (e c n) -> p e c n", e=2, c=C)
        wcq = wflat[:, 9216:9472].rearrange("p (c n) -> p c n", c=C)
        wdn1 = wflat[:, 0:1024].rearrange("p (e c n) -> p e c n", e=2, c=C)
        kbd = wflat[:, 1024:4224].rearrange("p (j h q) -> p j h q", j=2, h=HEADS)
        sself = wflat[0:S, 4224:7424].rearrange("p (j h q) -> p j h q", j=2, h=HEADS)
        wgu = wflat[:, 0:5504].rearrange("p (g e c n) -> p g e c n", g=2, e=2, c=C)
        wdown = wflat[:, 5504:8576].rearrange("p (e c n) -> p e c n", e=2, c=FC1)
        gsilu = wflat[:, 8576:9376].rearrange("p (j t) -> p j t", j=2)
        hgu = wflat[:, 9376:9776]
        wcd = wflat[:, 9776:10032]
        wk0 = watt[:, 0:1024].rearrange("p (c n) -> p c n", c=8)
        wv0 = watt[:, 1024:2048]
        wck = watt[:, 2048:2176]
        wcv = watt[:, 2176:2304]
        wcvh = watt[:, 0:2048].rearrange("p (h n) -> p h n", h=HEADS)
        wmem = watt[:, 0:256].rearrange("p (c n) -> p c n", c=C)
        wmemT = watt[:, 256:512]
        wgate = watt[:, 512:1536].rearrange("p (c n) -> p c n", c=4)
        big8 = big[:, :].rearrange("p (c t) -> p c t", c=8)
        qk = big[:, 0:4 * T].rearrange("p (c t) -> p c t", c=4)
        qsb = big[:, 4 * T:4 * T + 4 * S].rearrange("p (j c t) -> p j c t", j=2, c=C)
        ptself = big[0:S, 5 * T:7 * T].rearrange("p (h q) -> p h q", h=HEADS)
        ctok = big[0:S, 7 * T + 512:7 * T + 768]
        cq = big[:, 0:T]
        cT = big[:, T:2 * T]
        qbd1 = big[:, 4 * T:6 * T]
        hexp = big[:, 0:12 * HALF].rearrange("p (e c t) -> p e c t", e=2, c=FC1)
        mc = big[:, 0:2 * T].rearrange("p (c t) -> p c t", c=C)
        gate = big[:, 2 * T:4 * T].rearrange("p (c t) -> p c t", c=C)
        ctxT = xn
        rotated = work[:, 4736:5536].rearrange("p (j t) -> p j t", j=2)
        postab = wflat[0:S, 4096:4096 + 2 * P]
        pos_i = wflat[:, 4352:4452].bitcast(I32)
        pos_f = wflat[:, 4452:4552]
        pos_neg = wflat[:, 4552:4652]
        onehot = wflat[0:S, 4652:4752]
        tt_i = big[:, 0:T].bitcast(I32)
        tt_one = big[:, T:2 * T].rearrange("p (b s) -> p b s", b=B)
        VEC = {n: k for k, n in enumerate(
            ["ln_q_g", "ln_q_b", "ln_ff_g", "ln_ff_b", "ln_in", "ln_cross", "ln_post", "n2", "n3", "b2", "b3"])}

        def raw_ctx(l):
            return raw if len(ATTS[l]["groups"]) > 1 else raw_narrow

        def vcol(name, c):
            return vec[:, 2 * VEC[name] + c:2 * VEC[name] + c + 1]

        A = {n: sem(n) for names in STARTED_BY.values() for n in names}
        passed = {n: sem(f"passed_{n}") for n in ("loads", "scores")}
        load_consts = sem("load_consts")
        load_x = [sem("load_x_first"), sem("load_x_second")]
        load_w0 = sem("load_w0")
        load_wo = sem("load_wo")
        load_w12 = sem("load_w12")
        load_qkv = sem("load_qkv")
        load_w1att = sem("load_w1att")
        load_d1 = sem("load_d1")
        load_rot = sem("load_rot")
        load_cd = sem("load_cd")
        load_gu = sem("load_gu")
        load_down = sem("load_down")
        load_w23 = sem("load_w23")
        consts = sem("consts")
        mean_mm = sem("mean_mm")
        centred = sem("centred")
        squared = sem("squared")
        var_mm = sem("var_mm")
        std_ok = sem("std_ok")
        norm_step = sem("norm_step")
        norm_ok = sem("norm_ok")
        gates_ok = sem("gates_ok")
        DENSE = ["q0", "o0", "f1", "f2", "qk", "rt", "vt", "d1", "cq", "cd", "gu", "dn", "g2", "g3"]
        mm = {n: sem(f"{n}_mm") for n in DENSE}
        ev = {n: sem(f"{n}_ev") for n in DENSE}
        rt_s = sem("rt_s")
        xe_v = sem("xe_v")
        xe_l = sem("xe_l")
        gu_h = sem("gu_h")
        gu_silu = sem("gu_silu")
        pos_ok = sem("pos_ok")
        cossin_mm = sem("cossin_mm")
        cossin_ok = sem("cossin_ok")
        bias_zero = sem("bias_zero")
        gu_v = sem("gu_v")
        vm_step = sem("vm_step")
        wcv_step = sem("wcv_step")
        fuse = sem("fuse")
        rope = sem("rope")
        sa_kbd = sem("sa_kbd")
        sa_s = sem("sa_s")
        sa_m = sem("sa_m")
        sa_x = sem("sa_x")
        sa_sub = sem("sa_sub")
        sa_e = sem("sa_e")
        sa_den = sem("sa_den")
        sa_t = sem("sa_t")
        sa_pt = sem("sa_pt")
        sa_c = sem("sa_c")
        sa_ct = sem("sa_ct")
        sa_ctt = sem("sa_ctt")
        sa_out = sem("sa_out")
        wcv_ok = sem("wcv_ok")
        stored = sem("stored")

        base = [{n: LEAD + B * sum(COUNTS[m][n] for m in range(l)) for n in A} for l in range(5)]

        def at(l, name, i, j, k=0):
            n = COUNTS[l][name]
            return i * (2 * n) + (base[l][name] + j * n + k)

        def done(l, name):
            return base[l + 1][name]

        def wait(eng, l, name, i, j, k=0):
            eng.wait_ge(A[name], at(l, name, i, j, k))

        def carry_wait(eng, name):
            eng.sem_inc(passed[name], 1)

        def next_batch(i, j):
            return i, j + 1

        def q_batch(a, i, j):
            return (i, j + 1) if len(a["groups"]) > 1 else (i, j + 2)

        def plan(a, k, nxt, after_next=False):
            groups = a["groups"]
            if len(groups) == 1:
                return ([(a["s_slots"][j], ("s", 0, 0, j)) for j in range(3)] if nxt else []) + \
                    ([(a["q_slot"], ("q", 0))] if after_next else [])
            last = k == len(groups) - 1
            ng = 0 if last else k + 1
            items = [("s", ng, u, j) for u in range(len(groups[ng])) for j in range(3)] if nxt or not last else []
            q_items = [("q", x) for x in range(len(a["q_pieces"]))] if nxt else []
            if k == len(groups) - 2:
                items += q_items
            n = len(items)
            return [(m * a["item_slots"] // n, it) for m, it in enumerate(items)]

        def unit_index(a, g, u):
            return sum(len(x) for x in a["groups"][:g]) + u

        def unit_col(a, g, u):
            return sum(sum(x) for x in a["groups"][:g]) + sum(a["groups"][g][:u])

        def slot_of(a, g, u, j):
            odd = (g if len(a["groups"]) > 1 else j) % 2
            return 4 * odd + u

        def q_cols(a, x):
            h0, h1 = a["q_pieces"][x]
            return h0 * S, h1 * S

        def q_need(a, col):
            return next(x + 1 for x in range(len(a["q_pieces"])) if q_cols(a, x)[1] >= min(col, q_cols(a, len(a["q_pieces"]) - 1)[1]))

        def s_cols(a):
            return P if a["kind"] < 2 else S

        block = ctx.enter_context(nc.Block())

        @block.sync
        def _(sp):
            for n in STARTED_BY["sync"]:
                sp.sem_inc(A[n], LEAD)
            for t in range(2):
                sp.dma_start(x[:, :, t * HALF:(t + 1) * HALF], ins["xT"][:, :, t * HALF:(t + 1) * HALF])\
                  .then_inc(load_x[t], 16)
            for dst, src in [(vec[:, :], ins["vec"]), (ident[:, :], ins["ident"]), 
                             (hmask8[:, :], ins["hmask8"]), (hmask16[:, :], ins["hmask16"]),
                             (tgate[:, :], ins["gates"].partition_broadcast(P)),
                             (postab, ins["postab"]), (pos_i, ins["pos"].partition_broadcast(P)),
                             (tt_i, ins["tt"].partition_broadcast(P))]:
                sp.dma_start(dst, src).then_inc(load_consts, 16)
            sp.dma_start(wq, ins["wq"]).then_inc(load_w0, 16)
            sp.dma_start(wk0, ins["wk0"]).then_inc(load_w0, 16)
            sp.dma_start(wv0, ins["wv0"]).then_inc(load_w0, 16)

            def attention_loads(l, ready=None, first=False):
                narrow = len(ATTS[l]["groups"]) == 1

                def load_ctxT(i, j):
                    wait(sp, l, "t_lo" if narrow else "n_lo", i, j - 1, 1)
                    carry_wait(sp, "loads")
                    sp.dma_start(raw[:, 0:SK], ins["ctxT"][bass.ds(sp.snap(i * 2 + j), 1), :, :]
                                 .rearrange("o p k -> p (o k)")).then_inc(A["raw_t"], 16)

                def load_queries(i, j):
                    b = sp.snap(i * 2 + j)
                    ready(i, j)
                    if l == 1:
                        wait(sp, l, "qbd", i, j - 1, 0)
                    elif narrow:
                        wait(sp, l, "q_mm", i, j, 0)
                    else:
                        wait(sp, l, "q_mm", i, j - 1, 0)
                    carry_wait(sp, "loads")
                    if l == 0:
                        sp.dma_start(qb[:, j, :].rearrange("p (c t) -> p c t", c=8),
                                     big8[:, :, bass.ds(b * S, S)]).then_inc(A["q_in"], 16)
                    elif l == 1:
                        sp.dma_start(qb[:, j, 0:S], cq[:, bass.ds(b * S, S)]).then_inc(A["q_in"], 16)
                    else:
                        sp.dma_start(qb[:, j % 2, 0:2 * S].rearrange("p (c t) -> p c t", c=C),
                                     x[:, :, bass.ds(b * S, S)]).then_inc(A["q_in"], 16)

                def load_mask(i, j):
                    wait(sp, l, "bias", i, j - 1, 1)
                    carry_wait(sp, "loads")
                    sp.dma_start(mask_u8, ins["mask"][bass.ds(sp.snap(i * 2 + j), 1), :].rearrange("o k -> (o k)")
                                 .partition_broadcast(P)).then_inc(A["raw_m"], 16)

                def load_ctx(i, j):
                    if narrow:
                        wait(sp, l, "n_lo", i, j - 1, 1)
                    else:
                        wait(sp, l, "t_lo", i, j, 1)
                    carry_wait(sp, "loads")
                    ctx_b = ins["ctx"][bass.ds(sp.snap(i * 2 + j), 1), :, :]
                    rawn = raw_ctx(l).rearrange("p (c d) -> p c d", c=CHUNKS)
                    sp.dma_start(rawn[:, 0:FULL, :], ctx_b[:, 0:FULL * P, :]
                                 .rearrange("o (c p) d -> p (o c) d", p=P)).then_inc(A["raw_n"], 16)
                    sp.dma_start(rawn[0:TAIL, FULL:CHUNKS, :], ctx_b[:, FULL * P:SK, :]
                                 .rearrange("o (c p) d -> p (o c) d", p=TAIL)).then_inc(A["raw_n"], 16)

                if first:
                    load_ctxT(0, 0)
                elif narrow:
                    load_queries(0, 0)
                    with sp.Fori(0, B // 2 - 1) as i:
                        for j in range(2):
                            load_ctxT(i, j + 1)
                            load_queries(i, j + 1)
                            load_ctx(i, j)
                    load_ctxT(B // 2 - 1, 1)
                    load_queries(B // 2 - 1, 1)
                    for j in range(2):
                        load_ctx(B // 2 - 1, j)
                else:
                    with sp.Fori(0, B // 2) as i:
                        for j in range(2):
                            load_ctxT(i, j)
                            load_queries(i, j)
                            if l == 0:
                                load_mask(i, j)
                            load_ctx(i, j)

            sp.wait_ge(consts, 2)
            attention_loads(0, lambda i, j: sp.wait_ge(ev["q0"], 16))
            sp.wait_ge(A["t_mm"], done(0, "t_mm"))
            sp.dma_start(wo, ins["wo"]).then_inc(load_wo, 16)
            sp.dma_start(w1, ins["w1"]).then_inc(load_w12, 16)
            sp.dma_start(w2, ins["w2"]).then_inc(load_w12, 16)
            for e in range(2):
                sp.dma_start(wqkv[:, e, :, :], ins["qkv"][e]).then_inc(load_qkv, 16)
            sp.dma_start(wcq, ins["wcq"]).then_inc(load_qkv, 16)
            sp.wait_ge(A["bias"], done(0, "bias"))
            sp.dma_start(rot, ins["rot"]).then_inc(load_rot, 16)
            sp.dma_start(causal, ins["causal"]).then_inc(load_rot, 16)
            sp.wait_ge(A["c_mm"], done(0, "c_mm"))
            sp.dma_start(wck, ins["wck"]).then_inc(load_w1att, 16)
            sp.dma_start(wcv, ins["wcv"]).then_inc(load_w1att, 16)
            sp.wait_ge(mm["o0"], 4)
            for e in range(2):
                sp.dma_start(wdn1[:, e, :, :], ins["dense1"][e]).then_inc(load_d1, 16)

            attention_loads(1, lambda i, j: sp.wait_ge(ev["cq"], 2))
            sp.wait_ge(A["n_lo"], done(1, "n_lo"))
            attention_loads(2, first=True)
            sp.wait_ge(A["t_mm"], done(1, "t_mm"))
            sp.dma_start(wcd, ins["wcd"]).then_inc(load_cd, 16)
            for g in range(2):
                for e in range(2):
                    sp.dma_start(wgu[:, g, e, :, :], ins["gu"][g, e]).then_inc(load_gu, 16)
            for e in range(2):
                sp.dma_start(wdown[:, e, 0:FC1 - 1, :], ins["down"][e, 0:(FC1 - 1) * P, :]
                             .rearrange("(c p) n -> p c n", p=P)).then_inc(load_down, 16)
                sp.dma_start(wdown[0:FF1 % P, e, FC1 - 1, :], ins["down"][e, (FC1 - 1) * P:FF1, :])\
                  .then_inc(load_down, 16)
            for l in (2, 3):
                if l == 2:
                    sp.wait_ge(mm["cd"], 4)
                else:
                    sp.wait_ge(mm["g2"], 4)
                sp.dma_start(wmem, ins["wmem"][l - 2]).then_inc(load_w23, 16)
                sp.dma_start(wmemT, ins["wmemT"][l - 2]).then_inc(load_w23, 16)
                sp.dma_start(wgate, ins["wgate"][l - 2]).then_inc(load_w23, 16)
                def ready(i, j):
                    of_first = isinstance(i, int) and (i, j) == (0, 0)
                    if l == 2:
                        sp.wait_ge(ev["dn"], 2 if of_first else 4)
                    else:
                        sp.wait_ge(norm_ok, 14 if of_first else 16)
                attention_loads(l, ready)
                if l == 2:
                    attention_loads(3, first=True)
            for t in range(2):
                sp.wait_ge(norm_ok, 16 + 2 * t + 2)
                sp.dma_start(out[:, :, t * HALF:(t + 1) * HALF], x[:, :, t * HALF:(t + 1) * HALF]).then_inc(stored, 16)
            sp.wait_ge(stored, 32)

        @block.tensor
        def _(pe):
            for n in STARTED_BY["tensor"]:
                pe.sem_inc(A[n], LEAD)
            pe.sem_inc(sa_ctt, LEAD)
            pe.sem_inc(sa_s, LEAD)
            pe.sem_inc(sa_c, LEAD)

            def bank(t, m):
                return ps[:, 4 * t + m % 4, 0:HALF]

            def half(ap, t):
                return ap[:, t * HALF:(t + 1) * HALF]

            def norm(n, centre):
                if centre:
                    for t in range(2):
                        if n == 0:
                            pe.wait_ge(load_x[t], 16)
                            pe.wait_ge(consts, 1)
                        else:
                            pe.wait_ge(ev["o0"], 2 * t + 2)
                        for c in range(C):
                            last = pe.matmul(bank(t, 0), ones[:, :], half(x[:, c, :], t), start=c == 0, stop=c == C - 1)
                        last.then_inc(mean_mm, 1)
                for t in range(2):
                    pe.wait_ge(squared, 2 * n + t + 1)
                    for c in range(C):
                        last = pe.matmul(bank(t, 1), ones[:, :], half(xn[:, c, :], t), start=c == 0, stop=c == C - 1)
                    last.then_inc(var_mm, 1)

            def dense(name, tiles, operands, ready):
                for t in range(2):
                    ready(t)
                    for m in range(tiles):
                        if m >= 4:
                            pe.wait_ge(ev[name], t * tiles + m - 3)
                        ops = operands(t, m)
                        rows = ops[0][0].shape[1]
                        for n, (w, v) in enumerate(ops):
                            last = pe.matmul(bank(t, m)[0:rows, :], w, v, start=n == 0, stop=n == len(ops) - 1)
                        last.then_inc(mm[name], 1)

            def gate_chunk(l, t, m):
                for n in range(4):
                    last = pe.matmul(bank(t, m), wgate[:, n, m * P:(m + 1) * P],
                                     half((x if n < 2 else mc)[:, n % 2, :], t), start=n == 0, stop=n == 3)
                last.then_inc(mm[f"g{l}"], 1)

            def attention(l):
                a = ATTS[l]
                groups, tiles, ring = a["groups"], a["tiles"], a["ring"]
                nu = sum(len(g) for g in groups)
                nq, nt, ngr = len(a["q_pieces"]), len(tiles), len(groups)

                def q_piece(i, j, xq):
                    p = j % 2
                    c0, c1 = q_cols(a, xq)
                    if xq < 3:
                        wait(pe, l, "s_neg", i, j - 1, 3 * nu - 3 + xq + 1)
                    else:
                        wait(pe, l, "q_lo", i, j, xq - 2)
                    if l == 1:
                        wait(pe, l, "qbd", i, j, 1)
                    elif xq == 0:
                        wait(pe, l, "q_in", i, j, 16)
                    dst = ps[:, xq % 3, :]
                    if l == 0:
                        h0, h1 = a["q_pieces"][xq]
                        for n in range(h0, h1):
                            h = head_at(n)
                            r = DH0 * (h % 2)
                            last = pe.matmul(dst[:, (n - h0) * S:(n - h0 + 1) * S], wk0[r:r + DH0, h // 2, :],
                                             qb[r:r + DH0, p, (h // 2) * S:(h // 2 + 1) * S], start=True, stop=True)
                    elif l == 1:
                        last = pe.matmul(dst[:, 0:c1 - c0], wck, qbd1[:, c0:c1], start=True, stop=True)
                    else:
                        for c in range(C):
                            last = pe.matmul(dst[:, 0:S], wmem[:, c, :], qb[:, p, c * S:(c + 1) * S],
                                             start=c == 0, stop=c == C - 1)
                    last.then_inc(A["q_mm"], 1)

                def s_piece(i, j, g, u, jj):
                    p = j % 2
                    n = 3 * unit_index(a, g, u) + jj
                    col = unit_col(a, g, u)
                    m = s_cols(a)
                    if jj == 0:
                        wait(pe, l, "q_lo", i, j, q_need(a, col + m))
                    if n == 0:
                        wait(pe, l, "t_lo", i, j, 1)
                    if n < 3:
                        if nq == 1 and n > 0:
                            wait(pe, l, "s_neg", i, j - 1, 3 * nu - 3 + n + 1)
                        else:
                            wait(pe, l, "q_lo", i, j, nq if nq == 1 else nq - 3 + n + 1)
                    else:
                        wait(pe, l, "s_neg", i, j, n - 2)
                    k0, k1 = PIECES[jj]
                    dst = ps[0:m, jj, 0:k1 - k0]
                    for r, (w, v) in enumerate([(qhi, thi), (qhi, tlo), (qlo, thi)]):
                        last = pe.matmul(dst, w[:, p, col:col + m], v[:, p, k0:k1], start=r == 0, stop=r == 2)
                    last.then_inc(A["s_mm"], 1)

                def t_tile(i, j, k, c):
                    tt = k * nt + c
                    if c == 0:
                        wait(pe, l, "p_exp", i, j, unit_index(a, k, len(groups[k]) - 1) + 1)
                    wait(pe, l, "pt_lo", i, j, tt - ring + 1)
                    dst = ps[:, 3 + tt % ring, :]
                    off = 0
                    for ch in tiles[c]:
                        kr, ks = chunk_rows(ch), chunk_start(ch)
                        for u, rows in enumerate(groups[k]):
                            src = wide[0:rows, slot_of(a, k, u, j), ks:ks + kr]
                            last = pe.transpose(dst[0:kr, off:off + rows], src, ident[0:rows, 0:rows])
                            off += rows
                    last.then_inc(A["t_mm"], 1)

                def pv_tile(i, j, k, c):
                    p = j % 2
                    tt = k * nt + c
                    if c == 0:
                        wait(pe, l, "n_lo", i, j, 1)
                        wait(pe, l, "o_ev", i, j, k)
                    wait(pe, l, "pt_lo", i, j, tt + 1)
                    w = sum(groups[k])
                    for n, ch in enumerate(tiles[c]):
                        kr = chunk_rows(ch)
                        for r, (lh, rh) in enumerate([(nhi, pthi), (nhi, ptlo), (nlo, pthi)]):
                            last = pe.matmul(ps[:, 6, 0:w], lh[0:kr, p, ch, :],
                                             rh[0:kr, tt % ring, n * w:(n + 1) * w],
                                             start=ch == 0 and r == 0, stop=ch == CHUNKS - 1 and r == 2)
                    last.then_inc(A["pv_mm"], 1)

                def rb(i, j, k):
                    wait(pe, l, "diag", i, j, unit_index(a, k, len(groups[k]) - 1) + 1)
                    if k == 0:
                        wait(pe, l, "c_ev", i, j, 0)
                    else:
                        wait(pe, l, "rb_sb", i, j, k)
                    off = 0
                    for u, rows in enumerate(groups[k]):
                        last = pe.matmul(ps[:, 7, off:off + rows], ones[0:rows, :], diag[0:rows, u, 0:rows],
                                         start=True, stop=True)
                        off += rows
                    last.then_inc(A["rb_mm"], 1)

                def c_piece(i, j, xq):
                    if xq == 0:
                        wait(pe, l, "o_ev", i, j, ngr)
                        wait(pe, l, "rb_sb", i, j, ngr)
                    else:
                        wait(pe, l, "c_ev", i, j, xq)
                    if l == 0:
                        for h in range(8 * xq, 8 * xq + 8):
                            r, c = DH0 * (h % 2), (h // 2 - 4 * xq) * S
                            n = next(n for n in range(HEADS) if head_at(n) == h)
                            last = pe.matmul(ps[r:r + DH0, 7, c:c + S], wv0[:, h * DH0:(h + 1) * DH0],
                                             outT[:, n * S:(n + 1) * S], start=True, stop=True)
                    elif l == 1:
                        for h in range(HEADS):
                            last = pe.matmul(ps[:, 7, 0:S], wcvh[:, h, :], outT[:, h * S:(h + 1) * S],
                                             start=h == 0, stop=h == HEADS - 1)
                    else:
                        for c in range(C):
                            last = pe.matmul(ps[:, 7, c * S:(c + 1) * S], wmemT[:, c * P:(c + 1) * P],
                                             outT[:, 0:S], start=True, stop=True)
                    last.then_inc(A["c_mm"], 1)

                def item(i, j, it):
                    if it[0] == "q":
                        q_piece(i, j, it[1])
                    else:
                        s_piece(i, j, *it[1:])

                def step(i, j, k, nxt, before=None, after_next=False):
                    last = k == ngr - 1
                    items = plan(a, k, nxt, after_next)
                    for s in range(nt + 2):
                        if s < nt:
                            t_tile(i, j, k, s)
                        for at_slot, it in items:
                            if at_slot == s:
                                item(*(q_batch(a, i, j) if it[0] == "q" else next_batch(i, j) if last else (i, j)), it)
                        if s >= 2:
                            pv_tile(i, j, k, s - 2)
                        if before is not None and s - a["c_slot"] in range(a["c_pieces"]):
                            c_piece(*before, s - a["c_slot"])
                        if s == a["rb_slot"]:
                            rb(i, j, k)
                        if ngr == 1 and not nxt and s in (1, 2):
                            if s == 1:
                                pe.wait_ge(A["c_ev"], at(l, "c_ev", B // 4, 0))
                                pe.wait_ge(A["s_neg"], done(l, "s_neg"))
                            gate_chunk(l, 0, s - 1)

                for xq in range(nq):
                    q_piece(0, 0, xq)
                for u in range(len(groups[0])):
                    for jj in range(3):
                        s_piece(0, 0, 0, u, jj)
                if ngr == 1:
                    q_piece(0, 1, 0)
                step(0, 0, 0, True, after_next=True)
                if ngr > 1:
                    with pe.Fori(0, B // 2 - 1) as i:
                        for j in range(2):
                            for k in range(1, ngr):
                                step(i, j, k, True)
                            step(i, j + 1, 0, True, before=(i, j))
                    for j in range(2):
                        for k in range(1, ngr):
                            step(B // 2 - 1, j, k, j == 0)
                        if j == 0:
                            step(B // 2 - 1, 1, 0, False, before=(B // 2 - 1, 0))
                else:
                    with pe.Fori(0, B // 2 - 2) as i:
                        for j in range(2):
                            step(i, j + 1, 0, True, before=(i, j), after_next=True)
                    for b in (B - 3, B - 2, B - 1):
                        step(b // 2, b % 2, 0, b < B - 1, before=((b - 1) // 2, (b - 1) % 2), after_next=b < B - 2)
                for xq in range(a["c_pieces"]):
                    c_piece(B // 2 - 1, 1, xq)

            norm(0, True)

            def ready(t):
                pe.wait_ge(norm_ok, 2 * t + 2)
                if t == 0:
                    pe.wait_ge(load_w0, 48)
            dense("q0", 8, lambda t, m: [(wq[:, c, m * P:(m + 1) * P], half(xn[:, c, :], t)) for c in range(C)], ready)
            pe.wait_ge(ev["q0"], 16)
            pe.wait_ge(pos_ok, 5)
            for n in range(2):
                last = pe.matmul(ps[:, 7, n * S:(n + 1) * S], postab[:, n * P:(n + 1) * P], onehot, start=True, stop=True)
            last.then_inc(cossin_mm, 1)
            attention(0)

            def ready(t):
                pe.wait_ge(A["c_ev"], done(0, "c_ev"))
                pe.wait_ge(load_wo, 16)
            dense("o0", 2, lambda t, m: [(wo[:, c, m * P:(m + 1) * P], half(big8[:, c, :], t)) for c in range(8)], ready)
            norm(1, True)

            def ready(t):
                pe.wait_ge(norm_ok, 4 + 2 * t + 2)
                pe.wait_ge(load_w12, 32)
            dense("f1", 8, lambda t, m: [(w1[:, c, m * P:(m + 1) * P], half(xn[:, c, :], t)) for c in range(C)], ready)

            def ready(t):
                pe.wait_ge(ev["f1"], 8 * t + 8)
            dense("f2", 2, lambda t, m: [(w2[:, c, m * P:(m + 1) * P], half(big8[:, c, :], t)) for c in range(8)], ready)

            norm(2, False)

            def experts(w, t, m, n=P):
                return [(w[:, e, c, m * P:m * P + n], half(xe[:, e, c, :], t)) for e in range(2) for c in range(C)]

            def ready(t):
                pe.wait_ge(xe_l, t + 1)
                pe.wait_ge(load_qkv, 48)
            dense("qk", 4, lambda t, m: experts(wqkv, t, m), ready)

            def ready(t):
                pe.wait_ge(ev["qk"], 4 * t + 4)
                pe.wait_ge(load_rot, 32)
            dense("rt", 4, lambda t, m: [(rot, half(qk[:, m, :], t))], ready)

            for b in range(B):
                pe.wait_ge(rt_s, b + 1)
                for n in range(4):
                    e, c = n // 2, n % 2
                    last = pe.matmul(ps[0:S, b, 0:D], xe[:, e, c, b * S:(b + 1) * S], wqkv[:, e, c, 2 * D:3 * D],
                                     start=n == 0, stop=n == 3)
                last.then_inc(mm["vt"], 1)

            def sa_scores(i, j):
                pe.wait_ge(sa_kbd, i * 2 + (LEAD + j + 1))
                for n in range(4):
                    pe.wait_ge(sa_m, i * 8 + (LEAD + 4 * (j - 1) + n + 1))
                    last = pe.matmul(ps[0:S, n, 0:4 * S], qsb[:, j % 2, n // 2, :], kbd[:, j % 2, 4 * n:4 * n + 4, :],
                                     start=True, stop=True)
                    last.then_inc(sa_s, 1)

            def sa_transposes(i, j):
                pe.wait_ge(sa_e, i * 2 + (LEAD + j + 1))
                for n in range(4):
                    pe.wait_ge(sa_pt, i * 8 + (LEAD + 4 * j + n - 1))
                    for h in range(4):
                        last = pe.transpose(ps[0:S, 4 + n % 2, h * S:(h + 1) * S], sself[:, j % 2, 4 * n + h, :],
                                            ident[0:S, 0:S])
                    last.then_inc(sa_t, 1)

            def sa_values(i, j):
                pe.wait_ge(sa_pt, i * 8 + (LEAD + 4 * j + 4))
                pe.wait_ge(sa_ct, i * 2 + (LEAD + j))
                for h in range(HEADS):
                    last = pe.matmul(ps[0:S, 6, h * HD1:(h + 1) * HD1], ptself[:, h, :],
                                     vtok[:, bass.ds(i * 2 + j, 1), h * HD1:(h + 1) * HD1].rearrange("p o d -> p (o d)"),
                                     start=True, stop=True)
                last.then_inc(sa_c, 1)

            def sa_turn(i, j):
                pe.wait_ge(sa_ct, i * 2 + (LEAD + j + 1))
                pe.wait_ge(sa_out, i * 2 + (LEAD + j))
                for c in range(C):
                    last = pe.transpose(ps[:, 7, c * S:(c + 1) * S], ctok[:, c * P:(c + 1) * P], ident[0:S, 0:S])
                last.then_inc(sa_ctt, 1)

            pe.wait_ge(ev["vt"], 8)
            sa_scores(0, 0)
            sa_scores(0, 1)
            sa_transposes(0, 0)
            sa_values(0, 0)
            with pe.Fori(0, B // 2 - 1) as i:
                for j in (1, 2):
                    sa_scores(i, j + 1)
                    sa_transposes(i, j)
                    sa_turn(i, j - 1)
                    sa_values(i, j)
            sa_transposes(B // 2 - 1, 1)
            sa_turn(B // 2 - 1, 0)
            sa_values(B // 2 - 1, 1)
            sa_turn(B // 2 - 1, 1)

            def ready(t):
                pe.wait_ge(xe_l, 2 + t + 1)
                pe.wait_ge(load_d1, 32)
            dense("d1", 2, lambda t, m: experts(wdn1, t, m), ready)

            norm(3, False)

            def ready(t):
                pe.wait_ge(norm_ok, 8 + 2 * t + 2)
            dense("cq", 1, lambda t, m: [(wcq[:, c, :], half(xn[:, c, :], t)) for c in range(C)], ready)
            pe.wait_ge(ev["cq"], 2)
            pe.wait_ge(wcv_ok, 1)
            pe.wait_ge(load_w1att, 32)
            attention(1)

            def ready(t):
                pe.wait_ge(A["c_ev"], done(1, "c_ev"))
                pe.wait_ge(load_cd, 16)
            dense("cd", 2, lambda t, m: [(wcd[:, m * P:(m + 1) * P], half(cT, t))], ready)

            norm(4, False)
            for t in range(2):
                if t == 0:
                    pe.wait_ge(load_gu, 64)
                pe.wait_ge(xe_l, 4 + t + 1)
                for m in range(FC1):
                    rows = min(P, FF1 - m * P)
                    if m >= 2:
                        pe.wait_ge(gu_h, t * FC1 + m - 1)
                    for g in range(2):
                        for n in range(4):
                            e, c = n // 2, n % 2
                            last = pe.matmul(ps[0:rows, 4 * t + (2 * m + g) % 4, 0:HALF],
                                             wgu[:, g, e, c, m * P:m * P + rows], half(xe[:, e, c, :], t),
                                             start=n == 0, stop=n == 3)
                        last.then_inc(mm["gu"], 1)
                if t == 0:
                    pe.wait_ge(load_down, 64)
                pe.wait_ge(ev["gu"], t * FC1 + FC1)
                for m in range(C):
                    for n in range(2 * FC1):
                        e, c = n // FC1, n % FC1
                        rows = min(P, FF1 - c * P)
                        last = pe.matmul(bank(t, m), wdown[0:rows, e, c, m * P:(m + 1) * P], hexp[0:rows, e, c, :],
                                         start=n == 0, stop=n == 2 * FC1 - 1)
                    last.then_inc(mm["dn"], 1)

            for l in (2, 3):
                pe.wait_ge(load_w23, 48 * (l - 1))
                if l == 2:
                    pe.wait_ge(ev["dn"], 4)
                else:
                    pe.wait_ge(norm_ok, 14)
                attention(l)
                pe.wait_ge(A["c_ev"], done(l, "c_ev"))
                for m in range(C):
                    gate_chunk(l, 1, m)
                norm(l + 3, False)

        @block.scalar
        def _(act):
            for n in STARTED_BY["scalar"]:
                act.sem_inc(A[n], LEAD)
            act.sem_inc(sa_e, LEAD)
            act.sem_inc(sa_pt, LEAD)
            act.sem_inc(sa_out, LEAD)

            def bank(t, m):
                return ps[:, 4 * t + m % 4, 0:HALF]

            def tok(ap, t):
                return ap[:, :, t * HALF:(t + 1) * HALF]

            def norm(n, centre, eps):
                for t in range(2):
                    if centre:
                        act.wait_ge(centred, 2 * n + t + 1)
                        src = xc
                    else:
                        x_ready(n, t)
                        src = x
                    act.activation(tok(xn, t), tok(src, t), ACT.Square).then_inc(squared, 1)
                for t in range(2):
                    act.wait_ge(var_mm, 2 * n + t + 1)
                    act.activation(rstd[:, t * HALF:(t + 1) * HALF], bank(t, 1), ACT.Sqrt, bias=eps[:, 0:1],
                                   scale=1.0 / D)\
                       .then_inc(std_ok, 1)

            def x_ready(n, t):
                if n == 2:
                    act.wait_ge(ev["f2"], 2 * t + 2)
                elif n == 3:
                    act.wait_ge(ev["d1"], 2 * t + 2)
                elif n == 4:
                    act.wait_ge(ev["cd"], 2 * t + 2)
                else:
                    act.wait_ge(fuse, 4 * (n - 5) + 2 * t + 2)

            def attention(l):
                a = ATTS[l]
                groups, tiles, ring = a["groups"], a["tiles"], a["ring"]
                nt, ngr = len(tiles), len(groups)
                scale = 1.0 if l < 2 else D ** -0.5

                def q_hi(i, j, xq):
                    wait(act, l, "q_mm", i, j, xq + 1)
                    c0, c1 = q_cols(a, xq)
                    act.activation(qhi[:, j % 2, c0:c1], ps[:, xq % 3, 0:c1 - c0], ACT.Copy, scale=scale)\
                       .then_inc(A["q_hi"], 1)

                def p_exp(i, j, g, u):
                    s = slot_of(a, g, u, j)
                    m = s_cols(a)
                    wait(act, l, "nmax", i, j, unit_index(a, g, u) + 1)
                    act.activation(wide[0:m, s, :], wide[0:m, s, :], ACT.Exp, bias=negmax[0:m, s:s + 1], scale=-1.0,
                                   accum_out=den[0:m, s:s + 1]).then_inc(A["p_exp"], 1)

                def pt_hi(i, j, k, c):
                    tt = k * nt + c
                    kr = chunk_rows(tiles[c][0])
                    w = sum(groups[k]) * len(tiles[c])
                    wait(act, l, "pv_mm", i, j, tt - ring + 1)
                    wait(act, l, "t_mm", i, j, tt + 1)
                    act.activation(pthi[0:kr, tt % ring, 0:w], ps[0:kr, 3 + tt % ring, 0:w], ACT.Copy)\
                       .then_inc(A["pt_hi"], 1)

                def rb_out(i, j, k):
                    g_par = (k if ngr > 1 else j) % 2
                    w = sum(groups[k])
                    wait(act, l, "o_ev", i, j, k - 1)
                    wait(act, l, "rb_mm", i, j, k + 1)
                    act.activation(rbc[:, g_par, 0:w], ps[:, 7, 0:w], ACT.Copy).then_inc(A["rb_sb"], 1)

                def c_out(i, j, xq):
                    b = i * 2 + j
                    wait(act, l, "c_mm", i, j, xq + 1)
                    if l == 0:
                        dst, w = big8[:, 4 * xq:4 * xq + 4, bass.ds(b * S, S)], 4
                    elif l == 1:
                        dst, w = cT[:, bass.ds(b * S, S)].unsqueeze(1), 1
                    else:
                        dst, w = mc[:, :, bass.ds(b * S, S)], 2
                    act.activation(dst, ps[:, 7, 0:w * S].rearrange("p (c t) -> p c t", c=w), ACT.Copy)\
                       .then_inc(A["c_ev"], 1)

                def step(i, j, k, nxt, before=None, after_next=False):
                    last = k == ngr - 1
                    items = plan(a, k, nxt, after_next)
                    bi = next_batch(i, j) if last else (i, j)
                    for s in range(nt + 2):
                        if s < nt:
                            pt_hi(i, j, k, s)
                        for at_slot, it in items:
                            if at_slot == s and it[0] == "q":
                                q_hi(*q_batch(a, i, j), it[1])
                        for at_slot, it in items:
                            if at_slot == s - a["exp_lag"] and it[0] == "s" and it[3] == 2:
                                p_exp(*bi, it[1], it[2])
                        if before is not None and s - a["c_slot"] in range(a["c_pieces"]):
                            c_out(*before, s - a["c_slot"])
                        if s == a["rb_slot"] + 1:
                            rb_out(i, j, k)

                for xq in range(len(a["q_pieces"])):
                    q_hi(0, 0, xq)
                for u in range(len(groups[0])):
                    p_exp(0, 0, 0, u)
                if ngr == 1:
                    q_hi(0, 1, 0)
                step(0, 0, 0, True, after_next=True)
                if ngr > 1:
                    with act.Fori(0, B // 2 - 1) as i:
                        for j in range(2):
                            for k in range(1, ngr):
                                step(i, j, k, True)
                            step(i, j + 1, 0, True, before=(i, j))
                    for j in range(2):
                        for k in range(1, ngr):
                            step(B // 2 - 1, j, k, j == 0)
                        if j == 0:
                            step(B // 2 - 1, 1, 0, False, before=(B // 2 - 1, 0))
                else:
                    with act.Fori(0, B // 2 - 2) as i:
                        for j in range(2):
                            step(i, j + 1, 0, True, before=(i, j), after_next=True)
                    for b in (B - 3, B - 2, B - 1):
                        step(b // 2, b % 2, 0, b < B - 1, before=((b - 1) // 2, (b - 1) % 2), after_next=b < B - 2)
                for xq in range(a["c_pieces"]):
                    c_out(B // 2 - 1, 1, xq)

            act.wait_ge(consts, 1)
            norm(0, True, eps5)
            act.wait_ge(consts, 3)
            for t in range(2):
                for m in range(8):
                    act.wait_ge(mm["q0"], 8 * t + m + 1)
                    act.activation(big8[:, m, t * HALF:(t + 1) * HALF], bank(t, m), ACT.Copy, scale=DH0 ** -0.5)\
                       .then_inc(ev["q0"], 1)
            act.wait_ge(load_consts, 16 * 8)
            act.activation(tgate[:, :], tgate[:, :], ACT.Tanh).then_inc(gates_ok, 1)
            act.wait_ge(cossin_mm, 1)
            act.activation(cossin[:, :, :], ps[:, 7, 0:2 * S].rearrange("p (n s) -> p n s", n=2), ACT.Copy)\
               .then_inc(cossin_ok, 1)
            attention(0)
            norm(1, True, eps5)
            for t in range(2):
                for m in range(8):
                    act.wait_ge(mm["f1"], 8 * t + m + 1)
                    act.activation(big8[:, m, t * HALF:(t + 1) * HALF], bank(t, m), ACT.Gelu).then_inc(ev["f1"], 1)
            norm(2, False, eps6)
            for t in range(2):
                for m in range(4):
                    act.wait_ge(mm["qk"], 4 * t + m + 1)
                    act.activation(qk[:, m, t * HALF:(t + 1) * HALF], bank(t, m), ACT.Copy,
                                   scale=HD1 ** -0.5 if m < C else 1.0).then_inc(ev["qk"], 1)
            for b in range(B):
                act.wait_ge(mm["vt"], b + 1)
                act.activation(vtok[:, b, :], ps[0:S, b, 0:D], ACT.Copy).then_inc(ev["vt"], 1)

            def sa_exp(i, j):
                act.wait_ge(sa_sub, i * 2 + (LEAD + j + 1))
                act.activation(sself[:, j % 2, :, :], sself[:, j % 2, :, :], ACT.Exp).then_inc(sa_e, 1)

            def sa_copies(i, j):
                for n in range(4):
                    act.wait_ge(sa_t, i * 8 + (4 * j + n + 1))
                    if n == 0:
                        act.wait_ge(sa_c, i * 2 + (LEAD + j))
                    act.activation(ptself[:, 4 * n:4 * n + 4, :], ps[0:S, 4 + n % 2, 0:4 * S]
                                   .rearrange("p (h q) -> p h q", h=4), ACT.Copy).then_inc(sa_pt, 1)

            def sa_result(i, j):
                act.wait_ge(sa_ctt, i * 2 + (LEAD + j + 1))
                act.activation(ctxT[:, :, bass.ds((i * 2 + j) * S, S)],
                               ps[:, 7, 0:2 * S].rearrange("p (c t) -> p c t", c=C), ACT.Copy).then_inc(sa_out, 1)

            sa_exp(0, 0)
            sa_copies(0, 0)
            sa_exp(0, 1)
            with act.Fori(0, B // 2 - 1) as i:
                for j in (1, 2):
                    sa_copies(i, j)
                    sa_result(i, j - 1)
                    sa_exp(i, j + 1)
            sa_copies(B // 2 - 1, 1)
            sa_result(B // 2 - 1, 0)
            sa_result(B // 2 - 1, 1)

            norm(3, False, eps6)
            for t in range(2):
                act.wait_ge(mm["cq"], t + 1)
                act.activation(cq[:, t * HALF:(t + 1) * HALF], bank(t, 0), ACT.Copy, scale=float(np.float32(CHD1 ** -0.5)))\
                   .then_inc(ev["cq"], 1)
            attention(1)
            norm(4, False, eps6)
            for t in range(2):
                for m in range(FC1):
                    rows = min(P, FF1 - m * P)
                    act.wait_ge(mm["gu"], 2 * (t * FC1 + m) + 1)
                    if t * FC1 + m >= 2:
                        act.wait_ge(gu_h, t * FC1 + m - 1)
                    act.activation(gsilu[0:rows, m % 2, :], ps[0:rows, 4 * t + (2 * m) % 4, 0:HALF], ACT.Silu)\
                       .then_inc(gu_silu, 1)
            for l in (2, 3):
                attention(l)
                name = f"g{l}"
                for t in range(2):
                    for m in range(C):
                        act.wait_ge(mm[name], 2 * t + m + 1)
                        act.activation(gate[:, m, t * HALF:(t + 1) * HALF], bank(t, m), ACT.Sigmoid,
                                       bias=vcol(f"b{l}", m)).then_inc(ev[name], 1)
                norm(l + 3, False, eps6)

        @block.vector
        def _(dve):
            for n in STARTED_BY["vector"]:
                dve.sem_inc(A[n], LEAD)
            for s_ in (sa_m, sa_x, sa_sub, sa_den, sa_ct):
                dve.sem_inc(s_, LEAD)
            steps = [0]

            def chain(ins):
                steps[0] += 1
                ins.then_inc(norm_step, 1)
                dve.wait_ge(norm_step, steps[0])

            def bank(t, m):
                return ps[:, 4 * t + m % 4, 0:HALF]

            def tok(ap, t):
                return ap[:, :, t * HALF:(t + 1) * HALF]

            def both(ap):
                return ap.unsqueeze(1).to_broadcast([P, C, HALF])

            def half(ap, c, t):
                return ap[:, c, t * HALF:(t + 1) * HALF]

            def norm(n, centre, g, bvec, dst=xn, experts=False):
                if centre:
                    for t in range(2):
                        dve.wait_ge(mean_mm, 2 * n + t + 1)
                        dve.scalar_tensor_tensor(tok(xc, t), both(bank(t, 0)), -1.0 / D, tok(x, t), ALU.mult, ALU.add)\
                           .then_inc(centred, 1)
                src = xc if centre else x
                if n == 0:
                    dve.wait_ge(load_consts, 16 * 8)
                for t in range(2):
                    r = rstd[:, t * HALF:(t + 1) * HALF]
                    dve.wait_ge(std_ok, 2 * n + t + 1)
                    chain(dve.reciprocal(r, r))
                    if experts:
                        rv, rl = rmask[:, 0, :], rmask[:, 1, :]
                        chain(dve.tensor_tensor(rv, r, vm[:, t * HALF:(t + 1) * HALF], ALU.mult))
                        chain(dve.tensor_tensor(rl, r, rv, ALU.subtract))
                        for e, re in enumerate((rv, rl)):
                            for c in range(C):
                                last = dve.scalar_tensor_tensor(xe[:, e, c, t * HALF:(t + 1) * HALF], half(src, c, t),
                                                                vcol(g, c), re, ALU.mult, ALU.mult)
                            last.then_inc((xe_v, xe_l)[e], 1)
                        continue
                    for c in range(C):
                        d = half(dst, c, t)
                        last = dve.scalar_tensor_tensor(d, half(src, c, t), vcol(g, c), r, ALU.mult, ALU.mult)
                        if bvec is not None:
                            chain(last)
                            last = dve.tensor_scalar(d, d, vcol(bvec, c), None, ALU.add)
                        last.then_inc(norm_ok, 1)

            def residual(name, gcol=None):
                for t in range(2):
                    for m in range(C):
                        dve.wait_ge(mm[name], 2 * t + m + 1)
                        xs = x[:, m, t * HALF:(t + 1) * HALF]
                        if gcol is None:
                            dve.tensor_tensor(xs, bank(t, m), xs, ALU.add).then_inc(ev[name], 1)
                        else:
                            dve.scalar_tensor_tensor(xs, bank(t, m), tgate[:, gcol:gcol + 1], xs, ALU.mult, ALU.add)\
                               .then_inc(ev[name], 1)

            def attention(l, first=False):
                a = ATTS[l]
                groups, tiles, ring = a["groups"], a["tiles"], a["ring"]
                nu = sum(len(g) for g in groups)
                nt, ngr = len(tiles), len(groups)
                scale = 1.0 if l < 2 else D ** -0.5

                def t_hi(i, j):
                    wait(dve, l, "s_mm", i, j - 1, 0)
                    wait(dve, l, "raw_t", i, j, 16)
                    dve.tensor_copy(thi[:, j % 2, :], raw[:, 0:SK]).then_inc(A["t_hi"], 1)

                def n_hi(i, j):
                    wait(dve, l, "pv_mm", i, j - 1, 0)
                    wait(dve, l, "raw_n", i, j, 32)
                    dve.tensor_copy(nhi[:, j % 2, :, :], raw_ctx(l).rearrange("p (c d) -> p c d", c=CHUNKS)).then_inc(A["n_hi"], 1)

                def t_lo(i, j):
                    wait(dve, l, "t_hi", i, j, 1)
                    dve.tensor_tensor(tlo[:, j % 2, :], raw[:, 0:SK], thi[:, j % 2, :].bitcast(FP32), ALU.subtract)\
                       .then_inc(A["t_lo"], 1)

                def make_bias(i, j):
                    if l == 0:
                        wait(dve, l, "raw_m", i, j, 16)
                        dve.tensor_scalar(bias[:, j % 2, :], mask_u8, BIG, -BIG, ALU.mult, ALU.add)\
                           .then_inc(A["bias"], 1)

                def q_lo(i, j, xq):
                    c0, c1 = q_cols(a, xq)
                    wait(dve, l, "q_hi", i, j, xq + 1)
                    dve.scalar_tensor_tensor(qlo[:, j % 2, c0:c1], ps[:, xq % 3, 0:c1 - c0], scale,
                                             qhi[:, j % 2, c0:c1].bitcast(FP32), ALU.mult, ALU.subtract)\
                       .then_inc(A["q_lo"], 1)

                def s_neg(i, j, g, u, jj):
                    n = 3 * unit_index(a, g, u) + jj
                    s = slot_of(a, g, u, j)
                    m = s_cols(a)
                    k0, k1 = PIECES[jj]
                    if n == 0 and l > 0 and isinstance(i, int) and i == 0:
                        dve.wait_ge(bias_zero, l)
                    if jj == 0 and u == 0:
                        if n == 0 and l == 0:
                            wait(dve, l, "bias", i, j, 1)
                        wait(dve, l, "t_mm", i, j, (g - 1) * nt)
                    wait(dve, l, "s_mm", i, j, n + 1)
                    carry_wait(dve, "scores")
                    dve.tensor_tensor_reduce(out=wide[0:m, s, k0:k1], in0=ps[0:m, jj, 0:k1 - k0],
                                             in1=bias[0:m, j % 2 if l == 0 else 0, k0:k1], scale=-1.0, scalar=FMAX,
                                             op0=ALU.add, op1=ALU.min, accum_out=negmin3[0:m, s, jj:jj + 1])\
                       .then_inc(A["s_neg"], 1)

                def nmax(i, j, g, u):
                    s = slot_of(a, g, u, j)
                    m = s_cols(a)
                    wait(dve, l, "s_neg", i, j, 3 * unit_index(a, g, u) + 3)
                    dve.tensor_reduce(negmax[0:m, s:s + 1], negmin3[0:m, s, :], AX.X, ALU.min).then_inc(A["nmax"], 1)

                def rden(i, j, g, u):
                    s = slot_of(a, g, u, j)
                    m = s_cols(a)
                    wait(dve, l, "p_exp", i, j, unit_index(a, g, u) + 1)
                    dve.reciprocal(rdn[0:m, s:s + 1], den[0:m, s:s + 1]).then_inc(A["rden"], 1)

                def pt_lo(i, j, k, c):
                    tt = k * nt + c
                    kr = chunk_rows(tiles[c][0])
                    w = sum(groups[k]) * len(tiles[c])
                    wait(dve, l, "pt_hi", i, j, tt + 1)
                    dve.tensor_tensor(ptlo[0:kr, tt % ring, 0:w], ps[0:kr, 3 + tt % ring, 0:w],
                                      pthi[0:kr, tt % ring, 0:w].bitcast(FP32), ALU.subtract).then_inc(A["pt_lo"], 1)

                def o_ev(i, j, k):
                    g_par = (k if ngr > 1 else j) % 2
                    w = sum(groups[k])
                    c0 = unit_col(a, k, 0)
                    if k == 0:
                        wait(dve, l, "c_mm", i, j, 0)
                    wait(dve, l, "rb_sb", i, j, k + 1)
                    wait(dve, l, "pv_mm", i, j, (k + 1) * nt)
                    dve.tensor_tensor(outT[:, c0:c0 + w], ps[:, 6, 0:w], rbc[:, g_par, 0:w], ALU.mult)\
                       .then_inc(A["o_ev"], 1)

                def step(i, j, k, nxt, after_next=False):
                    last = k == ngr - 1
                    items = plan(a, k, nxt, after_next)
                    bi = next_batch(i, j) if last else (i, j)
                    nb = next_batch(i, j)
                    for s in range(nt + 2):
                        if s < nt and ngr == 1:
                            pt_lo(i, j, k, s)
                        for at_slot, it in items:
                            if at_slot == s:
                                if it[0] == "q":
                                    q_lo(*q_batch(a, i, j), it[1])
                                else:
                                    s_neg(*bi, *it[1:])
                                    if it[3] == 2:
                                        nmax(*bi, it[1], it[2])
                        if s < nt and ngr > 1:
                            pt_lo(i, j, k, s)
                        for at_slot, it in items:
                            if at_slot == s - a["rden_lag"] and it[0] == "s" and it[3] == 2:
                                rden(*bi, it[1], it[2])
                        if nxt and ngr > 1:
                            if k == 0 and s == 3:
                                t_hi(*nb)
                            if k == 1 and s == 3:
                                n_hi(*nb)
                            if k == 1 and s == 6:
                                make_bias(*nb)
                        if ngr == 1 and s == a["n_slot"] and nxt:
                            n_hi(*nb)
                        if ngr == 1 and s == a["t_slot"] and after_next:
                            t_hi(i, j + 2)
                            t_lo(i, j + 2)
                    for at_slot, it in items:
                        if at_slot > nt + 1 - a["rden_lag"] and it[0] == "s" and it[3] == 2:
                            rden(*bi, it[1], it[2])
                    o_ev(i, j, k)

                if first or l == 0:
                    t_hi(0, 0)
                    if ngr == 1:
                        t_lo(0, 0)
                if first:
                    return
                make_bias(0, 0)
                for xq in range(len(a["q_pieces"])):
                    q_lo(0, 0, xq)
                for u in range(len(groups[0])):
                    for jj in range(3):
                        s_neg(0, 0, 0, u, jj)
                    nmax(0, 0, 0, u)
                n_hi(0, 0)
                if ngr == 1:
                    q_lo(0, 1, 0)
                    t_hi(0, 1)
                    t_lo(0, 1)
                for u in range(len(groups[0])):
                    rden(0, 0, 0, u)
                with dve.Fori(0, B // 2 - 1) as i:
                    for j in range(2):
                        for k in range(ngr):
                            step(i, j, k, True, True)
                for j in range(2):
                    for k in range(ngr):
                        step(B // 2 - 1, j, k, j == 0)

            norm(0, True, "ln_q_g", "ln_q_b")
            attention(0)
            dve.wait_ge(gates_ok, 1)
            residual("o0", 0)
            norm(1, True, "ln_ff_g", "ln_ff_b")
            residual("f2", 1)
            norm(2, False, "ln_in", None, experts=True)
            dve.wait_ge(cossin_ok, 1)
            for t in range(2):
                for m in range(4):
                    n = 4 * t + m
                    q4 = qk[:, m, t * HALF:(t + 1) * HALF].rearrange("p (b s) -> p b s", s=S)
                    r4 = rotated[:, n % 2, :].rearrange("p (b s) -> p b s", s=S)
                    cos4 = cossin[:, 0, :].unsqueeze(1).to_broadcast([P, 4, S])
                    sin4 = cossin[:, 1, :].unsqueeze(1).to_broadcast([P, 4, S])
                    dve.wait_ge(mm["rt"], n + 1)
                    if n >= 2:
                        dve.wait_ge(rope, 2 * (n - 1))
                    dve.tensor_tensor(r4, bank(t, m).rearrange("p (b s) -> p b s", s=S), sin4, ALU.mult).then_inc(rt_s, 1)
                    dve.tensor_tensor(q4, q4, cos4, ALU.mult).then_inc(rope, 1)
                    dve.wait_ge(rope, 2 * n + 1)
                    dve.wait_ge(rt_s, n + 1)
                    dve.tensor_tensor(q4, q4, r4, ALU.add).then_inc(rope, 1)

            def sa_soft(i, j):
                s_ = sself[:, j % 2, :, :]
                smax = rstat[:, j % 2, 0:HEADS]
                for n in range(4):
                    dve.wait_ge(sa_s, i * 8 + (LEAD + 4 * j + n + 1))
                    if n == 0:
                        dve.wait_ge(sa_pt, i * 8 + (LEAD + 4 * j - 4))
                    dve.tensor_tensor(s_[:, 4 * n:4 * n + 4, :],
                                      ps[0:S, n, 0:4 * S].rearrange("p (h q) -> p h q", h=4),
                                      causal.unsqueeze(1).to_broadcast([S, 4, S]), ALU.add).then_inc(sa_m, 1)
                dve.wait_ge(sa_m, i * 8 + (LEAD + 4 * j + 4))
                dve.tensor_reduce(smax, s_, AX.X, ALU.max).then_inc(sa_x, 1)
                dve.wait_ge(sa_x, i * 2 + (LEAD + j + 1))
                dve.tensor_tensor(s_, s_, smax.unsqueeze(2).to_broadcast([S, HEADS, S]), ALU.subtract).then_inc(sa_sub, 1)

            def sa_norm(i, j):
                ssum, srec = rstat[:, j % 2, HEADS:2 * HEADS], rstat[:, j % 2, 2 * HEADS:3 * HEADS]
                dve.wait_ge(sa_e, i * 2 + (LEAD + j + 1))
                dve.tensor_reduce(ssum, sself[:, j % 2, :, :], AX.X, ALU.add).then_inc(sa_den, 1)
                dve.wait_ge(sa_den, i * 4 + (LEAD + 2 * j + 1))
                dve.reciprocal(srec, ssum).then_inc(sa_den, 1)
                dve.wait_ge(sa_den, i * 4 + (LEAD + 2 * j + 2))
                dve.wait_ge(sa_ctt, i * 2 + (LEAD + j))
                dve.wait_ge(sa_c, i * 2 + (LEAD + j + 1))
                dve.tensor_tensor(ctok.rearrange("p (h d) -> p h d", h=HEADS),
                                  ps[0:S, 6, 0:D].rearrange("p (h d) -> p h d", h=HEADS),
                                  srec.unsqueeze(2).to_broadcast([S, HEADS, HD1]), ALU.mult).then_inc(sa_ct, 1)

            sa_soft(0, 0)
            with dve.Fori(0, B // 2 - 1) as i:
                for j in range(2):
                    sa_soft(i, j + 1)
                    sa_norm(i, j)
            sa_soft(B // 2 - 1, 1)
            sa_norm(B // 2 - 1, 0)
            sa_norm(B // 2 - 1, 1)

            for t in range(2):
                dve.wait_ge(sa_out, LEAD + 4 * t + 4)
                dve.tensor_tensor(tok(xe[:, 0, :, :], t), tok(ctxT, t), both(vm[:, t * HALF:(t + 1) * HALF]), ALU.mult)\
                   .then_inc(xe_v, 1)
            attention(1, first=True)
            residual("d1")
            norm(3, False, "ln_cross", None)
            attention(1)
            residual("cd")
            norm(4, False, "ln_post", None, experts=True)
            attention(2, first=True)
            for t in range(2):
                for m in range(FC1):
                    n = t * FC1 + m
                    rows = min(P, FF1 - m * P)
                    dve.wait_ge(mm["gu"], 2 * n + 2)
                    dve.wait_ge(gu_silu, n + 1)
                    if n >= 1:
                        dve.wait_ge(ev["gu"], n)
                    dve.tensor_tensor(hgu[0:rows, :], ps[0:rows, 4 * t + (2 * m + 1) % 4, 0:HALF],
                                      gsilu[0:rows, m % 2, :], ALU.mult).then_inc(gu_h, 1)
                for m in range(C):
                    dve.wait_ge(mm["dn"], 2 * t + m + 1)
                    xs = x[:, m, t * HALF:(t + 1) * HALF]
                    dve.tensor_tensor(xs, bank(t, m), xs, ALU.add).then_inc(ev["dn"], 1)
            for l in (2, 3):
                attention(l)
                if l == 2:
                    attention(3, first=True)
                name = f"g{l}"
                for t in range(2):
                    for m in range(C):
                        dve.wait_ge(ev[name], 2 * t + m + 1)
                        gs = gate[:, m, t * HALF:(t + 1) * HALF]
                        xs = x[:, m, t * HALF:(t + 1) * HALF]
                        chain(dve.tensor_tensor(gs, gs, mc[:, m, t * HALF:(t + 1) * HALF], ALU.mult))
                        if m == 0:
                            dve.wait_ge(mm[name], 2 * t + 2)
                        dve.tensor_tensor(xs, xs, gs, ALU.add).then_inc(fuse, 1)
                norm(l + 3, False, f"n{l}", None, dst=x)

        @block.gpsimd
        def _(pool):
            for n in STARTED_BY["gpsimd"]:
                pool.sem_inc(A[n], LEAD)
            pool.sem_inc(sa_kbd, LEAD)
            pool.memset(eps5[:, :], 1e-5)
            pool.memset(eps6[:, :], 1e-6)
            pool.memset(ones[:, :], 1.0).then_inc(consts, 1)
            pool.memset(raw, 0.0)
            for q in (qhi, qlo):
                pool.memset(q[:, :, HEADS * S:].bitcast(FP32), 0.0)
            pool.memset(vm[:, :], 0.0).then_inc(consts, 1)

            pool.wait_ge(load_consts, 16 * 8)
            pool.tensor_copy(pos_f, pos_i).then_inc(pos_ok, 1)
            pool.wait_ge(pos_ok, 1)
            pool.tensor_scalar(pos_neg, pos_f, 0.0, float(S), ALU.is_lt, ALU.mult).then_inc(pos_ok, 1)
            pool.wait_ge(pos_ok, 2)
            pool.tensor_tensor(pos_f, pos_f, pos_neg, ALU.add).then_inc(pos_ok, 1)
            pool.wait_ge(pos_ok, 3)
            pool.tensor_scalar(pos_f, pos_f, 0.0, float(S - 1), ALU.max, ALU.min).then_inc(pos_ok, 1)
            pool.wait_ge(pos_ok, 4)
            pool.tensor_scalar(onehot, pos_f[0:S, :], vec[0:S, 22:23], None, ALU.is_equal).then_inc(pos_ok, 1)

            pool.tensor_scalar(tt_one.rearrange("p b s -> p (b s)"), tt_i, 1.0, None, ALU.is_equal).then_inc(vm_step, 1)
            pool.wait_ge(vm_step, 1)
            pool.tensor_tensor(vm[:, :].rearrange("p (b s) -> p b s", b=B)[:, :, 0:S - 1],
                               tt_one[:, :, 0:S - 1], tt_one[:, :, 1:S], ALU.mult).then_inc(consts, 1)

            def tok(ap, t):
                return ap[:, :, t * HALF:(t + 1) * HALF]

            def attention(l, first=False):
                a = ATTS[l]
                groups = a["groups"]
                ngr = len(groups)

                def t_lo(i, j):
                    wait(pool, l, "t_hi", i, j, 1)
                    pool.tensor_tensor(tlo[:, j % 2, :], raw[:, 0:SK], thi[:, j % 2, :].bitcast(FP32), ALU.subtract)\
                        .then_inc(A["t_lo"], 1)

                def n_lo(i, j):
                    wait(pool, l, "n_hi", i, j, 1)
                    pool.tensor_tensor(nlo[:, j % 2, :, :], raw_ctx(l).rearrange("p (c d) -> p c d", c=CHUNKS),
                                       nhi[:, j % 2, :, :].bitcast(FP32), ALU.subtract).then_inc(A["n_lo"], 1)

                def make_qbd(i, j):
                    if l == 1:
                        wait(pool, l, "q_mm", i, j, 0)
                        wait(pool, l, "q_in", i, j, 16)
                        pool.tensor_tensor(qbd1.rearrange("p (h q) -> p h q", h=HEADS),
                                           qb[:, j % 2, 0:S].unsqueeze(1).to_broadcast([P, HEADS, S]),
                                           hmask16[:, :].unsqueeze(2).to_broadcast([P, HEADS, S]), ALU.mult)\
                            .then_inc(A["qbd"], 1)

                def make_diag(i, j, g, u):
                    s = slot_of(a, g, u, j)
                    m = s_cols(a)
                    if u == 0:
                        wait(pool, l, "rb_mm", i, j, g)
                    wait(pool, l, "rden", i, j, unit_index(a, g, u) + 1)
                    pool.tensor_tensor(diag[0:m, u, 0:m], ident[0:m, 0:m], rdn[0:m, s:s + 1].to_broadcast([m, m]),
                                       ALU.mult).then_inc(A["diag"], 1)

                def step(i, j, k, nxt):
                    last = k == ngr - 1
                    if nxt and k == 0 and ngr > 1:
                        t_lo(*next_batch(i, j))
                    if nxt and ngr == 1:
                        n_lo(*next_batch(i, j))
                    if nxt and k == 1:
                        make_qbd(*next_batch(i, j))
                    for _, it in plan(a, k, nxt):
                        if it[0] == "s" and it[3] == 2:
                            make_diag(*(next_batch(i, j) if last else (i, j)), it[1], it[2])
                    if nxt and k == 1:
                        n_lo(*next_batch(i, j))

                if first or l == 0:
                    t_lo(0, 0)
                if first:
                    return
                make_qbd(0, 0)
                if l > 0:
                    pool.memset(bias[:, 0, :], 0.0).then_inc(bias_zero, 1)
                n_lo(0, 0)
                for u in range(len(groups[0])):
                    make_diag(0, 0, 0, u)
                with pool.Fori(0, B // 2 - 1) as i:
                    for j in range(2):
                        for k in range(ngr):
                            step(i, j, k, True)
                for j in range(2):
                    for k in range(ngr):
                        step(B // 2 - 1, j, k, j == 0)

            attention(0)

            def make_kbd(i, j):
                now = bass.ds((i * 2 + j) * S, S)
                pool.wait_ge(sa_s, i * 8 + (LEAD + 4 * j - 4))
                pool.tensor_copy(qsb[:, j, :, :], qk[:, 0:C, now])
                for c in range(C):
                    ins_ = pool.tensor_tensor(kbd[:, j, 8 * c:8 * c + 8, :],
                                              qk[:, 2 + c, now].unsqueeze(1).to_broadcast([P, 8, S]),
                                              hmask8[:, :].unsqueeze(2).to_broadcast([P, 8, S]), ALU.mult)
                ins_.then_inc(sa_kbd, 1)

            pool.wait_ge(rope, 16)
            with pool.Fori(0, B // 2) as i:
                for j in range(2):
                    make_kbd(i, j)
            for t in range(2):
                pool.wait_ge(xe_v, 2 + t + 1)
                pool.tensor_tensor(tok(xe[:, 1, :, :], t), tok(ctxT, t), tok(xe[:, 0, :, :], t), ALU.subtract)\
                    .then_inc(xe_l, 1)
            pool.wait_ge(load_w1att, 32)
            pool.memset(watt[:, 0:2048], 0.0).then_inc(wcv_step, 1)
            pool.wait_ge(wcv_step, 1)
            pool.tensor_copy(watt[:, 0:16 * (P + CHD1)].rearrange("p (h n) -> p h n", h=HEADS)[:, :, 0:CHD1],
                             wcv.rearrange("p (h d) -> p h d", h=HEADS)).then_inc(wcv_ok, 1)
            attention(1, first=True)
            pool.wait_ge(ev["cq"], 2)
            attention(1)
            for t in range(2):
                if t == 1:
                    pool.wait_ge(mm["dn"], 2)
                for m in range(FC1):
                    n = t * FC1 + m
                    rows = min(P, FF1 - m * P)
                    pool.wait_ge(gu_h, n + 1)
                    pool.tensor_tensor(hexp[0:rows, 0, m, :], hgu[0:rows, :], vm[0:rows, t * HALF:(t + 1) * HALF],
                                       ALU.mult).then_inc(gu_v, 1)
                    pool.wait_ge(gu_v, n + 1)
                    pool.tensor_tensor(hexp[0:rows, 1, m, :], hgu[0:rows, :], hexp[0:rows, 0, m, :],
                                       ALU.subtract).then_inc(ev["gu"], 1)
            for l in (2, 3):
                if l == 2:
                    pool.wait_ge(mm["gu"], 4 * FC1)
                else:
                    pool.wait_ge(norm_ok, 16)
                attention(l)

    return nc


def _columns(v):
    return v.reshape(C, P).T


def _chunks(w):
    return w.reshape(-1, P, w.shape[1]).transpose(1, 0, 2)


def _constants():
    f = np.float32
    d = np.arange(P) % HD1
    rot = np.zeros((P, P), f)
    rot[(np.arange(P) // HD1) * HD1 + (d + HD1 // 2) % HD1, np.arange(P)] = 1
    inv = (f(1.0) / f(10000.0) ** (np.arange(0, HD1, 2).astype(f) / f(HD1))).astype(f)
    ang = np.outer(np.arange(S).astype(f), inv).astype(f)[:, d % (HD1 // 2)]
    sign = np.where(d < HD1 // 2, f(-1), f(1))
    return dict(
        ident=np.eye(P, dtype=f), rot=rot, postab=np.concatenate([np.cos(ang), np.sin(ang) * sign], 1).astype(f),
        hmask8=(np.arange(P)[:, None] // HD1 == np.arange(8)[None]).astype(f),
        hmask16=(np.arange(P)[:, None] // CHD1 == np.arange(HEADS)[None]).astype(f),
        causal=np.where(np.tril(np.ones((S, S), bool)), f(0), f(-BIG)).astype(f))


def kernel(**inputs):
    import concourse.bacc as bacc
    from concourse.bass_utils import run_bass_kernel_spmd

    g = {k: np.asarray(v) for k, v in inputs.items()}
    g0 = lambda k: g["L0_xattn_" + k]
    g1 = lambda k: g["L1_xattn_" + k]
    ctx = g["ctx_1024"]
    wkv, ckv = g0("Wkv"), g1("ckv_w")
    vec = [g0("ln_q_g"), g0("ln_q_b"), g0("ln_ff_g"), g0("ln_ff_b"), g1("ln_in_w"), g1("ln_post_cross_w"),
           g1("ln_post_attn_w"), g["L2_xattn_norm_w"], g["L3_xattn_norm_w"], g["L2_xattn_b_gate"], g["L3_xattn_b_gate"]]
    f = np.float32
    arrays = dict(
        xT=g["x"].reshape(T, D).T.reshape(C, P, T).transpose(1, 0, 2), ctx=ctx, ctxT=ctx.transpose(0, 2, 1),
        mask=g["mask_BxS2_bk0"], tt=g["mask_BxS_ik0"].reshape(T), pos=g["pos_1xS"].reshape(S),
        vec=np.concatenate([_columns(v) for v in vec] + [np.arange(P, dtype=f)[:, None], np.zeros((P, 1), f)], 1),
        gates=np.concatenate([g0("attn_gate"), g0("ff_gate")]),
        wq=_chunks(g0("Wq")), wk0=_chunks(wkv[:, :F0].T), wv0=wkv[:, F0:], wo=_chunks(g0("Wo")),
        w1=_chunks(g0("W1")), w2=_chunks(g0("W2")),
        qkv=np.stack([_chunks(g1("v_qkv")), _chunks(g1("l_qkv"))]),
        dense1=np.stack([_chunks(g1("v_dense")), _chunks(g1("l_dense"))]),
        wcq=_chunks(g1("cq_w")), wck=ckv[:, :DM].T, wcv=ckv[:, DM:], wcd=g1("cdense_w"),
        gu=np.stack([np.stack([_chunks(g1(e + k)) for e in ("v_", "l_")]) for k in ("gate", "up")]),
        down=np.stack([g1("v_down"), g1("l_down")]),
        wmem=np.stack([_chunks(g[f"L{n}_xattn_W_mem"]) for n in (2, 3)]),
        wmemT=np.stack([g[f"L{n}_xattn_W_mem"].T for n in (2, 3)]),
        wgate=np.stack([_chunks(g[f"L{n}_xattn_W_gate"].T) for n in (2, 3)]),
        **_constants())
    nc = bacc.Bacc("TRN2", target_bir_lowering=False, num_devices=1)
    maps, aps = {}, {}
    for n, v in arrays.items():
        maps["in_" + n] = np.ascontiguousarray(v)
        aps[n] = nc.dram_tensor("in_" + n, v.shape, mybir.dt.from_np(v.dtype), kind="ExternalInput").ap()
    out = nc.dram_tensor("out_xT", (P, C, T), FP32, kind="ExternalOutput").ap()
    build_layers(nc, aps, out)
    r = run_bass_kernel_spmd(nc, [maps], core_ids=[0])
    y = r.results[0]["out_xT"]
    return y.transpose(2, 1, 0).reshape(B, S, D)
```

```python
import numpy as np
import concourse.bass as bass
from concourse import mybir
from contextlib import ExitStack

FP32 = mybir.dt.float32
FP32R = mybir.dt.float32r
U8 = mybir.dt.uint8
I32 = mybir.dt.int32
ALU = mybir.AluOpType
ACT = mybir.ActivationFunctionType
AX = mybir.AxisListType

P = 128
B, S, D = 8, 100, 256
T = B * S
HALF = T // 2
C = D // P
SK, DM = 1444, 128
HEADS = 16
DH0 = 64
F0 = 1024
HD1, CHD1 = 16, 8
FF1 = 688
FC1 = -(-FF1 // P)
BIG = 3.0e38
FMAX = 3.4e38

CHUNKS = 12
FULL = 10
TAIL = (SK - FULL * P) // 2
assert FULL * P + 2 * TAIL == SK


def chunk_rows(c):
    return P if c < FULL else TAIL


def chunk_start(c):
    return c * P if c < FULL else FULL * P + (c - FULL) * TAIL


PIECES = [(0, 512), (512, 1024), (1024, SK)]

WIDE = dict(groups=[[128] * 4, [128] * 3, [128] * 3, [128, 128, 64]],
            q_pieces=[(0, 3), (3, 6), (6, 8), (8, 11), (11, 14), (14, 16)],
            tiles=[[c] for c in range(CHUNKS)], ring=3,
            score_slots=8, query_slot=8, exp_lag=1, rden_slot=1, rb_slot=8, c_slot=3, t_slot=3, n_slot=3, bias_slot=6)
NARROW = dict(groups=[[S]], q_pieces=[(0, 1)],
              tiles=[[0, 1, 2, 3], [4, 5, 6, 7], [8, 9], [10, 11]], ring=2,
              s_slots=(0, 0, 1), exp_lag=2, q_slot=3, rden_slot=0, rb_slot=3, c_slot=1, n_slot=2, t_slot=3)
ATTS = [dict(WIDE, kind=0, c_pieces=2), dict(WIDE, kind=1, c_pieces=1),
        dict(NARROW, kind=2, c_pieces=1), dict(NARROW, kind=3, c_pieces=1)]


def head_at(n):
    return 2 * n if n < HEADS // 2 else 2 * n - HEADS + 1


LEAD = 1024


def batch_counts(a):
    nu = sum(len(g) for g in a["groups"])
    ng, nt, nq = len(a["groups"]), len(a["tiles"]), len(a["q_pieces"])
    return dict(raw_t=16, raw_n=32, raw_m=16 if a["kind"] == 0 else 0, q_in=0 if a["kind"] == 1 else 16,
                t_hi=1, n_hi=1, t_lo=1, n_lo=1, bias=1 if a["kind"] == 0 else 0,
                qbd=1 if a["kind"] == 1 else 0, q_mm=nq, q_hi=nq, q_lo=nq,
                s_mm=3 * nu, s_neg=3 * nu, nmax=nu, p_exp=nu, rden=3 * ng, diag=ng,
                t_mm=ng * nt, pt_hi=ng * nt, pt_lo=ng * nt, pv_mm=ng * nt,
                rb_mm=ng, rb_sb=ng, o_ev=ng if ng > 1 else 2, c_mm=a["c_pieces"], c_ev=a["c_pieces"])


COUNTS = [batch_counts(a) for a in ATTS]
STARTED_BY = dict(sync=["raw_t", "raw_n", "raw_m", "q_in"],
                  vector=["t_hi", "n_hi", "bias", "q_lo", "s_neg", "nmax", "rden", "pt_lo", "o_ev"],
                  gpsimd=["t_lo", "n_lo", "qbd", "diag"],
                  scalar=["q_hi", "p_exp", "pt_hi", "rb_sb", "c_ev"],
                  tensor=["q_mm", "s_mm", "t_mm", "pv_mm", "rb_mm", "c_mm"])


def build_layers(nc, ins, out):
    ctx = ExitStack()
    with ctx:
        def sb(name, shape, dt=FP32):
            return ctx.enter_context(nc.sbuf_tensor(name, shape, dt))

        def sem(name):
            return ctx.enter_context(nc.semaphore(name))

        x = sb("x", [P, C, T])
        big = sb("big", [P, 8 * T])
        wide = sb("wide", [P, 7, SK])
        work = sb("work", [P, 8384])
        qhi = sb("qhi", [P, 2, 1664], FP32R)
        qlo = sb("qlo", [P, 2, 1664], FP32R)
        thi = sb("thi", [P, 2, SK], FP32R)
        tlo = sb("tlo", [P, 2, SK], FP32R)
        nhi = sb("nhi", [P, 2, CHUNKS, DM], FP32R)
        nlo = sb("nlo", [P, 2, CHUNKS, DM], FP32R)
        pt = sb("pt", [P, 3, 2, 512], FP32R)
        watt = sb("watt", [P, 2304])
        vec = sb("vec", [P, 23])
        ident = sb("ident", [P, P])
        ones_r = sb("ones_r", [P, P], FP32R)
        diag_hi = sb("diag_hi", [P, 4, P], FP32R)
        diag_lo = sb("diag_lo", [P, 4, P], FP32R)
        hmask8 = sb("hmask8", [P, 8])
        hmask16 = sb("hmask16", [P, HEADS])
        eps5 = sb("eps5", [P, 1])
        eps6 = sb("eps6", [P, 1])
        vm = sb("vm", [P, T])
        cossin = sb("cossin", [P, 2, S])
        late = sb("late", [P, SK // 4 + 7])
        tgate = sb("tgate", [P, 2])
        negmin3 = sb("negmin3", [P, 7, 3])
        negmax = sb("negmax", [P, 7])
        rdn_hi = sb("rdn_hi", [P, 7], FP32R)
        ps = ctx.enter_context(nc.psum_tensor("ps", [P, 8, 512], FP32))

        pthi, ptlo = pt[:, :, 0, :], pt[:, :, 1, :]
        ones = ones_r[:, :].bitcast(FP32)
        mask_u8 = late[:, 0:SK // 4].bitcast(U8)
        warm = late[:, SK // 4:SK // 4 + 1]
        rot = late[:, 0:P]
        causal = late[0:S, P:P + S]
        rstat = late[0:S, P + S:P + S + 6 * HEADS].rearrange("p (j n) -> p j n", j=2)
        raw = work[:, 0:1536]
        outT = work[:, 1536:3136]
        bias = work[:, 3136:6024].rearrange("p (j k) -> p j k", j=2)
        rbc = work[:, 6024:6536]
        den, rdn, rdn_lo = (work[:, 8136 + 7 * n:8143 + 7 * n] for n in range(3))
        qb = work[:, 6536:8136].rearrange("p (j k) -> p j k", j=2)
        raw_narrow = wide[:, 5:7, :].rearrange("p u k -> p (u k)")[:, 0:1536]
        xe = work[:, 1536:4736].rearrange("p (e c t) -> p e c t", e=2, c=C)
        xn = work[:, 4736:6336].rearrange("p (c t) -> p c t", c=C)
        xc = work[:, 1536:3136].rearrange("p (c t) -> p c t", c=C)
        rstd = work[:, 7136:7936]
        rmask = work[:, 6336:7136].rearrange("p (e t) -> p e t", e=2)
        vtok = work[0:S, 6336:8384].rearrange("p (b d) -> p b d", b=B)
        wflat = wide[:, :, :].rearrange("p u k -> p (u k)")
        wq = wflat[:, 0:2048].rearrange("p (c n) -> p c n", c=C)
        wo = wflat[:, 0:2048].rearrange("p (c n) -> p c n", c=8)
        w1 = wflat[:, 2048:4096].rearrange("p (c n) -> p c n", c=C)
        w2 = wflat[:, 4096:6144].rearrange("p (c n) -> p c n", c=8)
        wqkv = wflat[:, 6144:9216].rearrange("p (e c n) -> p e c n", e=2, c=C)
        wcq = wflat[:, 9216:9472].rearrange("p (c n) -> p c n", c=C)
        wdn1 = wflat[:, 0:1024].rearrange("p (e c n) -> p e c n", e=2, c=C)
        kbd = wflat[:, 1024:4224].rearrange("p (j h q) -> p j h q", j=2, h=HEADS)
        sself = wflat[0:S, 4224:7424].rearrange("p (j h q) -> p j h q", j=2, h=HEADS)
        wgu = wflat[:, 0:5504].rearrange("p (g e c n) -> p g e c n", g=2, e=2, c=C)
        wdown = wflat[:, 5504:8576].rearrange("p (e c n) -> p e c n", e=2, c=FC1)
        gsilu = wflat[:, 8576:9376].rearrange("p (j t) -> p j t", j=2)
        hgu = wflat[:, 9376:9776]
        wcd = wflat[:, 9776:10032]
        wk0 = watt[:, 0:1024].rearrange("p (c n) -> p c n", c=8)
        wv0 = watt[:, 1024:2048]
        wck = watt[:, 2048:2176]
        wcv = watt[:, 2176:2304]
        wcvh = watt[:, 0:2048].rearrange("p (h n) -> p h n", h=HEADS)
        wmem = [watt[:, o:o + 256].rearrange("p (c n) -> p c n", c=C) for o in (0, 1536)]
        wmemT = [watt[:, o:o + 256] for o in (256, 1792)]
        wgate = watt[:, 512:1536].rearrange("p (c n) -> p c n", c=4)
        big8 = big[:, :].rearrange("p (c t) -> p c t", c=8)
        qk = big[:, 0:4 * T].rearrange("p (c t) -> p c t", c=4)
        qsb = big[:, 4 * T:4 * T + 4 * S].rearrange("p (j c t) -> p j c t", j=2, c=C)
        ptself = big[0:S, 5 * T:7 * T].rearrange("p (h q) -> p h q", h=HEADS)
        ctok = big[0:S, 7 * T + 512:7 * T + 768]
        cq = big[:, 0:T]
        cT = big[:, T:2 * T]
        qbd1 = big[:, 4 * T:6 * T]
        hexp = big[:, 0:12 * HALF].rearrange("p (e c t) -> p e c t", e=2, c=FC1)
        mc = big[:, 0:2 * T].rearrange("p (c t) -> p c t", c=C)
        gate = big[:, 2 * T:4 * T].rearrange("p (c t) -> p c t", c=C)
        ctxT = xn
        rotated = work[:, 4736:5536].rearrange("p (j t) -> p j t", j=2)
        postab = wflat[0:S, 4096:4096 + 2 * P]
        pos_i = wflat[:, 4352:4452].bitcast(I32)
        pos_f = wflat[:, 4452:4552]
        pos_neg = wflat[:, 4552:4652]
        onehot = wflat[0:S, 4652:4752]
        tt_i = big[:, 0:T].bitcast(I32)
        tt_one = big[:, T:2 * T].rearrange("p (b s) -> p b s", b=B)
        VEC = {n: k for k, n in enumerate(
            ["ln_q_g", "ln_q_b", "ln_ff_g", "ln_ff_b", "ln_in", "ln_cross", "ln_post", "n2", "n3", "b2", "b3"])}

        def raw_ctx(l):
            return raw if len(ATTS[l]["groups"]) > 1 else raw_narrow

        def vcol(name, c):
            return vec[:, 2 * VEC[name] + c:2 * VEC[name] + c + 1]

        A = {n: sem(n) for names in STARTED_BY.values() for n in names}
        passed = {n: sem(f"passed_{n}") for n in ("loads", "scores")}
        load_consts = sem("load_consts")
        load_x = [sem("load_x_first"), sem("load_x_second")]
        load_w0 = sem("load_w0")
        load_wo = sem("load_wo")
        load_w12 = sem("load_w12")
        load_qkv = sem("load_qkv")
        load_w1att = sem("load_w1att")
        load_d1 = sem("load_d1")
        load_rot = sem("load_rot")
        load_cd = sem("load_cd")
        load_gu = sem("load_gu")
        load_down = sem("load_down")
        load_mem = sem("load_mem")
        load_gate = sem("load_gate")
        consts = sem("consts")
        mean_mm = sem("mean_mm")
        centred = sem("centred")
        squared = sem("squared")
        var_mm = sem("var_mm")
        std_ok = sem("std_ok")
        norm_step = sem("norm_step")
        norm_ok = sem("norm_ok")
        gates_ok = sem("gates_ok")
        DENSE = ["q0", "o0", "f1", "f2", "qk", "rt", "vt", "d1", "cq", "cd", "gu", "dn", "g2", "g3"]
        mm = {n: sem(f"{n}_mm") for n in DENSE}
        ev = {n: sem(f"{n}_ev") for n in DENSE}
        rt_s = sem("rt_s")
        xe_v = sem("xe_v")
        xe_l = sem("xe_l")
        gu_h = sem("gu_h")
        gu_silu = sem("gu_silu")
        pos_ok = sem("pos_ok")
        cossin_mm = sem("cossin_mm")
        cossin_ok = sem("cossin_ok")
        bias_zero = sem("bias_zero")
        gu_v = sem("gu_v")
        vm_step = sem("vm_step")
        wcv_step = sem("wcv_step")
        fuse = sem("fuse")
        rope = sem("rope")
        sa_kbd = sem("sa_kbd")
        sa_s = sem("sa_s")
        sa_m = sem("sa_m")
        sa_x = sem("sa_x")
        sa_sub = sem("sa_sub")
        sa_e = sem("sa_e")
        sa_den = sem("sa_den")
        sa_t = sem("sa_t")
        sa_pt = sem("sa_pt")
        sa_c = sem("sa_c")
        sa_ct = sem("sa_ct")
        sa_ctt = sem("sa_ctt")
        sa_out = sem("sa_out")
        wcv_ok = sem("wcv_ok")
        stored = sem("stored")

        base = [{n: LEAD + B * sum(COUNTS[m][n] for m in range(l)) for n in A} for l in range(5)]

        def at(l, name, i, j, k=0):
            n = COUNTS[l][name]
            return i * (2 * n) + (base[l][name] + j * n + k)

        def done(l, name):
            return base[l + 1][name]

        def wait(eng, l, name, i, j, k=0):
            eng.wait_ge(A[name], at(l, name, i, j, k))

        def carry_wait(eng, name):
            eng.sem_inc(passed[name], 1)

        def next_batch(i, j):
            return i, j + 1

        def q_batch(a, i, j):
            return (i, j + 1) if len(a["groups"]) > 1 else (i, j + 2)

        def plan(a, k, nxt, after_next=False):
            groups = a["groups"]
            if len(groups) == 1:
                return ([(a["s_slots"][j], ("s", 0, 0, j)) for j in range(3)] if nxt else []) + \
                    ([(a["q_slot"], ("q", 0))] if after_next else [])
            last = k == len(groups) - 1
            ng = 0 if last else k + 1
            scores = [("s", ng, u, j) for u in range(len(groups[ng])) for j in range(3)] if nxt or not last else []
            queries = [("q", x) for x in range(len(a["q_pieces"]))] if nxt and k == len(groups) - 2 else []
            n = len(scores)
            return sorted([((m * a["score_slots"] + n // 2) // n, it) for m, it in enumerate(scores)] +
                          [(a["query_slot"] + m, it) for m, it in enumerate(queries)], key=lambda p: p[0])

        def unit_index(a, g, u):
            return sum(len(x) for x in a["groups"][:g]) + u

        def unit_col(a, g, u):
            return sum(sum(x) for x in a["groups"][:g]) + sum(a["groups"][g][:u])

        def slot_of(a, g, u, j):
            odd = (g if len(a["groups"]) > 1 else j) % 2
            return 4 * odd + u

        def q_cols(a, x):
            h0, h1 = a["q_pieces"][x]
            return h0 * S, h1 * S

        def q_need(a, col):
            return next(x + 1 for x in range(len(a["q_pieces"])) if q_cols(a, x)[1] >= min(col, q_cols(a, len(a["q_pieces"]) - 1)[1]))

        def s_cols(a):
            return P if a["kind"] < 2 else S

        block = ctx.enter_context(nc.Block())

        @block.sync
        def _(sp):
            for n in STARTED_BY["sync"]:
                sp.sem_inc(A[n], LEAD)
            for t in range(2):
                sp.dma_start(x[:, :, t * HALF:(t + 1) * HALF], ins["xT"][:, :, t * HALF:(t + 1) * HALF])\
                  .then_inc(load_x[t], 16)
            for dst, src in [(vec[:, :], ins["vec"]), (ident[:, :], ins["ident"]),
                             (hmask8[:, :], ins["hmask8"]), (hmask16[:, :], ins["hmask16"]),
                             (tgate[:, :], ins["gates"].partition_broadcast(P)),
                             (postab, ins["postab"]), (pos_i, ins["pos"].partition_broadcast(P)),
                             (tt_i, ins["tt"].partition_broadcast(P))]:
                sp.dma_start(dst, src).then_inc(load_consts, 16)
            sp.dma_start(wq, ins["wq"]).then_inc(load_w0, 16)
            sp.dma_start(wk0, ins["wk0"]).then_inc(load_w0, 16)
            sp.dma_start(wv0, ins["wv0"]).then_inc(load_w0, 16)

            def attention_loads(l, ready=None, first=False):
                narrow = len(ATTS[l]["groups"]) == 1

                def load_ctxT(i, j):
                    wait(sp, l, "t_lo" if narrow else "n_lo", i, j - 1, 1)
                    carry_wait(sp, "loads")
                    sp.dma_start(raw[:, 0:SK], ins["ctxT"][bass.ds(sp.snap(i * 2 + j), 1), :, :]
                                 .rearrange("o p k -> p (o k)")).then_inc(A["raw_t"], 16)

                def load_queries(i, j):
                    b = sp.snap(i * 2 + j)
                    ready(i, j)
                    if narrow:
                        wait(sp, l, "q_mm", i, j, 0)
                    else:
                        wait(sp, l, "q_mm", i, j - 1, 0)
                    carry_wait(sp, "loads")
                    if l == 0:
                        sp.dma_start(qb[:, j % 2, :].rearrange("p (c t) -> p c t", c=8),
                                     big8[:, :, bass.ds(b * S, S)]).then_inc(A["q_in"], 16)
                    else:
                        sp.dma_start(qb[:, j % 2, 0:2 * S].rearrange("p (c t) -> p c t", c=C),
                                     x[:, :, bass.ds(b * S, S)]).then_inc(A["q_in"], 16)

                def load_mask(i, j):
                    wait(sp, l, "bias", i, j - 1, 1)
                    carry_wait(sp, "loads")
                    sp.dma_start(mask_u8, ins["mask"][bass.ds(sp.snap(i * 2 + j), 1), :].rearrange("o k -> (o k)")
                                 .partition_broadcast(P)).then_inc(A["raw_m"], 16)

                def load_ctx(i, j):
                    if narrow:
                        wait(sp, l, "n_lo", i, j - 1, 1)
                    else:
                        wait(sp, l, "t_lo", i, j, 1)
                    carry_wait(sp, "loads")
                    ctx_b = ins["ctx"][bass.ds(sp.snap(i * 2 + j), 1), :, :]
                    rawn = raw_ctx(l).rearrange("p (c d) -> p c d", c=CHUNKS)
                    sp.dma_start(rawn[:, 0:FULL, :], ctx_b[:, 0:FULL * P, :]
                                 .rearrange("o (c p) d -> p (o c) d", p=P)).then_inc(A["raw_n"], 16)
                    sp.dma_start(rawn[0:TAIL, FULL:CHUNKS, :], ctx_b[:, FULL * P:SK, :]
                                 .rearrange("o (c p) d -> p (o c) d", p=TAIL)).then_inc(A["raw_n"], 16)

                if first:
                    load_ctxT(0, 0)
                elif narrow:
                    load_queries(0, 0)
                    with sp.Fori(0, B // 2 - 1) as i:
                        for j in range(2):
                            load_ctxT(i, j + 1)
                            load_queries(i, j + 1)
                            load_ctx(i, j)
                    load_ctxT(B // 2 - 1, 1)
                    load_queries(B // 2 - 1, 1)
                    for j in range(2):
                        load_ctx(B // 2 - 1, j)
                else:
                    def rest_of(i, j):
                        if l == 0:
                            load_mask(i, j)
                        load_ctx(i, j)

                    def start_of(i, j):
                        load_ctxT(i, j)
                        if l == 0:
                            load_queries(i, j)

                    start_of(0, 0)
                    with sp.Fori(0, B // 2 - 1) as i:
                        for j in range(2):
                            rest_of(i, j)
                            start_of(i, j + 1)
                    rest_of(B // 2 - 1, 0)
                    start_of(B // 2 - 1, 1)
                    rest_of(B // 2 - 1, 1)

            sp.wait_ge(consts, 2)
            attention_loads(0, lambda i, j: sp.wait_ge(ev["q0"], 8 if isinstance(i, int) and (i, j) == (0, 0) else 16))
            sp.wait_ge(A["t_mm"], done(0, "t_mm") - CHUNKS)
            sp.dma_start(wo, ins["wo"]).then_inc(load_wo, 16)
            sp.dma_start(w1, ins["w1"]).then_inc(load_w12, 16)
            sp.wait_ge(A["t_mm"], done(0, "t_mm"))
            sp.dma_start(w2, ins["w2"]).then_inc(load_w12, 16)
            for e in range(2):
                sp.dma_start(wqkv[:, e, :, :], ins["qkv"][e]).then_inc(load_qkv, 16)
            sp.dma_start(wcq, ins["wcq"]).then_inc(load_qkv, 16)
            sp.wait_ge(A["bias"], done(0, "bias"))
            sp.dma_start(rot, ins["rot"]).then_inc(load_rot, 16)
            sp.dma_start(causal, ins["causal"]).then_inc(load_rot, 16)
            sp.wait_ge(A["c_mm"], done(0, "c_mm"))
            sp.dma_start(wck, ins["wck"]).then_inc(load_w1att, 16)
            sp.dma_start(wcv, ins["wcv"]).then_inc(load_w1att, 16)
            sp.wait_ge(mm["o0"], 4)
            for e in range(2):
                sp.dma_start(wdn1[:, e, :, :], ins["dense1"][e]).then_inc(load_d1, 16)

            attention_loads(1)
            sp.wait_ge(A["n_lo"], done(1, "n_lo"))
            attention_loads(2, first=True)
            sp.wait_ge(A["t_mm"], done(1, "t_mm") - CHUNKS)
            for g in range(2):
                for e in range(2):
                    sp.dma_start(wgu[:, g, e, :, :], ins["gu"][g, e]).then_inc(load_gu, 16)
            sp.wait_ge(A["t_mm"], done(1, "t_mm"))
            sp.dma_start(wcd, ins["wcd"]).then_inc(load_cd, 16)
            for e in range(2):
                sp.dma_start(wdown[:, e, 0:FC1 - 1, :], ins["down"][e, 0:(FC1 - 1) * P, :]
                             .rearrange("(c p) n -> p c n", p=P)).then_inc(load_down, 16)
                sp.dma_start(wdown[0:FF1 % P, e, FC1 - 1, :], ins["down"][e, (FC1 - 1) * P:FF1, :])\
                  .then_inc(load_down, 16)
            sp.wait_ge(A["c_mm"], done(1, "c_mm"))
            for l in (2, 3):
                sp.dma_start(wmem[l - 2], ins["wmem"][l - 2]).then_inc(load_mem, 16)
                sp.dma_start(wmemT[l - 2], ins["wmemT"][l - 2]).then_inc(load_mem, 16)
            for l in (2, 3):
                if l == 3:
                    sp.wait_ge(mm["g2"], 4)
                sp.dma_start(wgate, ins["wgate"][l - 2]).then_inc(load_gate, 16)
                def ready(i, j):
                    of_first = isinstance(i, int) and (i, j) == (0, 0)
                    if l == 2:
                        sp.wait_ge(ev["dn"], 2 if of_first else 4)
                    else:
                        sp.wait_ge(norm_ok, 14 if of_first else 16)
                attention_loads(l, ready)
                if l == 2:
                    attention_loads(3, first=True)
            for t in range(2):
                sp.wait_ge(norm_ok, 16 + 2 * t + 2)
                sp.dma_start(out[:, :, t * HALF:(t + 1) * HALF], x[:, :, t * HALF:(t + 1) * HALF]).then_inc(stored, 16)
            sp.wait_ge(stored, 32)

        @block.tensor
        def _(pe):
            for n in STARTED_BY["tensor"]:
                pe.sem_inc(A[n], LEAD)
            pe.sem_inc(sa_ctt, LEAD)
            pe.sem_inc(sa_s, LEAD)
            pe.sem_inc(sa_c, LEAD)

            def bank(t, m):
                return ps[:, 4 * t + m % 4, 0:HALF]

            def half(ap, t):
                return ap[:, t * HALF:(t + 1) * HALF]

            def mean(n, t):
                if n == 0:
                    pe.wait_ge(load_x[t], 16)
                    pe.wait_ge(consts, 1)
                else:
                    pe.wait_ge(ev["o0"], 2 * t + 2)
                for c in range(C):
                    last = pe.matmul(bank(t, 0), ones, half(x[:, c, :], t), start=c == 0, stop=c == C - 1)
                last.then_inc(mean_mm, 1)

            def var(n, t):
                pe.wait_ge(squared, 2 * n + t + 1)
                for c in range(C):
                    last = pe.matmul(bank(t, 1), ones, half(xn[:, c, :], t), start=c == 0, stop=c == C - 1)
                last.then_inc(var_mm, 1)

            def dense(name, tiles, operands, ready, between=None):
                for t in range(2):
                    ready(t)
                    for m in range(tiles):
                        if m >= 4:
                            pe.wait_ge(ev[name], t * tiles + m - 3)
                        if t == 1 and between:
                            between(m)
                        ops = operands(t, m)
                        rows = ops[0][0].shape[1]
                        for n, (w, v) in enumerate(ops):
                            last = pe.matmul(bank(t, m)[0:rows, :], w, v, start=n == 0, stop=n == len(ops) - 1)
                        last.then_inc(mm[name], 1)

            def gate_chunk(l, t, m):
                pe.wait_ge(load_gate, 16 * (l - 1))
                for n in range(4):
                    last = pe.matmul(bank(t, m), wgate[:, n, m * P:(m + 1) * P],
                                     half((x if n < 2 else mc)[:, n % 2, :], t), start=n == 0, stop=n == 3)
                last.then_inc(mm[f"g{l}"], 1)

            def attention(l):
                a = ATTS[l]
                groups, tiles, ring = a["groups"], a["tiles"], a["ring"]
                nu = sum(len(g) for g in groups)
                nq, nt, ngr = len(a["q_pieces"]), len(tiles), len(groups)

                def q_piece(i, j, xq):
                    p = j % 2
                    c0, c1 = q_cols(a, xq)
                    if xq < 3:
                        wait(pe, l, "s_neg", i, j - 1, 3 * nu - 3 + xq + 1)
                    else:
                        wait(pe, l, "q_lo", i, j, xq - 2)
                    if l == 1:
                        wait(pe, l, "qbd", i, j, 1)
                    elif xq == 0:
                        wait(pe, l, "q_in", i, j, 16)
                    dst = ps[:, xq % 3, :]
                    if l == 0:
                        h0, h1 = a["q_pieces"][xq]
                        for n in range(h0, h1):
                            h = head_at(n)
                            r = DH0 * (h % 2)
                            last = pe.matmul(dst[:, (n - h0) * S:(n - h0 + 1) * S], wk0[r:r + DH0, h // 2, :],
                                             qb[r:r + DH0, p, (h // 2) * S:(h // 2 + 1) * S], start=True, stop=True)
                    elif l == 1:
                        last = pe.matmul(dst[:, 0:c1 - c0], wck, qbd1[:, c0:c1], start=True, stop=True)
                    else:
                        for c in range(C):
                            last = pe.matmul(dst[:, 0:S], wmem[l - 2][:, c, :], qb[:, p, c * S:(c + 1) * S],
                                             start=c == 0, stop=c == C - 1)
                    last.then_inc(A["q_mm"], 1)

                def s_piece(i, j, g, u, jj):
                    p = j % 2
                    n = 3 * unit_index(a, g, u) + jj
                    col = unit_col(a, g, u)
                    m = s_cols(a)
                    if jj == 0:
                        wait(pe, l, "q_lo", i, j, q_need(a, col + m))
                    if n == 0:
                        wait(pe, l, "t_lo", i, j, 1)
                    if n < 3:
                        if nq == 1 and n > 0:
                            wait(pe, l, "s_neg", i, j - 1, 3 * nu - 3 + n + 1)
                        else:
                            wait(pe, l, "q_lo", i, j, nq if nq == 1 else nq - 3 + n + 1)
                    else:
                        wait(pe, l, "s_neg", i, j, n - 2)
                    k0, k1 = PIECES[jj]
                    dst = ps[0:m, jj, 0:k1 - k0]
                    for r, (w, v) in enumerate([(qhi, thi), (qhi, tlo), (qlo, thi)]):
                        last = pe.matmul(dst, w[:, p, col:col + m], v[:, p, k0:k1], start=r == 0, stop=r == 2)
                    last.then_inc(A["s_mm"], 1)

                def t_tile(i, j, k, c):
                    tt = k * nt + c
                    if c == 0:
                        wait(pe, l, "p_exp", i, j, unit_index(a, k, len(groups[k]) - 1) + 1)
                    wait(pe, l, "pt_lo", i, j, tt - ring + 1)
                    dst = ps[:, 3 + tt % ring, :]
                    off = 0
                    for ch in tiles[c]:
                        kr, ks = chunk_rows(ch), chunk_start(ch)
                        for u, rows in enumerate(groups[k]):
                            src = wide[0:rows, slot_of(a, k, u, j), ks:ks + kr]
                            last = pe.transpose(dst[0:kr, off:off + rows], src, ident[0:rows, 0:rows])
                            off += rows
                    last.then_inc(A["t_mm"], 1)

                def pv_tile(i, j, k, c):
                    p = j % 2
                    tt = k * nt + c
                    if c == 0:
                        wait(pe, l, "n_lo", i, j, 1)
                        wait(pe, l, "o_ev", i, j, k)
                    wait(pe, l, "pt_lo", i, j, tt + 1)
                    w = sum(groups[k])
                    for n, ch in enumerate(tiles[c]):
                        kr = chunk_rows(ch)
                        if ngr == 1:
                            cols = slice(n * w, (n + 1) * w)
                            products = [(2 * w, nhi, pt[0:kr, tt % ring, :, cols]), (w, nlo, pthi[0:kr, tt % ring, cols])]
                            for r, (cw, lh, rh) in enumerate(products if ch == 0 else products[::-1]):
                                last = pe.matmul(ps[:, 6, 0:cw], lh[0:kr, p, ch, :], rh,
                                                 start=ch == 0 and r == 0, stop=ch == CHUNKS - 1 and r == 1)
                            continue
                        for r, (lh, rh) in enumerate([(nhi, pthi), (nhi, ptlo), (nlo, pthi)]):
                            last = pe.matmul(ps[:, 6, 0:w], lh[0:kr, p, ch, :],
                                             rh[0:kr, tt % ring, n * w:(n + 1) * w],
                                             start=ch == 0 and r == 0, stop=ch == CHUNKS - 1 and r == 2)
                    last.then_inc(A["pv_mm"], 1)

                def rb(i, j, k):
                    wait(pe, l, "diag", i, j, k + 1)
                    if k == 0:
                        wait(pe, l, "c_ev", i, j, 0)
                    else:
                        wait(pe, l, "rb_sb", i, j, k)
                    off = 0
                    for u, rows in enumerate(groups[k]):
                        for r, d in enumerate((diag_hi, diag_lo)):
                            last = pe.matmul(ps[:, 7, off:off + rows], ones_r[0:rows, :], d[0:rows, u, 0:rows],
                                             start=r == 0, stop=r == 1)
                        off += rows
                    last.then_inc(A["rb_mm"], 1)

                def c_piece(i, j, xq):
                    if xq == 0:
                        wait(pe, l, "o_ev", i, j, COUNTS[l]["o_ev"])
                        wait(pe, l, "rb_sb", i, j, ngr)
                    else:
                        wait(pe, l, "c_ev", i, j, xq)
                    if l == 0:
                        for h in range(8 * xq, 8 * xq + 8):
                            r, c = DH0 * (h % 2), (h // 2 - 4 * xq) * S
                            n = next(n for n in range(HEADS) if head_at(n) == h)
                            last = pe.matmul(ps[r:r + DH0, 7, c:c + S], wv0[:, h * DH0:(h + 1) * DH0],
                                             outT[:, n * S:(n + 1) * S], start=True, stop=True)
                    elif l == 1:
                        for h in range(HEADS):
                            last = pe.matmul(ps[:, 7, 0:S], wcvh[:, h, :], outT[:, h * S:(h + 1) * S],
                                             start=h == 0, stop=h == HEADS - 1)
                    else:
                        for c in range(C):
                            last = pe.matmul(ps[:, 7, c * S:(c + 1) * S], wmemT[l - 2][:, c * P:(c + 1) * P],
                                             outT[:, 0:S], start=True, stop=True)
                    last.then_inc(A["c_mm"], 1)

                def item(i, j, it):
                    if it[0] == "q":
                        q_piece(i, j, it[1])
                    else:
                        s_piece(i, j, *it[1:])

                def step(i, j, k, nxt, before=None, after_next=False):
                    last = k == ngr - 1
                    items = plan(a, k, nxt, after_next)
                    for s in range(nt + 2):
                        if s < nt:
                            t_tile(i, j, k, s)
                        for at_slot, it in items:
                            if at_slot == s:
                                item(*(q_batch(a, i, j) if it[0] == "q" else next_batch(i, j) if last else (i, j)), it)
                        if s >= 2:
                            pv_tile(i, j, k, s - 2)
                        if before is not None and s - a["c_slot"] in range(a["c_pieces"]):
                            c_piece(*before, s - a["c_slot"])
                        if s == a["rb_slot"]:
                            rb(i, j, k)
                        if ngr == 1 and not nxt and s in (1, 2):
                            if s == 1:
                                pe.wait_ge(A["c_ev"], at(l, "c_ev", B // 4, 0))
                                pe.wait_ge(A["s_neg"], done(l, "s_neg"))
                            gate_chunk(l, 0, s - 1)

                for xq in range(nq):
                    q_piece(0, 0, xq)
                for u in range(len(groups[0])):
                    for jj in range(3):
                        s_piece(0, 0, 0, u, jj)
                if ngr == 1:
                    q_piece(0, 1, 0)
                step(0, 0, 0, True, after_next=True)
                if ngr > 1:
                    with pe.Fori(0, B // 2 - 1) as i:
                        for j in range(2):
                            for k in range(1, ngr):
                                step(i, j, k, True)
                            step(i, j + 1, 0, True, before=(i, j))
                    for j in range(2):
                        for k in range(1, ngr):
                            step(B // 2 - 1, j, k, j == 0)
                        if j == 0:
                            step(B // 2 - 1, 1, 0, False, before=(B // 2 - 1, 0))
                else:
                    with pe.Fori(0, B // 2 - 2) as i:
                        for j in range(2):
                            step(i, j + 1, 0, True, before=(i, j), after_next=True)
                    for b in (B - 3, B - 2, B - 1):
                        step(b // 2, b % 2, 0, b < B - 1, before=((b - 1) // 2, (b - 1) % 2), after_next=b < B - 2)
                for xq in range(a["c_pieces"]):
                    c_piece(B // 2 - 1, 1, xq)

            for t in range(2):
                mean(0, t)
            for t in range(2):
                var(0, t)

            def ready(t):
                pe.wait_ge(norm_ok, 2 * t + 2)
                if t == 0:
                    pe.wait_ge(load_w0, 48)
            dense("q0", 8, lambda t, m: [(wq[:, c, m * P:(m + 1) * P], half(xn[:, c, :], t)) for c in range(C)], ready)
            pe.wait_ge(ev["q0"], 16)
            pe.wait_ge(pos_ok, 5)
            for n in range(2):
                last = pe.matmul(ps[:, 7, n * S:(n + 1) * S], postab[:, n * P:(n + 1) * P], onehot, start=True, stop=True)
            last.then_inc(cossin_mm, 1)
            attention(0)

            def ready(t):
                pe.wait_ge(A["c_ev"], done(0, "c_ev"))
                pe.wait_ge(load_wo, 16)
            dense("o0", 2, lambda t, m: [(wo[:, c, m * P:(m + 1) * P], half(big8[:, c, :], t)) for c in range(8)], ready,
                  lambda m: mean(1, 0) if m == 0 else var(1, 0))
            mean(1, 1)
            var(1, 1)

            def ready(t):
                pe.wait_ge(norm_ok, 4 + 2 * t + 2)
                pe.wait_ge(load_w12, 32)
            dense("f1", 8, lambda t, m: [(w1[:, c, m * P:(m + 1) * P], half(xn[:, c, :], t)) for c in range(C)], ready)

            def ready(t):
                pe.wait_ge(ev["f1"], 8 * t + 8)
            dense("f2", 2, lambda t, m: [(w2[:, c, m * P:(m + 1) * P], half(big8[:, c, :], t)) for c in range(8)], ready,
                  lambda m: var(2, 0) if m == 1 else None)

            var(2, 1)

            def experts(w, t, m, n=P):
                return [(w[:, e, c, m * P:m * P + n], half(xe[:, e, c, :], t)) for e in range(2) for c in range(C)]

            def ready(t):
                pe.wait_ge(xe_l, t + 1)
                pe.wait_ge(load_qkv, 48)
            dense("qk", 4, lambda t, m: experts(wqkv, t, m), ready)

            def ready(t):
                pe.wait_ge(ev["qk"], 4 * t + 4)
                pe.wait_ge(load_rot, 32)
            dense("rt", 4, lambda t, m: [(rot, half(qk[:, m, :], t))], ready)

            for b in range(B):
                pe.wait_ge(rt_s, b + 1)
                for n in range(4):
                    e, c = n // 2, n % 2
                    last = pe.matmul(ps[0:S, b, 0:D], xe[:, e, c, b * S:(b + 1) * S], wqkv[:, e, c, 2 * D:3 * D],
                                     start=n == 0, stop=n == 3)
                last.then_inc(mm["vt"], 1)

            def sa_scores(i, j):
                pe.wait_ge(sa_kbd, i * 2 + (LEAD + j + 1))
                for n in range(4):
                    pe.wait_ge(sa_m, i * 8 + (LEAD + 4 * (j - 1) + n + 1))
                    last = pe.matmul(ps[0:S, n, 0:4 * S], qsb[:, j % 2, n // 2, :], kbd[:, j % 2, 4 * n:4 * n + 4, :],
                                     start=True, stop=True)
                    last.then_inc(sa_s, 1)

            def sa_transposes(i, j):
                pe.wait_ge(sa_e, i * 2 + (LEAD + j + 1))
                for n in range(4):
                    pe.wait_ge(sa_pt, i * 8 + (LEAD + 4 * j + n - 1))
                    for h in range(4):
                        last = pe.transpose(ps[0:S, 4 + n % 2, h * S:(h + 1) * S], sself[:, j % 2, 4 * n + h, :],
                                            ident[0:S, 0:S])
                    last.then_inc(sa_t, 1)

            def sa_values(i, j):
                pe.wait_ge(sa_pt, i * 8 + (LEAD + 4 * j + 4))
                pe.wait_ge(sa_ct, i * 2 + (LEAD + j))
                for h in range(HEADS):
                    last = pe.matmul(ps[0:S, 6, h * HD1:(h + 1) * HD1], ptself[:, h, :],
                                     vtok[:, bass.ds(i * 2 + j, 1), h * HD1:(h + 1) * HD1].rearrange("p o d -> p (o d)"),
                                     start=True, stop=True)
                last.then_inc(sa_c, 1)

            def sa_turn(i, j):
                pe.wait_ge(sa_ct, i * 2 + (LEAD + j + 1))
                pe.wait_ge(sa_out, i * 2 + (LEAD + j))
                for c in range(C):
                    last = pe.transpose(ps[:, 7, c * S:(c + 1) * S], ctok[:, c * P:(c + 1) * P], ident[0:S, 0:S])
                last.then_inc(sa_ctt, 1)

            pe.wait_ge(ev["vt"], 8)
            sa_scores(0, 0)
            sa_scores(0, 1)
            sa_transposes(0, 0)
            sa_values(0, 0)
            with pe.Fori(0, B // 2 - 1) as i:
                for j in (1, 2):
                    sa_scores(i, j + 1)
                    sa_transposes(i, j)
                    sa_turn(i, j - 1)
                    sa_values(i, j)
            sa_transposes(B // 2 - 1, 1)
            sa_turn(B // 2 - 1, 0)
            sa_values(B // 2 - 1, 1)

            for t in range(2):
                if t == 0:
                    pe.wait_ge(load_d1, 32)
                    pe.wait_ge(sa_m, LEAD + 4 * B)
                else:
                    sa_turn(B // 2 - 1, 1)
                pe.wait_ge(xe_l, 2 + t + 1)
                for m in range(C):
                    if t == 1 and m == 1:
                        var(3, 0)
                    ops = experts(wdn1, t, m)
                    for n, (w, v) in enumerate(ops):
                        last = pe.matmul(bank(t, m), w, v, start=n == 0, stop=n == len(ops) - 1)
                    last.then_inc(mm["d1"], 1)

            var(3, 1)

            def ready(t):
                pe.wait_ge(norm_ok, 8 + 2 * t + 2)
            dense("cq", 1, lambda t, m: [(wcq[:, c, :], half(xn[:, c, :], t)) for c in range(C)], ready)
            pe.wait_ge(ev["cq"], 2)
            pe.wait_ge(wcv_ok, 1)
            pe.wait_ge(load_w1att, 32)
            attention(1)

            def ready(t):
                pe.wait_ge(A["c_ev"], done(1, "c_ev"))
                pe.wait_ge(load_cd, 16)
            dense("cd", 2, lambda t, m: [(wcd[:, m * P:(m + 1) * P], half(cT, t))], ready,
                  lambda m: var(4, 0) if m == 1 else None)

            var(4, 1)
            for t in range(2):
                if t == 0:
                    pe.wait_ge(load_gu, 64)
                pe.wait_ge(xe_l, 4 + t + 1)
                for m in range(FC1):
                    rows = min(P, FF1 - m * P)
                    if m >= 2:
                        pe.wait_ge(gu_h, t * FC1 + m - 1)
                    for g in range(2):
                        for n in range(4):
                            e, c = n // 2, n % 2
                            last = pe.matmul(ps[0:rows, 4 * t + (2 * m + g) % 4, 0:HALF],
                                             wgu[:, g, e, c, m * P:m * P + rows], half(xe[:, e, c, :], t),
                                             start=n == 0, stop=n == 3)
                        last.then_inc(mm["gu"], 1)
                if t == 0:
                    pe.wait_ge(load_down, 64)
                pe.wait_ge(gu_h, t * FC1 + FC1 - 1)
                for m in range(C):
                    for n in range(2 * FC1):
                        e, c = n % 2, n // 2
                        if m == 0 and e == 0:
                            pe.wait_ge(ev["gu"], t * FC1 + c + 1)
                        rows = min(P, FF1 - c * P)
                        last = pe.matmul(bank(t, m), wdown[0:rows, e, c, m * P:(m + 1) * P], hexp[0:rows, e, c, :],
                                         start=n == 0, stop=n == 2 * FC1 - 1)
                    last.then_inc(mm["dn"], 1)

            for l in (2, 3):
                pe.wait_ge(load_mem, 64)
                if l == 2:
                    pe.wait_ge(ev["dn"], 4)
                else:
                    pe.wait_ge(norm_ok, 14)
                attention(l)
                pe.wait_ge(A["c_ev"], done(l, "c_ev"))
                for m in range(C):
                    gate_chunk(l, 1, m)
                for t in range(2):
                    var(l + 3, t)

        @block.scalar
        def _(act):
            for n in STARTED_BY["scalar"]:
                act.sem_inc(A[n], LEAD)
            act.sem_inc(sa_e, LEAD)
            act.sem_inc(sa_pt, LEAD)
            act.sem_inc(sa_out, LEAD)

            def bank(t, m):
                return ps[:, 4 * t + m % 4, 0:HALF]

            def tok(ap, t):
                return ap[:, :, t * HALF:(t + 1) * HALF]

            def norm(n, centre, eps):
                table(ACT.Sqrt)
                for t in range(2):
                    if centre:
                        act.wait_ge(centred, 2 * n + t + 1)
                        src = xc
                    else:
                        x_ready(n, t)
                        src = x
                    act.activation(tok(xn, t), tok(src, t), ACT.Square).then_inc(squared, 1)
                    act.wait_ge(var_mm, 2 * n + t + 1)
                    act.activation(rstd[:, t * HALF:(t + 1) * HALF], bank(t, 1), ACT.Sqrt, bias=eps[:, 0:1],
                                   scale=1.0 / D)\
                       .then_inc(std_ok, 1)

            def table(func):
                act.activation(warm[:, 0:1], eps5[:, 0:1], func)

            def x_ready(n, t):
                if n == 2:
                    act.wait_ge(ev["f2"], 2 * t + 2)
                elif n == 3:
                    act.wait_ge(ev["d1"], 2 * t + 2)
                elif n == 4:
                    act.wait_ge(ev["cd"], 2 * t + 2)
                else:
                    act.wait_ge(fuse, 4 * (n - 5) + 2 * t + 2)

            def attention(l):
                a = ATTS[l]
                groups, tiles, ring = a["groups"], a["tiles"], a["ring"]
                nt, ngr = len(tiles), len(groups)
                scale = 1.0 if l < 2 else D ** -0.5

                def q_hi(i, j, xq):
                    wait(act, l, "q_mm", i, j, xq + 1)
                    c0, c1 = q_cols(a, xq)
                    act.activation(qhi[:, j % 2, c0:c1], ps[:, xq % 3, 0:c1 - c0], ACT.Copy, scale=scale)\
                       .then_inc(A["q_hi"], 1)

                def p_exp(i, j, g, u):
                    s = slot_of(a, g, u, j)
                    m = s_cols(a)
                    wait(act, l, "nmax", i, j, unit_index(a, g, u) + 1)
                    act.activation(wide[0:m, s, :], wide[0:m, s, :], ACT.Exp, bias=negmax[0:m, s:s + 1], scale=-1.0,
                                   accum_out=den[0:m, s:s + 1]).then_inc(A["p_exp"], 1)

                def pt_hi(i, j, k, c):
                    tt = k * nt + c
                    kr = chunk_rows(tiles[c][0])
                    w = sum(groups[k]) * len(tiles[c])
                    wait(act, l, "pv_mm", i, j, tt - ring + 1)
                    wait(act, l, "t_mm", i, j, tt + 1)
                    act.activation(pthi[0:kr, tt % ring, 0:w], ps[0:kr, 3 + tt % ring, 0:w], ACT.Copy)\
                       .then_inc(A["pt_hi"], 1)

                def rb_out(i, j, k):
                    w = sum(groups[k])
                    wait(act, l, "o_ev", i, j, k)
                    wait(act, l, "rb_mm", i, j, k + 1)
                    act.activation(rbc[:, 0:w], ps[:, 7, 0:w], ACT.Copy).then_inc(A["rb_sb"], 1)

                def c_out(i, j, xq):
                    b = i * 2 + j
                    wait(act, l, "c_mm", i, j, xq + 1)
                    if l == 0:
                        dst, w = big8[:, 4 * xq:4 * xq + 4, bass.ds(b * S, S)], 4
                    elif l == 1:
                        dst, w = cT[:, bass.ds(b * S, S)].unsqueeze(1), 1
                    else:
                        dst, w = mc[:, :, bass.ds(b * S, S)], 2
                    act.activation(dst, ps[:, 7, 0:w * S].rearrange("p (c t) -> p c t", c=w), ACT.Copy)\
                       .then_inc(A["c_ev"], 1)

                def step(i, j, k, nxt, before=None, after_next=False):
                    last = k == ngr - 1
                    items = plan(a, k, nxt, after_next)
                    bi = next_batch(i, j) if last else (i, j)
                    for s in range(nt + 2):
                        if s < nt:
                            pt_hi(i, j, k, s)
                        for at_slot, it in items:
                            if at_slot == s and it[0] == "q":
                                q_hi(*q_batch(a, i, j), it[1])
                        for at_slot, it in items:
                            if at_slot == s - a["exp_lag"] and it[0] == "s" and it[3] == 2:
                                p_exp(*bi, it[1], it[2])
                        if before is not None and s - a["c_slot"] in range(a["c_pieces"]):
                            c_out(*before, s - a["c_slot"])
                        if s == a["rb_slot"] + 1:
                            rb_out(i, j, k)

                for xq in range(len(a["q_pieces"])):
                    q_hi(0, 0, xq)
                for u in range(len(groups[0])):
                    p_exp(0, 0, 0, u)
                if ngr == 1:
                    q_hi(0, 1, 0)
                step(0, 0, 0, True, after_next=True)
                if ngr > 1:
                    with act.Fori(0, B // 2 - 1) as i:
                        for j in range(2):
                            for k in range(1, ngr):
                                step(i, j, k, True)
                            step(i, j + 1, 0, True, before=(i, j))
                    for j in range(2):
                        for k in range(1, ngr):
                            step(B // 2 - 1, j, k, j == 0)
                        if j == 0:
                            step(B // 2 - 1, 1, 0, False, before=(B // 2 - 1, 0))
                else:
                    with act.Fori(0, B // 2 - 2) as i:
                        for j in range(2):
                            step(i, j + 1, 0, True, before=(i, j), after_next=True)
                    for b in (B - 3, B - 2, B - 1):
                        step(b // 2, b % 2, 0, b < B - 1, before=((b - 1) // 2, (b - 1) % 2), after_next=b < B - 2)
                for xq in range(a["c_pieces"]):
                    c_out(B // 2 - 1, 1, xq)

            act.wait_ge(consts, 1)
            norm(0, True, eps5)
            act.wait_ge(consts, 3)
            for t in range(2):
                for m in range(8):
                    act.wait_ge(mm["q0"], 8 * t + m + 1)
                    act.activation(big8[:, m, t * HALF:(t + 1) * HALF], bank(t, m), ACT.Copy, scale=DH0 ** -0.5)\
                       .then_inc(ev["q0"], 1)
            act.wait_ge(load_consts, 16 * 8)
            act.activation(tgate[:, :], tgate[:, :], ACT.Tanh).then_inc(gates_ok, 1)
            act.wait_ge(cossin_mm, 1)
            act.activation(cossin[:, :, :], ps[:, 7, 0:2 * S].rearrange("p (n s) -> p n s", n=2), ACT.Copy)\
               .then_inc(cossin_ok, 1)
            attention(0)
            norm(1, True, eps5)
            for t in range(2):
                for m in range(8):
                    act.wait_ge(mm["f1"], 8 * t + m + 1)
                    act.activation(big8[:, m, t * HALF:(t + 1) * HALF], bank(t, m), ACT.Gelu).then_inc(ev["f1"], 1)
            norm(2, False, eps6)
            for t in range(2):
                for m in range(4):
                    act.wait_ge(mm["qk"], 4 * t + m + 1)
                    act.activation(qk[:, m, t * HALF:(t + 1) * HALF], bank(t, m), ACT.Copy,
                                   scale=HD1 ** -0.5 if m < C else 1.0).then_inc(ev["qk"], 1)
            for b in range(B):
                act.wait_ge(mm["vt"], b + 1)
                act.activation(vtok[:, b, :], ps[0:S, b, 0:D], ACT.Copy).then_inc(ev["vt"], 1)

            def sa_exp(i, j):
                act.wait_ge(sa_sub, i * 2 + (LEAD + j + 1))
                act.activation(sself[:, j % 2, :, :], sself[:, j % 2, :, :], ACT.Exp).then_inc(sa_e, 1)

            def sa_copies(i, j):
                for n in range(4):
                    act.wait_ge(sa_t, i * 8 + (4 * j + n + 1))
                    if n == 0:
                        act.wait_ge(sa_c, i * 2 + (LEAD + j))
                    act.activation(ptself[:, 4 * n:4 * n + 4, :], ps[0:S, 4 + n % 2, 0:4 * S]
                                   .rearrange("p (h q) -> p h q", h=4), ACT.Copy).then_inc(sa_pt, 1)

            def sa_result(i, j):
                act.wait_ge(sa_ctt, i * 2 + (LEAD + j + 1))
                act.activation(ctxT[:, :, bass.ds((i * 2 + j) * S, S)],
                               ps[:, 7, 0:2 * S].rearrange("p (c t) -> p c t", c=C), ACT.Copy).then_inc(sa_out, 1)

            sa_exp(0, 0)
            sa_copies(0, 0)
            sa_exp(0, 1)
            with act.Fori(0, B // 2 - 1) as i:
                for j in (1, 2):
                    sa_copies(i, j)
                    sa_result(i, j - 1)
                    sa_exp(i, j + 1)
            sa_copies(B // 2 - 1, 1)
            sa_result(B // 2 - 1, 0)
            sa_result(B // 2 - 1, 1)

            norm(3, False, eps6)
            for t in range(2):
                act.wait_ge(mm["cq"], t + 1)
                act.activation(cq[:, t * HALF:(t + 1) * HALF], bank(t, 0), ACT.Copy, scale=float(np.float32(CHD1 ** -0.5)))\
                   .then_inc(ev["cq"], 1)
            attention(1)
            norm(4, False, eps6)
            for t in range(2):
                for m in range(FC1):
                    rows = min(P, FF1 - m * P)
                    act.wait_ge(mm["gu"], 2 * (t * FC1 + m) + 1)
                    if t * FC1 + m >= 2:
                        act.wait_ge(gu_h, t * FC1 + m - 1)
                    act.activation(gsilu[0:rows, m % 2, :], ps[0:rows, 4 * t + (2 * m) % 4, 0:HALF], ACT.Silu)\
                       .then_inc(gu_silu, 1)
            for l in (2, 3):
                attention(l)
                name = f"g{l}"
                for t in range(2):
                    for m in range(C):
                        act.wait_ge(mm[name], 2 * t + m + 1)
                        act.activation(gate[:, m, t * HALF:(t + 1) * HALF], bank(t, m), ACT.Sigmoid,
                                       bias=vcol(f"b{l}", m)).then_inc(ev[name], 1)
                norm(l + 3, False, eps6)

        @block.vector
        def _(dve):
            for n in STARTED_BY["vector"]:
                dve.sem_inc(A[n], LEAD)
            for s_ in (sa_m, sa_x, sa_sub, sa_den, sa_ct):
                dve.sem_inc(s_, LEAD)
            steps = [0]

            def chain(ins):
                steps[0] += 1
                ins.then_inc(norm_step, 1)
                dve.wait_ge(norm_step, steps[0])

            def bank(t, m):
                return ps[:, 4 * t + m % 4, 0:HALF]

            def tok(ap, t):
                return ap[:, :, t * HALF:(t + 1) * HALF]

            def both(ap):
                return ap.unsqueeze(1).to_broadcast([P, C, HALF])

            def half(ap, c, t):
                return ap[:, c, t * HALF:(t + 1) * HALF]

            def centre(n, t):
                dve.wait_ge(mean_mm, 2 * n + t + 1)
                dve.scalar_tensor_tensor(tok(xc, t), both(bank(t, 0)), -1.0 / D, tok(x, t), ALU.mult, ALU.add)\
                   .then_inc(centred, 1)

            def norm(n, t, g, bvec=None, src=x, dst=xn, experts=False, between=None):
                r = rstd[:, t * HALF:(t + 1) * HALF]
                dve.wait_ge(std_ok, 2 * n + t + 1)
                chain(dve.reciprocal(r, r))
                if between:
                    between()
                if experts:
                    rv, rl = rmask[:, 0, :], rmask[:, 1, :]
                    chain(dve.tensor_tensor(rv, r, vm[:, t * HALF:(t + 1) * HALF], ALU.mult))
                    chain(dve.tensor_tensor(rl, r, rv, ALU.subtract))
                    for e, re in enumerate((rv, rl)):
                        for c in range(C):
                            last = dve.scalar_tensor_tensor(xe[:, e, c, t * HALF:(t + 1) * HALF], half(src, c, t),
                                                            vcol(g, c), re, ALU.mult, ALU.mult)
                        last.then_inc((xe_v, xe_l)[e], 1)
                    return
                for c in range(C):
                    d = half(dst, c, t)
                    last = dve.scalar_tensor_tensor(d, half(src, c, t), vcol(g, c), r, ALU.mult, ALU.mult)
                    if bvec is not None:
                        chain(last)
                        last = dve.tensor_scalar(d, d, vcol(bvec, c), None, ALU.add)
                    last.then_inc(norm_ok, 1)

            def residual(name, t, m, gcol=None):
                dve.wait_ge(mm[name], 2 * t + m + 1)
                xs = x[:, m, t * HALF:(t + 1) * HALF]
                if gcol is None:
                    dve.tensor_tensor(xs, bank(t, m), xs, ALU.add).then_inc(ev[name], 1)
                else:
                    dve.scalar_tensor_tensor(xs, bank(t, m), tgate[:, gcol:gcol + 1], xs, ALU.mult, ALU.add)\
                       .then_inc(ev[name], 1)

            def residual_norm(name, n, *norm_args, gcol=None, short=False, **norm_kwargs):
                centred_too = norm_kwargs.get("src") is xc
                for m in range(C):
                    residual(name, 0, m, gcol)
                if centred_too:
                    centre(n, 0)
                residual(name, 1, 0, gcol)
                if short:
                    residual(name, 1, 1, gcol)
                    norm(n, 0, *norm_args, **norm_kwargs)
                else:
                    norm(n, 0, *norm_args, **norm_kwargs, between=lambda: residual(name, 1, 1, gcol))
                if centred_too:
                    centre(n, 1)
                norm(n, 1, *norm_args, **norm_kwargs)

            def attention(l, first=False):
                a = ATTS[l]
                groups, tiles, ring = a["groups"], a["tiles"], a["ring"]
                nu = sum(len(g) for g in groups)
                nt, ngr = len(tiles), len(groups)
                scale = 1.0 if l < 2 else D ** -0.5

                def t_hi(i, j):
                    wait(dve, l, "s_mm", i, j - 1, 0)
                    wait(dve, l, "raw_t", i, j, 16)
                    dve.tensor_copy(thi[:, j % 2, :], raw[:, 0:SK]).then_inc(A["t_hi"], 1)

                def n_hi(i, j):
                    wait(dve, l, "pv_mm", i, j - 1, 0)
                    wait(dve, l, "raw_n", i, j, 32)
                    dve.tensor_copy(nhi[:, j % 2, :, :], raw_ctx(l).rearrange("p (c d) -> p c d", c=CHUNKS)).then_inc(A["n_hi"], 1)

                def t_lo(i, j):
                    wait(dve, l, "t_hi", i, j, 1)
                    dve.tensor_tensor(tlo[:, j % 2, :], raw[:, 0:SK], thi[:, j % 2, :].bitcast(FP32), ALU.subtract)\
                       .then_inc(A["t_lo"], 1)

                def make_bias(i, j):
                    if l == 0:
                        wait(dve, l, "raw_m", i, j, 16)
                        dve.tensor_scalar(bias[:, j % 2, :], mask_u8, BIG, -BIG, ALU.mult, ALU.add)\
                           .then_inc(A["bias"], 1)

                def q_lo(i, j, xq):
                    c0, c1 = q_cols(a, xq)
                    wait(dve, l, "q_hi", i, j, xq + 1)
                    dve.scalar_tensor_tensor(qlo[:, j % 2, c0:c1], ps[:, xq % 3, 0:c1 - c0], scale,
                                             qhi[:, j % 2, c0:c1].bitcast(FP32), ALU.mult, ALU.subtract)\
                       .then_inc(A["q_lo"], 1)

                def s_neg(i, j, g, u, jj):
                    n = 3 * unit_index(a, g, u) + jj
                    s = slot_of(a, g, u, j)
                    m = s_cols(a)
                    k0, k1 = PIECES[jj]
                    if n == 0 and l > 0 and isinstance(i, int) and i == 0:
                        dve.wait_ge(bias_zero, l)
                    if jj == 0 and u == 0:
                        if n == 0 and l == 0:
                            wait(dve, l, "bias", i, j, 1)
                        wait(dve, l, "t_mm", i, j, (g - 1) * nt)
                    wait(dve, l, "s_mm", i, j, n + 1)
                    carry_wait(dve, "scores")
                    dve.tensor_tensor_reduce(out=wide[0:m, s, k0:k1], in0=ps[0:m, jj, 0:k1 - k0],
                                             in1=bias[0:m, j % 2 if l == 0 else 0, k0:k1], scale=-1.0, scalar=FMAX,
                                             op0=ALU.add, op1=ALU.min, accum_out=negmin3[0:m, s, jj:jj + 1])\
                       .then_inc(A["s_neg"], 1)

                def nmax(i, j, g, u):
                    s = slot_of(a, g, u, j)
                    m = s_cols(a)
                    wait(dve, l, "s_neg", i, j, 3 * unit_index(a, g, u) + 3)
                    dve.tensor_reduce(negmax[0:m, s:s + 1], negmin3[0:m, s, :], AX.X, ALU.min).then_inc(A["nmax"], 1)

                def rden(i, j, g, part):
                    s = slot_of(a, g, 0, j)
                    m = s_cols(a)
                    e = s + len(groups[g])
                    if part == 0:
                        wait(dve, l, "p_exp", i, j, unit_index(a, g, len(groups[g]) - 1) + 1)
                        ins_ = dve.reciprocal(rdn[0:m, s:e], den[0:m, s:e])
                    elif part == 1:
                        wait(dve, l, "rden", i, j, 3 * g + 1)
                        ins_ = dve.tensor_copy(rdn_hi[0:m, s:e], rdn[0:m, s:e])
                    else:
                        wait(dve, l, "rden", i, j, 3 * g + 2)
                        ins_ = dve.tensor_tensor(rdn_lo[0:m, s:e], rdn[0:m, s:e], rdn_hi[0:m, s:e].bitcast(FP32),
                                                 ALU.subtract)
                    ins_.then_inc(A["rden"], 1)

                def pt_lo(i, j, k, c):
                    tt = k * nt + c
                    kr = chunk_rows(tiles[c][0])
                    w = sum(groups[k]) * len(tiles[c])
                    wait(dve, l, "pt_hi", i, j, tt + 1)
                    dve.tensor_tensor(ptlo[0:kr, tt % ring, 0:w], ps[0:kr, 3 + tt % ring, 0:w],
                                      pthi[0:kr, tt % ring, 0:w].bitcast(FP32), ALU.subtract).then_inc(A["pt_lo"], 1)

                def o_ev(i, j, k):
                    w = sum(groups[k])
                    c0 = unit_col(a, k, 0)
                    if k == 0:
                        wait(dve, l, "c_mm", i, j, 0)
                    wait(dve, l, "pv_mm", i, j, (k + 1) * nt)
                    if ngr > 1:
                        wait(dve, l, "rb_sb", i, j, k + 1)
                        dve.tensor_tensor(outT[:, c0:c0 + w], ps[:, 6, 0:w], rbc[:, 0:w], ALU.mult)\
                           .then_inc(A["o_ev"], 1)
                        return
                    wait(dve, l, "rb_sb", i, j, k + 1)
                    both_parts = outT[:, w:3 * w].rearrange("p (r q) -> p r q", r=2)
                    dve.tensor_tensor(both_parts, ps[:, 6, 0:2 * w].rearrange("p (r q) -> p r q", r=2),
                                      rbc[:, 0:w].unsqueeze(1).to_broadcast([P, 2, w]), ALU.mult).then_inc(A["o_ev"], 1)
                    wait(dve, l, "o_ev", i, j, 1)
                    dve.tensor_tensor(outT[:, 0:w], both_parts[:, 0, :], both_parts[:, 1, :], ALU.add)\
                       .then_inc(A["o_ev"], 1)

                def step(i, j, k, nxt, after_next=False):
                    last = k == ngr - 1
                    items = plan(a, k, nxt, after_next)
                    bi = next_batch(i, j) if last else (i, j)
                    nb = next_batch(i, j)
                    for s in range(nt + 2):
                        if s < nt and ngr == 1:
                            pt_lo(i, j, k, s)
                        for at_slot, it in items:
                            if at_slot == s:
                                if it[0] == "q":
                                    q_lo(*q_batch(a, i, j), it[1])
                                else:
                                    s_neg(*bi, *it[1:])
                                    if it[3] == 2:
                                        nmax(*bi, it[1], it[2])
                        if s < nt and ngr > 1:
                            pt_lo(i, j, k, s)
                        if s - a["rden_slot"] in range(3):
                            rden(i, j, k, s - a["rden_slot"])
                        if nxt and ngr > 1:
                            if k == 0 and s == a["t_slot"]:
                                t_hi(*nb)
                            if k == 1 and s == a["n_slot"]:
                                n_hi(*nb)
                            if k == 1 and s == a["bias_slot"]:
                                make_bias(*nb)
                        if ngr == 1 and s == a["n_slot"] and nxt:
                            n_hi(*nb)
                        if ngr == 1 and s == a["t_slot"] and after_next:
                            t_hi(i, j + 2)
                            t_lo(i, j + 2)
                    o_ev(i, j, k)

                if first or l == 0:
                    t_hi(0, 0)
                    if ngr == 1:
                        t_lo(0, 0)
                if first:
                    return
                make_bias(0, 0)
                for xq in range(len(a["q_pieces"])):
                    q_lo(0, 0, xq)
                for u in range(len(groups[0])):
                    for jj in range(3):
                        s_neg(0, 0, 0, u, jj)
                    nmax(0, 0, 0, u)
                n_hi(0, 0)
                if ngr == 1:
                    q_lo(0, 1, 0)
                    t_hi(0, 1)
                    t_lo(0, 1)
                with dve.Fori(0, B // 2 - 1) as i:
                    for j in range(2):
                        for k in range(ngr):
                            step(i, j, k, True, True)
                for j in range(2):
                    for k in range(ngr):
                        step(B // 2 - 1, j, k, j == 0)

            for t in range(2):
                centre(0, t)
            dve.wait_ge(load_consts, 16 * 8)
            for t in range(2):
                norm(0, t, "ln_q_g", "ln_q_b", src=xc)
            attention(0)
            dve.wait_ge(gates_ok, 1)
            residual_norm("o0", 1, "ln_ff_g", "ln_ff_b", gcol=0, src=xc)
            residual_norm("f2", 2, "ln_in", gcol=1, experts=True)
            dve.wait_ge(cossin_ok, 1)
            for t in range(2):
                for m in range(4):
                    n = 4 * t + m
                    q4 = qk[:, m, t * HALF:(t + 1) * HALF].rearrange("p (b s) -> p b s", s=S)
                    r4 = rotated[:, n % 2, :].rearrange("p (b s) -> p b s", s=S)
                    cos4 = cossin[:, 0, :].unsqueeze(1).to_broadcast([P, 4, S])
                    sin4 = cossin[:, 1, :].unsqueeze(1).to_broadcast([P, 4, S])
                    dve.wait_ge(mm["rt"], n + 1)
                    if n >= 2:
                        dve.wait_ge(rope, 2 * (n - 1))
                    dve.tensor_tensor(r4, bank(t, m).rearrange("p (b s) -> p b s", s=S), sin4, ALU.mult).then_inc(rt_s, 1)
                    dve.tensor_tensor(q4, q4, cos4, ALU.mult).then_inc(rope, 1)
                    dve.wait_ge(rope, 2 * n + 1)
                    dve.wait_ge(rt_s, n + 1)
                    dve.tensor_tensor(q4, q4, r4, ALU.add).then_inc(rope, 1)

            def sa_soft(i, j):
                s_ = sself[:, j % 2, :, :]
                smax = rstat[:, j % 2, 0:HEADS]
                for n in range(4):
                    dve.wait_ge(sa_s, i * 8 + (LEAD + 4 * j + n + 1))
                    if n == 0:
                        dve.wait_ge(sa_pt, i * 8 + (LEAD + 4 * j - 4))
                    dve.tensor_tensor(s_[:, 4 * n:4 * n + 4, :],
                                      ps[0:S, n, 0:4 * S].rearrange("p (h q) -> p h q", h=4),
                                      causal.unsqueeze(1).to_broadcast([S, 4, S]), ALU.add).then_inc(sa_m, 1)
                dve.wait_ge(sa_m, i * 8 + (LEAD + 4 * j + 4))
                dve.tensor_reduce(smax, s_, AX.X, ALU.max).then_inc(sa_x, 1)
                dve.wait_ge(sa_x, i * 2 + (LEAD + j + 1))
                dve.tensor_tensor(s_, s_, smax.unsqueeze(2).to_broadcast([S, HEADS, S]), ALU.subtract).then_inc(sa_sub, 1)

            def sa_norm(i, j):
                ssum, srec = rstat[:, j % 2, HEADS:2 * HEADS], rstat[:, j % 2, 2 * HEADS:3 * HEADS]
                dve.wait_ge(sa_e, i * 2 + (LEAD + j + 1))
                dve.tensor_reduce(ssum, sself[:, j % 2, :, :], AX.X, ALU.add).then_inc(sa_den, 1)
                dve.wait_ge(sa_den, i * 4 + (LEAD + 2 * j + 1))
                dve.reciprocal(srec, ssum).then_inc(sa_den, 1)
                dve.wait_ge(sa_den, i * 4 + (LEAD + 2 * j + 2))
                dve.wait_ge(sa_ctt, i * 2 + (LEAD + j))
                dve.wait_ge(sa_c, i * 2 + (LEAD + j + 1))
                dve.tensor_tensor(ctok.rearrange("p (h d) -> p h d", h=HEADS),
                                  ps[0:S, 6, 0:D].rearrange("p (h d) -> p h d", h=HEADS),
                                  srec.unsqueeze(2).to_broadcast([S, HEADS, HD1]), ALU.mult).then_inc(sa_ct, 1)

            sa_soft(0, 0)
            with dve.Fori(0, B // 2 - 1) as i:
                for j in range(2):
                    sa_soft(i, j + 1)
                    sa_norm(i, j)
            sa_soft(B // 2 - 1, 1)
            for t in range(2):
                if t == 1:
                    sa_norm(B // 2 - 1, 0)
                    sa_norm(B // 2 - 1, 1)
                dve.wait_ge(sa_out, LEAD + 4 * t + 4)
                dve.tensor_tensor(tok(xe[:, 0, :, :], t), tok(ctxT, t), both(vm[:, t * HALF:(t + 1) * HALF]), ALU.mult)\
                   .then_inc(xe_v, 1)
            attention(1, first=True)
            residual_norm("d1", 3, "ln_cross")
            attention(1)
            residual_norm("cd", 4, "ln_post", experts=True, short=True)
            attention(2, first=True)
            for t in range(2):
                for m in range(FC1):
                    n = t * FC1 + m
                    rows = min(P, FF1 - m * P)
                    dve.wait_ge(mm["gu"], 2 * n + 2)
                    dve.wait_ge(gu_silu, n + 1)
                    if n >= 1:
                        dve.wait_ge(ev["gu"], n)
                    dve.tensor_tensor(hgu[0:rows, :], ps[0:rows, 4 * t + (2 * m + 1) % 4, 0:HALF],
                                      gsilu[0:rows, m % 2, :], ALU.mult).then_inc(gu_h, 1)
                for m in range(C):
                    dve.wait_ge(mm["dn"], 2 * t + m + 1)
                    xs = x[:, m, t * HALF:(t + 1) * HALF]
                    dve.tensor_tensor(xs, bank(t, m), xs, ALU.add).then_inc(ev["dn"], 1)
            for l in (2, 3):
                attention(l)
                if l == 2:
                    attention(3, first=True)
                name = f"g{l}"
                for t in range(2):
                    for m in range(C):
                        dve.wait_ge(ev[name], 2 * t + m + 1)
                        gs = gate[:, m, t * HALF:(t + 1) * HALF]
                        xs = x[:, m, t * HALF:(t + 1) * HALF]
                        chain(dve.tensor_tensor(gs, gs, mc[:, m, t * HALF:(t + 1) * HALF], ALU.mult))
                        if m == 0:
                            dve.wait_ge(mm[name], 2 * t + 2)
                        dve.tensor_tensor(xs, xs, gs, ALU.add).then_inc(fuse, 1)
                for t in range(2):
                    norm(l + 3, t, f"n{l}", dst=x)

        @block.gpsimd
        def _(pool):
            for n in STARTED_BY["gpsimd"]:
                pool.sem_inc(A[n], LEAD)
            pool.sem_inc(sa_kbd, LEAD)
            pool.memset(eps5[:, :], 1e-5)
            pool.memset(eps6[:, :], 1e-6)
            pool.memset(ones, 1.0).then_inc(consts, 1)
            pool.memset(raw, 0.0)
            for q in (qhi, qlo):
                pool.memset(q[:, :, HEADS * S:].bitcast(FP32), 0.0)
            pool.memset(vm[:, :], 0.0).then_inc(consts, 1)

            pool.wait_ge(load_consts, 16 * 8)
            pool.tensor_copy(pos_f, pos_i).then_inc(pos_ok, 1)
            pool.wait_ge(pos_ok, 1)
            pool.tensor_scalar(pos_neg, pos_f, 0.0, float(S), ALU.is_lt, ALU.mult).then_inc(pos_ok, 1)
            pool.wait_ge(pos_ok, 2)
            pool.tensor_tensor(pos_f, pos_f, pos_neg, ALU.add).then_inc(pos_ok, 1)
            pool.wait_ge(pos_ok, 3)
            pool.tensor_scalar(pos_f, pos_f, 0.0, float(S - 1), ALU.max, ALU.min).then_inc(pos_ok, 1)
            pool.wait_ge(pos_ok, 4)
            pool.tensor_scalar(onehot, pos_f[0:S, :], vec[0:S, 22:23], None, ALU.is_equal).then_inc(pos_ok, 1)

            pool.tensor_scalar(tt_one.rearrange("p b s -> p (b s)"), tt_i, 1.0, None, ALU.is_equal).then_inc(vm_step, 1)
            pool.wait_ge(vm_step, 1)
            pool.tensor_tensor(vm[:, :].rearrange("p (b s) -> p b s", b=B)[:, :, 0:S - 1],
                               tt_one[:, :, 0:S - 1], tt_one[:, :, 1:S], ALU.mult).then_inc(consts, 1)

            def tok(ap, t):
                return ap[:, :, t * HALF:(t + 1) * HALF]

            def attention(l, first=False):
                a = ATTS[l]
                groups = a["groups"]
                ngr = len(groups)

                def t_lo(i, j):
                    wait(pool, l, "t_hi", i, j, 1)
                    pool.tensor_tensor(tlo[:, j % 2, :], raw[:, 0:SK], thi[:, j % 2, :].bitcast(FP32), ALU.subtract)\
                        .then_inc(A["t_lo"], 1)

                def n_lo(i, j):
                    wait(pool, l, "n_hi", i, j, 1)
                    pool.tensor_tensor(nlo[:, j % 2, :, :], raw_ctx(l).rearrange("p (c d) -> p c d", c=CHUNKS),
                                       nhi[:, j % 2, :, :].bitcast(FP32), ALU.subtract).then_inc(A["n_lo"], 1)

                def make_qbd(i, j):
                    if l == 1:
                        wait(pool, l, "q_mm", i, j, 0)
                        pool.tensor_tensor(qbd1.rearrange("p (h q) -> p h q", h=HEADS),
                                           cq[:, bass.ds((i * 2 + j) * S, S)].unsqueeze(1).to_broadcast([P, HEADS, S]),
                                           hmask16[:, :].unsqueeze(2).to_broadcast([P, HEADS, S]), ALU.mult)\
                            .then_inc(A["qbd"], 1)

                def make_diag(i, j, g):
                    s = slot_of(a, g, 0, j)
                    m = s_cols(a)
                    nu = len(groups[g])
                    wait(pool, l, "rb_mm", i, j, g)
                    wait(pool, l, "rden", i, j, 3 * g + 3)
                    eye = ident[0:m, 0:m].unsqueeze(1).to_broadcast([m, nu, m])
                    pool.tensor_tensor(diag_hi[0:m, 0:nu, 0:m], eye, rdn_hi[0:m, s:s + nu].bitcast(FP32)
                                       .unsqueeze(2).to_broadcast([m, nu, m]), ALU.mult)
                    pool.tensor_tensor(diag_lo[0:m, 0:nu, 0:m], eye, rdn_lo[0:m, s:s + nu]
                                       .unsqueeze(2).to_broadcast([m, nu, m]), ALU.mult).then_inc(A["diag"], 1)

                def step(i, j, k, nxt):
                    make_diag(i, j, k)
                    if nxt and k == 0 and ngr > 1:
                        t_lo(*next_batch(i, j))
                    if nxt and ngr == 1:
                        n_lo(*next_batch(i, j))
                    if nxt and k == 1:
                        make_qbd(*next_batch(i, j))
                    if nxt and k == 1:
                        n_lo(*next_batch(i, j))

                if first or l == 0:
                    t_lo(0, 0)
                if first:
                    return
                if l == 1:
                    pool.wait_ge(ev["cq"], 1)
                make_qbd(0, 0)
                if l == 1:
                    pool.wait_ge(ev["cq"], 2)
                if l > 0:
                    pool.memset(bias[:, 0, :], 0.0).then_inc(bias_zero, 1)
                n_lo(0, 0)
                with pool.Fori(0, B // 2 - 1) as i:
                    for j in range(2):
                        for k in range(ngr):
                            step(i, j, k, True)
                for j in range(2):
                    for k in range(ngr):
                        step(B // 2 - 1, j, k, j == 0)

            attention(0)

            def make_kbd(i, j):
                now = bass.ds((i * 2 + j) * S, S)
                pool.wait_ge(sa_s, i * 8 + (LEAD + 4 * j - 4))
                pool.tensor_copy(qsb[:, j % 2, :, :], qk[:, 0:C, now])
                for c in range(C):
                    ins_ = pool.tensor_tensor(kbd[:, j % 2, 8 * c:8 * c + 8, :],
                                              qk[:, 2 + c, now].unsqueeze(1).to_broadcast([P, 8, S]),
                                              hmask8[:, :].unsqueeze(2).to_broadcast([P, 8, S]), ALU.mult)
                ins_.then_inc(sa_kbd, 1)

            pool.wait_ge(rope, 8)
            make_kbd(0, 0)
            pool.wait_ge(rope, 16)
            with pool.Fori(0, B // 2 - 1) as i:
                for j in (1, 2):
                    make_kbd(i, j)
            make_kbd(B // 2 - 1, 1)
            for t in range(2):
                pool.wait_ge(xe_v, 2 + t + 1)
                pool.tensor_tensor(tok(xe[:, 1, :, :], t), tok(ctxT, t), tok(xe[:, 0, :, :], t), ALU.subtract)\
                    .then_inc(xe_l, 1)
            pool.wait_ge(load_w1att, 32)
            pool.memset(watt[:, 0:2048], 0.0).then_inc(wcv_step, 1)
            pool.wait_ge(wcv_step, 1)
            pool.tensor_copy(watt[:, 0:16 * (P + CHD1)].rearrange("p (h n) -> p h n", h=HEADS)[:, :, 0:CHD1],
                             wcv.rearrange("p (h d) -> p h d", h=HEADS)).then_inc(wcv_ok, 1)
            attention(1, first=True)
            attention(1)
            for t in range(2):
                if t == 1:
                    pool.wait_ge(mm["dn"], 2)
                for m in range(FC1):
                    n = t * FC1 + m
                    rows = min(P, FF1 - m * P)
                    pool.wait_ge(gu_h, n + 1)
                    pool.tensor_tensor(hexp[0:rows, 0, m, :], hgu[0:rows, :], vm[0:rows, t * HALF:(t + 1) * HALF],
                                       ALU.mult).then_inc(gu_v, 1)
                    pool.wait_ge(gu_v, n + 1)
                    pool.tensor_tensor(hexp[0:rows, 1, m, :], hgu[0:rows, :], hexp[0:rows, 0, m, :],
                                       ALU.subtract).then_inc(ev["gu"], 1)
            for l in (2, 3):
                if l == 2:
                    pool.wait_ge(mm["gu"], 4 * FC1)
                else:
                    pool.wait_ge(norm_ok, 16)
                attention(l)

    return nc


def _columns(v):
    return v.reshape(C, P).T


def _chunks(w):
    return w.reshape(-1, P, w.shape[1]).transpose(1, 0, 2)


def _constants():
    f = np.float32
    d = np.arange(P) % HD1
    rot = np.zeros((P, P), f)
    rot[(np.arange(P) // HD1) * HD1 + (d + HD1 // 2) % HD1, np.arange(P)] = 1
    inv = (f(1.0) / f(10000.0) ** (np.arange(0, HD1, 2).astype(f) / f(HD1))).astype(f)
    ang = np.outer(np.arange(S).astype(f), inv).astype(f)[:, d % (HD1 // 2)]
    sign = np.where(d < HD1 // 2, f(-1), f(1))
    return dict(
        ident=np.eye(P, dtype=f), rot=rot, postab=np.concatenate([np.cos(ang), np.sin(ang) * sign], 1).astype(f),
        hmask8=(np.arange(P)[:, None] // HD1 == np.arange(8)[None]).astype(f),
        hmask16=(np.arange(P)[:, None] // CHD1 == np.arange(HEADS)[None]).astype(f),
        causal=np.where(np.tril(np.ones((S, S), bool)), f(0), f(-BIG)).astype(f))


def kernel(**inputs):
    import concourse.bacc as bacc
    from concourse.bass_utils import run_bass_kernel_spmd

    g = {k: np.asarray(v) for k, v in inputs.items()}
    g0 = lambda k: g["L0_xattn_" + k]
    g1 = lambda k: g["L1_xattn_" + k]
    ctx = g["ctx_1024"]
    wkv, ckv = g0("Wkv"), g1("ckv_w")
    vec = [g0("ln_q_g"), g0("ln_q_b"), g0("ln_ff_g"), g0("ln_ff_b"), g1("ln_in_w"), g1("ln_post_cross_w"),
           g1("ln_post_attn_w"), g["L2_xattn_norm_w"], g["L3_xattn_norm_w"], g["L2_xattn_b_gate"], g["L3_xattn_b_gate"]]
    f = np.float32
    arrays = dict(
        xT=g["x"].reshape(T, D).T.reshape(C, P, T).transpose(1, 0, 2), ctx=ctx, ctxT=ctx.transpose(0, 2, 1),
        mask=g["mask_BxS2_bk0"], tt=g["mask_BxS_ik0"].reshape(T), pos=g["pos_1xS"].reshape(S),
        vec=np.concatenate([_columns(v) for v in vec] + [np.arange(P, dtype=f)[:, None]], 1),
        gates=np.concatenate([g0("attn_gate"), g0("ff_gate")]),
        wq=_chunks(g0("Wq")), wk0=_chunks(wkv[:, :F0].T), wv0=wkv[:, F0:], wo=_chunks(g0("Wo")),
        w1=_chunks(g0("W1")), w2=_chunks(g0("W2")),
        qkv=np.stack([_chunks(g1("v_qkv")), _chunks(g1("l_qkv"))]),
        dense1=np.stack([_chunks(g1("v_dense")), _chunks(g1("l_dense"))]),
        wcq=_chunks(g1("cq_w")), wck=ckv[:, :DM].T, wcv=ckv[:, DM:], wcd=g1("cdense_w"),
        gu=np.stack([np.stack([_chunks(g1(e + k)) for e in ("v_", "l_")]) for k in ("gate", "up")]),
        down=np.stack([g1("v_down"), g1("l_down")]),
        wmem=np.stack([_chunks(g[f"L{n}_xattn_W_mem"]) for n in (2, 3)]),
        wmemT=np.stack([g[f"L{n}_xattn_W_mem"].T for n in (2, 3)]),
        wgate=np.stack([_chunks(g[f"L{n}_xattn_W_gate"].T) for n in (2, 3)]),
        **_constants())
    nc = bacc.Bacc("TRN2", target_bir_lowering=False, num_devices=1)
    maps, aps = {}, {}
    for n, v in arrays.items():
        maps["in_" + n] = np.ascontiguousarray(v)
        aps[n] = nc.dram_tensor("in_" + n, v.shape, mybir.dt.from_np(v.dtype), kind="ExternalInput").ap()
    out = nc.dram_tensor("out_xT", (P, C, T), FP32, kind="ExternalOutput").ap()
    build_layers(nc, aps, out)
    r = run_bass_kernel_spmd(nc, [maps], core_ids=[0])
    y = r.results[0]["out_xT"]
    return y.transpose(2, 1, 0).reshape(B, S, D)
```
